# Optimizing a Trainium2 kernel written in Bass

```python
import numpy as np
import jax
import jax.numpy as jnp

def _softmax(x, axis=-1):
    return jax.nn.softmax(x, axis=axis)

def _gelu(x):
    return jax.nn.gelu(x, approximate=True)

def _silu(x):
    return jax.nn.silu(x)

def _sigmoid(x):
    return jax.nn.sigmoid(x)

def _layernorm(x, axis=-1, eps=1e-05):
    m = jnp.mean(x, axis=axis, keepdims=True)
    v = jnp.var(x, axis=axis, keepdims=True)
    return (x - m) / jnp.sqrt(v + eps)

def _scatter_add(tgt, idx, src, axis=0):
    return tgt.at[idx].add(src)

def _segment_sum(src, seg, n):
    return jax.ops.segment_sum(src, seg, n)
kernel_name = 'mk_perceiver_d1_seqx_r2_0635d6'

def setup_inputs(seed: int=0):
    np.random.seed(seed)
    _w = jnp.asarray

    def _rec_inputs():
        import jax
        import jax.numpy as jnp
        _rk = jax.random.key(seed)
        x = 7.22e-05 + 1 * jax.random.normal(jax.random.fold_in(_rk, 1), (32, 32, 1024), jnp.float32)
        _lenS = 32 - jax.random.randint(jax.random.fold_in(_rk, 7), (32,), 0, max(1, 32 // 4) + 1, jnp.int32)
        _lenS2 = 257 - jax.random.randint(jax.random.fold_in(_rk, 8), (32,), 0, max(1, 257 // 4) + 1, jnp.int32)
        _ctx_512P = jax.random.normal(jax.random.fold_in(_rk, 11), (32, 16, 256), jnp.float32)
        _ctx_512c = jax.random.dirichlet(jax.random.fold_in(_rk, 511), 0.3 * jnp.ones((16,), jnp.float32), (32, 257))
        _ctx_512t = jnp.einsum('bsk,bkd->bsd', _ctx_512c, _ctx_512P)
        _ctx_512t = _ctx_512t * jax.lax.rsqrt(jnp.mean(jnp.square(_ctx_512t)) + 1e-12) * 0.953939
        ctx_512 = -0.000514642 + 1.00011 * (_ctx_512t + 0.3 * jax.random.normal(jax.random.fold_in(_rk, 611), (32, 257, 256), jnp.float32))
        return (x, ctx_512)
    x, ctx_512 = _rec_inputs()

    def _L0_xattn_setup():
        import jax, jax.numpy as jnp
        import numpy as np
        B, S, H, NH, L = (2, 1024, 1024, 16, 256)
        HD = H // NH
        key = jax.random.key(seed)
        k1, k2, k3, k4, k5 = jax.random.split(key, 5)
        scale = 0.02
        return {'q': jax.random.normal(k1, (B, S, H), dtype=jnp.float32), 'latent_kv': jax.random.normal(k2, (B, S, L), dtype=jnp.float32), 'Wq': jax.random.normal(k3, (H, H), dtype=jnp.float32) * scale, 'Wkv_expand': jax.random.normal(k4, (2 * H, L), dtype=jnp.float32) * scale, 'Wout': jax.random.normal(k5, (H, H), dtype=jnp.float32) * scale}
    _L0_xattn_all = _L0_xattn_setup()
    _L0_xattn_in = {k: v for k, v in _L0_xattn_all.items() if k in ('Wq', 'Wkv_expand', 'Wout')}
    del _L0_xattn_all

    def _L0_attn_setup():
        import jax, jax.numpy as jnp
        import numpy as np
        import math
        D_MODEL = 1024
        D_STATE = 128
        R_MIN = 0.0
        R_MAX = 0.9
        MAX_PHASE = 6.283185307179586
        B_SZ = 4
        T_LEN = 1024
        key = jax.random.key(seed)
        k_x, k_bre, k_bim, k_cre, k_cim = jax.random.split(key, 5)
        x = jax.random.normal(k_x, (B_SZ, T_LEN, D_MODEL), dtype=jnp.float32)
        u = np.linspace(0.0, 1.0, D_STATE, dtype=np.float64)
        mag_init = np.clip(R_MIN + (R_MAX - R_MIN) * u, 1e-06, 1.0 - 1e-06)
        nu_init = -np.log(mag_init)
        nu_log = jnp.asarray(np.log(np.clip(np.expm1(nu_init), 1e-06, None)), dtype=jnp.float32)
        theta_log = jnp.asarray(np.linspace(math.log(0.0001), math.log(MAX_PHASE), D_STATE), dtype=jnp.float32)
        B_re = jax.random.normal(k_bre, (D_STATE, D_MODEL), dtype=jnp.float32) / math.sqrt(D_MODEL)
        B_im = jax.random.normal(k_bim, (D_STATE, D_MODEL), dtype=jnp.float32) / math.sqrt(D_MODEL)
        C_re = jax.random.normal(k_cre, (D_MODEL, D_STATE), dtype=jnp.float32) / math.sqrt(D_STATE)
        C_im = jax.random.normal(k_cim, (D_MODEL, D_STATE), dtype=jnp.float32) / math.sqrt(D_STATE)
        D = jnp.ones((D_MODEL,), dtype=jnp.float32)
        return {'x': x, 'nu_log': nu_log, 'theta_log': theta_log, 'B_re': B_re, 'B_im': B_im, 'C_re': C_re, 'C_im': C_im, 'D': D}
    _L0_attn_all = _L0_attn_setup()
    _L0_attn_in = {k: v for k, v in _L0_attn_all.items() if k in ('nu_log', 'theta_log', 'B_re', 'B_im', 'C_re', 'C_im', 'D')}
    del _L0_attn_all

    def _L0_ffn_setup():
        import jax, jax.numpy as jnp
        import numpy as np
        EPS = 1e-06
        K_STEPS = 4
        USE_GATING = True

        def layer_norm(x, gamma, beta):
            mu = jnp.mean(x, axis=-1, keepdims=True)
            var = jnp.mean(jnp.square(x - mu), axis=-1, keepdims=True)
            return (x - mu) * jax.lax.rsqrt(var + EPS) * gamma + beta
        key = jax.random.key(seed)
        B, L, D, H = (4, 2048, 1024, 4096)
        ks = jax.random.split(key, 16)
        s = 0.02
        return {'x': jax.random.normal(ks[0], (B, L, D), dtype=jnp.float32), 'in_gamma': jnp.ones((D,), jnp.float32), 'in_beta': jnp.zeros((D,), jnp.float32), 'agg_w': jax.random.normal(ks[1], (D, D), jnp.float32) * s, 'agg_b': jnp.zeros((D,), jnp.float32), 'pn_gamma': jnp.ones((D,), jnp.float32), 'pn_beta': jnp.zeros((D,), jnp.float32), 'd1_w': jax.random.normal(ks[2], (D, H), jnp.float32) * s, 'd1_b': jnp.zeros((H,), jnp.float32), 'd2_w': jax.random.normal(ks[3], (H, D), jnp.float32) * s, 'd2_b': jnp.zeros((D,), jnp.float32), 'bc_w': jax.random.normal(ks[4], (D, D), jnp.float32) * s, 'bc_b': jnp.zeros((D,), jnp.float32), 'gate_w': jax.random.normal(ks[5], (D, D), jnp.float32) * s, 'gate_b': jnp.zeros((D,), jnp.float32), 'out_gamma': jnp.ones((D,), jnp.float32), 'out_beta': jnp.zeros((D,), jnp.float32)}
    _L0_ffn_all = _L0_ffn_setup()
    _L0_ffn_in = {k: v for k, v in _L0_ffn_all.items() if k in ('in_gamma', 'in_beta', 'agg_w', 'agg_b', 'pn_gamma', 'pn_beta', 'd1_w', 'd1_b', 'd2_w', 'd2_b', 'bc_w', 'bc_b', 'gate_w', 'gate_b', 'out_gamma', 'out_beta')}
    del _L0_ffn_all
    return {'x': x, 'ctx_512': ctx_512, 'L0_xattn_Wq': _L0_xattn_in['Wq'], 'L0_xattn_Wkv_expand': _L0_xattn_in['Wkv_expand'], 'L0_xattn_Wout': _L0_xattn_in['Wout'], 'L0_attn_nu_log': _L0_attn_in['nu_log'], 'L0_attn_theta_log': _L0_attn_in['theta_log'], 'L0_attn_B_re': _L0_attn_in['B_re'], 'L0_attn_B_im': _L0_attn_in['B_im'], 'L0_attn_C_re': _L0_attn_in['C_re'], 'L0_attn_C_im': _L0_attn_in['C_im'], 'L0_attn_D': _L0_attn_in['D'], 'L0_ffn_in_gamma': _L0_ffn_in['in_gamma'], 'L0_ffn_in_beta': _L0_ffn_in['in_beta'], 'L0_ffn_agg_w': _L0_ffn_in['agg_w'], 'L0_ffn_agg_b': _L0_ffn_in['agg_b'], 'L0_ffn_pn_gamma': _L0_ffn_in['pn_gamma'], 'L0_ffn_pn_beta': _L0_ffn_in['pn_beta'], 'L0_ffn_d1_w': _L0_ffn_in['d1_w'], 'L0_ffn_d1_b': _L0_ffn_in['d1_b'], 'L0_ffn_d2_w': _L0_ffn_in['d2_w'], 'L0_ffn_d2_b': _L0_ffn_in['d2_b'], 'L0_ffn_bc_w': _L0_ffn_in['bc_w'], 'L0_ffn_bc_b': _L0_ffn_in['bc_b'], 'L0_ffn_gate_w': _L0_ffn_in['gate_w'], 'L0_ffn_gate_b': _L0_ffn_in['gate_b'], 'L0_ffn_out_gamma': _L0_ffn_in['out_gamma'], 'L0_ffn_out_beta': _L0_ffn_in['out_beta']}

def reference(x, ctx_512, L0_xattn_Wq, L0_xattn_Wkv_expand, L0_xattn_Wout, L0_attn_nu_log, L0_attn_theta_log, L0_attn_B_re, L0_attn_B_im, L0_attn_C_re, L0_attn_C_im, L0_attn_D, L0_ffn_in_gamma, L0_ffn_in_beta, L0_ffn_agg_w, L0_ffn_agg_b, L0_ffn_pn_gamma, L0_ffn_pn_beta, L0_ffn_d1_w, L0_ffn_d1_b, L0_ffn_d2_w, L0_ffn_d2_b, L0_ffn_bc_w, L0_ffn_bc_b, L0_ffn_gate_w, L0_ffn_gate_b, L0_ffn_out_gamma, L0_ffn_out_beta):
    import jax
    import jax.numpy as jnp

    def _L0_xattn_ref(q, latent_kv, Wq, Wkv_expand, Wout):
        import jax, jax.numpy as jnp
        import numpy as np
        B, S, H, NH, L = (2, 1024, 1024, 16, 256)
        HD = H // NH
        b, sq, _ = q.shape
        sk = latent_kv.shape[1]
        qp = q @ Wq.T
        kv = latent_kv @ Wkv_expand.T
        k, v = jnp.split(kv, 2, axis=-1)
        qh = qp.reshape(b, sq, NH, HD).transpose(0, 2, 1, 3)
        kh = k.reshape(b, sk, NH, HD).transpose(0, 2, 1, 3)
        vh = v.reshape(b, sk, NH, HD).transpose(0, 2, 1, 3)
        inv_sqrt_d = 1.0 / jnp.sqrt(jnp.float32(HD))
        scores = jnp.einsum('bhqd,bhkd->bhqk', qh, kh) * inv_sqrt_d
        causal = jnp.tril(jnp.ones((sq, sk), dtype=bool))
        scores = jnp.where(causal, scores, jnp.finfo(scores.dtype).min)
        attn = jax.nn.softmax(scores, axis=-1)
        out = jnp.einsum('bhqk,bhkd->bhqd', attn, vh)
        out = out.transpose(0, 2, 1, 3).reshape(b, sq, H)
        return out @ Wout.T

    def _L0_attn_ref(x, nu_log, theta_log, B_re, B_im, C_re, C_im, D):
        import jax, jax.numpy as jnp
        import numpy as np
        import math
        D_MODEL = 1024
        D_STATE = 128
        R_MIN = 0.0
        R_MAX = 0.9
        MAX_PHASE = 6.283185307179586
        B_SZ = 4
        T_LEN = 1024
        nu = jax.nn.softplus(nu_log)
        mag = jnp.exp(-jnp.exp(nu))
        theta = jnp.exp(theta_log)
        A_re = mag * jnp.cos(theta)
        A_im = mag * jnp.sin(theta)
        gamma = jnp.sqrt(jnp.clip(1.0 - mag * mag, 0.0))
        gB_re = gamma[:, None] * B_re
        gB_im = gamma[:, None] * B_im
        Bu_re = jnp.einsum('btd,nd->btn', x, gB_re)
        Bu_im = jnp.einsum('btd,nd->btn', x, gB_im)

        def step(h, bu):
            h_re, h_im = h
            bu_re, bu_im = bu
            new_re = A_re * h_re - A_im * h_im + bu_re
            new_im = A_re * h_im + A_im * h_re + bu_im
            return ((new_re, new_im), (new_re, new_im))
        Bsz = x.shape[0]
        h0 = jnp.zeros((Bsz, A_re.shape[0]), dtype=x.dtype)
        _, (H_re, H_im) = jax.lax.scan(step, (h0, h0), (jnp.swapaxes(Bu_re, 0, 1), jnp.swapaxes(Bu_im, 0, 1)))
        H_re = jnp.swapaxes(H_re, 0, 1)
        H_im = jnp.swapaxes(H_im, 0, 1)
        y = jnp.einsum('btn,dn->btd', H_re, C_re) - jnp.einsum('btn,dn->btd', H_im, C_im) + D * x
        return y

    def _L0_ffn_ref(x, in_gamma, in_beta, agg_w, agg_b, pn_gamma, pn_beta, d1_w, d1_b, d2_w, d2_b, bc_w, bc_b, gate_w, gate_b, out_gamma, out_beta):
        import jax, jax.numpy as jnp
        import numpy as np
        EPS = 1e-06
        K_STEPS = 4
        USE_GATING = True

        def layer_norm(x, gamma, beta):
            mu = jnp.mean(x, axis=-1, keepdims=True)
            var = jnp.mean(jnp.square(x - mu), axis=-1, keepdims=True)
            return (x - mu) * jax.lax.rsqrt(var + EPS) * gamma + beta
        x_norm = layer_norm(x, in_gamma, in_beta)
        thought = x_norm[:, -1, :] @ agg_w + agg_b
        for _ in range(K_STEPS):
            t = layer_norm(thought, pn_gamma, pn_beta)
            t = jax.nn.gelu(t @ d1_w + d1_b, approximate=False)
            thought = thought + (t @ d2_w + d2_b)
        broadcast = (thought @ bc_w + bc_b)[:, None, :]
        if USE_GATING:
            gate = jax.nn.sigmoid(x @ gate_w + gate_b)
            out = x + gate * broadcast
        else:
            out = x + broadcast
        return layer_norm(out, out_gamma, out_beta)
    x = x + _L0_xattn_ref(_layernorm(x, axis=-1), ctx_512, L0_xattn_Wq, L0_xattn_Wkv_expand, L0_xattn_Wout)
    x = x + _L0_attn_ref(_layernorm(x, axis=-1), L0_attn_nu_log, L0_attn_theta_log, L0_attn_B_re, L0_attn_B_im, L0_attn_C_re, L0_attn_C_im, L0_attn_D)
    x = x + _L0_ffn_ref(_layernorm(x, axis=-1), L0_ffn_in_gamma, L0_ffn_in_beta, L0_ffn_agg_w, L0_ffn_agg_b, L0_ffn_pn_gamma, L0_ffn_pn_beta, L0_ffn_d1_w, L0_ffn_d1_b, L0_ffn_d2_w, L0_ffn_d2_b, L0_ffn_bc_w, L0_ffn_bc_b, L0_ffn_gate_w, L0_ffn_gate_b, L0_ffn_out_gamma, L0_ffn_out_beta)
    return x

_drawn_inputs = setup_inputs


def setup_inputs(seed=0):
    import zlib

    import numpy as np

    out = dict(_drawn_inputs(seed))
    spreads = {'L0_attn_D': (1.0, 0.2),
     'L0_ffn_in_gamma': (1.0, 0.545),
     'L0_ffn_in_beta': (0.0, 0.555),
     'L0_ffn_agg_b': (0.0, 0.351),
     'L0_ffn_pn_gamma': (1.0, 0.2),
     'L0_ffn_pn_beta': (0.0, 0.433),
     'L0_ffn_d1_b': (0.0, 0.283),
     'L0_ffn_d2_b': (0.0, 0.1),
     'L0_ffn_bc_b': (0.0, 0.639),
     'L0_ffn_gate_b': (0.0, 0.8),
     'L0_ffn_out_gamma': (1.0, 0.2),
     'L0_ffn_out_beta': (0.0, 0.282)}
    factors = {'L0_xattn_Wq': 5.387}
    for name, (base, spread) in spreads.items():
        noise = np.random.default_rng([zlib.crc32(name.encode()), seed]).standard_normal(out[name].shape)
        drawn = base * np.exp(spread * noise) if base else spread * noise
        out[name] = jnp.asarray(drawn.astype(out[name].dtype))
    for name, factor in factors.items():
        out[name] = (out[name] * factor).astype(out[name].dtype)
    return out
```

```python
from contextlib import ExitStack

import concourse.bass as bass
from concourse import mybir

F32 = mybir.dt.float32
I32 = mybir.dt.int32
ALU = mybir.AluOpType
ACT = mybir.ActivationFunctionType
AX = mybir.AxisListType

P = 128
BANK = 512
TWO_PI = 6.283185307179586
MASKED = -1.0e38
LN_EPS = 1e-5
FFN_EPS = 1e-6


class Count:

    def __init__(self, sem):
        self.sem, self.n, self.term = sem, 0, 0

    def one(self, instruction, by=1):
        instruction.then_inc(self.sem, by)
        self.n += by
        return self.term + self.n

    def enter(self, turn, per_turn):
        self.start, self.per_turn, self.term = self.n, per_turn, turn * per_turn

    def leave(self, turns):
        assert self.n - self.start == self.per_turn, (self.n - self.start, self.per_turn)
        self.n, self.term = self.start + turns * self.per_turn, 0


def build(nc, x, ctx_512, Wq, Wkv, Wout, nu_log, theta_log, B_re, B_im, C_re, C_im, Dskip,
          in_gamma, in_beta, agg_w, agg_b, pn_gamma, pn_beta, d1_w, d1_b, d2_w, d2_b,
          bc_w, bc_b, gate_w, gate_b, out_gamma, out_beta, out):
    NB, SQ, D = x.shape
    L = ctx_512.shape[2]
    HEADS = 16
    HD = D // HEADS
    KD, KL = D // P, L // P
    BT = P // SQ
    G = NB // BT
    NST = nu_log.shape[0]
    HID = d1_w.shape[1]
    NJ = 4
    W4 = D // NJ
    H4 = HID // NJ
    STEPS = 4
    assert SQ == 32 and P == NST and L == 2 * P and W4 == 256 and H4 == 2 * BANK

    x_t = x.rearrange("b s d -> (b s) d").rearrange("(g p) d -> g p d", p=P)
    out_t = out.rearrange("b s d -> (b s) d").rearrange("(g p) d -> g p d", p=P)
    wo_t = Wout.rearrange("(g p) d -> g p d", p=P)

    with ExitStack() as ctx:
        mem = ctx.enter_context(nc.sbuf_tensor("mem", [P, 53200], F32))
        ps = ctx.enter_context(nc.psum_tensor("ps", [P, 8 * BANK], F32))
        top = [0]

        def take(cols, at=None):
            lo = top[0] if at is None else at
            if at is None:
                top[0] += cols
            assert lo + cols <= 53200, lo + cols
            return mem[:, lo:lo + cols]

        def shaped(ap, **dims):
            return ap.rearrange("p (" + " ".join(dims) + ") -> p " + " ".join(dims), **dims)

        R_WQ = 0
        R_WKV = KD * D
        R_O = R_WKV + KL * 2 * D
        R_WO = R_O + G * D
        R_BC = R_WO + KD * D
        R_T = R_BC + 4 * D
        wqT = shaped(take(KD * D, R_WQ), k=KD, n=D)
        wkvT = shaped(take(KL * 2 * D, R_WKV), k=KL, n=2 * D)
        o_all = shaped(take(G * D, R_O), g=G, n=D)
        woT = shaped(take(KD * D, R_WO), k=KD, n=D)
        bT = shaped(take(2 * D, R_BC), c=2, k=KD, n=NST)
        cT = shaped(take(2 * D, R_BC + 2 * D), c=2, n=D)
        x_all = shaped(take(G * D, R_WQ), g=G, n=D)
        gate_all = shaped(take(G * D, R_O), g=G, n=D)
        gw = shaped(take(KD * D, R_WO), k=KD, n=D)
        raw = [take(D, R_T + i * D) for i in range(4)]
        qT = shaped(take(D, R_T + 4 * D), c=KD, t=P)
        kT = shaped(take(D, R_T + 5 * D), c=KD, t=P)
        v = take(D, R_T + 6 * D)
        ctx_in = take(L, R_T + 7 * D)
        ctxT = shaped(take(L, R_T + 7 * D + L), k=KL, t=P)
        raw_bc = take(4 * P, R_T + 7 * D + 2 * L)
        top[0] = R_T + 8 * D
        R_U = top[0]
        x_in = take(D)
        xn = take(D)
        xnT = shaped(take(D), k=KD, t=P)
        raw_wo = take(D)
        scores = shaped(take(HEADS * SQ), h=HEADS, k=SQ)
        probs = take(HEADS * SQ)
        probsT = shaped(take(HEADS * P), h=HEADS, q=P)
        o_st = take(D, R_U + 2 * D)
        oT = shaped(take(D, R_U + 3 * D), k=KD, t=P)
        x1 = take(D, R_U + 4 * D)
        x1n = take(D, R_U + 5 * D)
        x1nT = shaped(take(D, R_U + 6 * D), k=KD, t=P)
        top[0] = R_U + 7 * D
        R_STATE = top[0]
        state = [shaped(take(2 * BT * 48), c=2, b=BT, t=48) for _ in range(2)]
        stmp = shaped(take(2 * P), c=2, b=BT, t=SQ)
        R_H = top[0]
        hT = shaped(take(2 * P), c=2, b=BT, t=SQ)
        R_SKIP = top[0]
        dskip = take(D)
        zst = take(D, R_U)
        zT = shaped(take(D, R_U + D), k=KD, t=P)
        hid = take(H4, R_U + 2 * D)
        hidT = shaped(take(H4, R_U + 3 * D), c=H4 // P, m=P)
        th = take(W4, R_U + 4 * D)
        thb = take(W4, R_U + 4 * D + W4)
        tn = take(W4, R_U + 4 * D + 2 * W4)
        bcast = shaped(take(D, R_U + 5 * D), j=NJ, n=W4)
        gate_bias = take(D, R_U + 6 * D)
        d1_bias = take(H4, R_SKIP)
        spread = shaped(take(G * P, R_STATE), g=G, t=P)
        tT = shaped(take(2 * P, R_H), c=2, m=P)
        t_mul = [take(D, R_T + i * D) for i in range(2)]
        t_z = [take(D, R_T + (2 + i) * D) for i in range(2)]
        t_gamma = take(D, R_T + 6 * D)
        t_beta = take(D, R_T + 7 * D)
        t_out = [take(D, R_T + (4 + i) * D) for i in range(2)]
        packed_names = ["in_g", "in_b", "agg_b", "pn_g", "pn_b", "d2_b", "bc_b"]
        packed = {n: take(W4) for n in packed_names}
        ident = take(P)
        same_row = take(P)
        causal = take(SQ)
        last_rows = take(G * 36)
        group_mask = take(NJ)
        small = take(160)
        mvz = shaped(take(2 * G), g=G, c=2)
        zscale = take(G)
        zshift = take(G)

        SLOT = 2 * D
        RING, RES = 3, 5
        ring = [take(SLOT, R_T + i * SLOT) for i in range(RING)]
        resident = [take(SLOT, R_WKV), take(SLOT, R_WKV + SLOT), take(SLOT, R_T + RING * SLOT),
                    take(SLOT, R_BC), take(SLOT, R_BC + SLOT)]
        D1P = 2 * KD
        D2P = HID // P // 2
        PIECES = D1P + D2P
        assert (PIECES - RES) % RING == 0

        s6 = shaped(small[:, 0:12], a=2, c=6)
        mv = small[:, 12:14]
        veps = small[:, 14:15]
        rstd = small[:, 15:16]
        power = small[:, 16:17]
        mx = small[:, 17:33]
        rs = small[:, 33:49]
        ri = small[:, 49:65]
        ssm = small[:, 65:85]
        apow = shaped(small[:, 85:100], l=5, c=3)
        gam = small[:, 100:101]
        s6f = small[:, 101:107]
        s24 = shaped(small[:, 107:131], j=NJ, c=6)
        ssmk = small[:, 131:133]
        powers8 = small[:, 133:141]
        half = small[:, 141:142]
        vz = small[:, 142:150]
        eps_tmp = small[:, 150:151]

        def bank(i, cols=BANK):
            return ps[:, i * BANK:i * BANK + cols]

        TA, TB = bank(0), bank(1)

        def sem(name):
            return ctx.enter_context(nc.semaphore(name))

        const_ready = sem("const_ready")
        ssm_in = sem("ssm_in")
        gam_ready = sem("gam_ready")
        ssm_pool = sem("ssm_pool")
        ssm_act = sem("ssm_act")
        ssm_arg = sem("ssm_arg")
        dve_chain = sem("dve_chain")
        act_chain = sem("act_chain")
        pool_chain = sem("pool_chain")
        raw_in = [sem(f"raw_in{i}") for i in range(4)]
        x_loaded = sem("x_loaded")
        ctx_loaded = sem("ctx_loaded")
        wo_loaded = sem("wo_loaded")
        bc_loaded = sem("bc_loaded")
        dskip_loaded = sem("dskip_loaded")
        a_full, a_free = sem("a_full"), sem("a_free")
        b_full, b_free = sem("b_full"), sem("b_free")
        var_ready = sem("var_ready")
        rstd_ready = sem("rstd_ready")
        xn_ready = sem("xn_ready")
        qk_full, qk_evac = sem("qk_full"), sem("qk_evac")
        v_full, v_evac = sem("v_full"), sem("v_evac")
        o_full, o_evac = sem("o_full"), sem("o_evac")
        s_full, s_read = sem("s_full"), sem("s_read")
        shifted_ready = sem("shifted_ready")
        exp_ready = sem("exp_ready")
        pT_ready = sem("pT_ready")
        ost_ready = sem("ost_ready")
        y_full, y_read = sem("y_full"), sem("y_read")
        x1_ready = sem("x1_ready")
        x1n_ready = sem("x1n_ready")
        xd_ready = sem("xd_ready")
        bu_full, bu_evac = sem("bu_full"), sem("bu_evac")
        h_ready = sem("h_ready")
        c_full, c_read = sem("c_full"), sem("c_read")
        par_loaded = sem("par_loaded")
        gbias_loaded = sem("gbias_loaded")
        gw_loaded = sem("gw_loaded")
        slot_in = [sem(f"slot_in{i}") for i in range(RING)]
        slot_used = sem("slot_used")
        res_in = sem("res_in")
        zv_ready, zr_ready = sem("zv_ready"), sem("zr_ready")
        st_in, st_full = sem("st_in"), sem("st_full")
        tn_ready = sem("tn_ready")
        z_ready = sem("z_ready")
        p_full, p_read = sem("p_full"), sem("p_read")
        hp_full, hp_read = sem("hp_full"), sem("hp_read")
        hsum_ready, hid_ready = sem("hsum_ready"), sem("hid_ready")
        g_full, g_read = sem("g_full"), sem("g_read")
        sig_ready = sem("sig_ready")
        bc_ready = sem("bc_ready")
        tail_in = sem("tail_in")
        bb_full, bb_read = sem("bb_full"), sem("bb_read")
        tz_ready = sem("tz_ready")
        fin_ready = sem("fin_ready")
        xd_half, bzero, tsum_ready = sem("xd_half"), sem("bzero"), sem("tsum_ready")
        zshift_ready, tz_used = sem("zshift_ready"), sem("tz_used")
        passed_dve, passed_pool, passed_pe = sem("passed_dve"), sem("passed_pool"), sem("passed_pe")
        out_done = [sem(f"out_done{i}") for i in range(2)]

        block = ctx.enter_context(nc.Block())

        NA0 = NB0 = KD + 4
        PER_TILE = 3
        NB1 = NB0 + PER_TILE * G
        N_RING = PIECES - RES
        RESIDENT_Q = [7, 15, 20, 26, 31]
        BC_DONE = 2 * (KD // 2) + STEPS * N_RING
        NB2 = NB1 + 2 * G
        AGG = KD // 2
        chunk_of = [(j, c) for j in range(NJ) for c in range(2)]

        def piece_source(q):
            if q < D1P:
                i, k = divmod(q, KD)
                return d1_w[k * P:(k + 1) * P, :].rearrange("p (j n) -> p j n", j=NJ)[:, :, i * BANK:(i + 1) * BANK]
            c, jp = divmod(q - D1P, 2)
            return d2_w.rearrange("(j c p) n -> p c j n", j=NJ, c=H4 // P)[:, c, 2 * jp:2 * jp + 2, :]

        def as_piece(slot, q):
            return shaped(slot, j=NJ, n=BANK) if q < D1P else shaped(slot, j=2, n=D)

        @block.sync
        def _(sp):
            def load_ctx(g):
                for j in range(BT):
                    sp.dma_start(ctx_in[32 * j:32 * j + SQ, :], ctx_512[g * BT + j, 0:SQ, :])\
                      .then_inc(ctx_loaded, 16)

            def load_prep(g):
                sp.dma_start(raw_wo, wo_t[g, :, :]).then_inc(wo_loaded, 16)
                for n, w in enumerate((C_re, C_im)):
                    sp.dma_start(raw_bc[:, n * P:(n + 1) * P], w[bass.ts(g, P), :]).then_inc(bc_loaded, 16)
                for n, w in enumerate((B_re, B_im)):
                    sp.dma_start(raw_bc[:, (2 + n) * P:(3 + n) * P], w[:, bass.ts(g, P)])\
                      .then_inc(bc_loaded, 16)

            sp.dma_start(x_in, x_t[0, :, :]).then_inc(x_loaded, 16)
            for n in range(KD + 4):
                s = n % 4
                if n >= 4:
                    sp.wait_ge(a_free, n - 3)
                    sp.wait_ge(b_free, n - 3)
                if n >= 4:
                    sp.dma_start(raw[s], Wq[(n - 4) * P:(n - 3) * P, :]).then_inc(raw_in[s], 16)
                else:
                    sp.dma_start(shaped(raw[s], r=4, n=L),
                                 Wkv[4 * n * P:4 * (n + 1) * P, :].rearrange("(r p) n -> p r n", p=P))\
                      .then_inc(raw_in[s], 16)
                if n == 3:
                    load_ctx(0)
            load_prep(0)
            sp.wait_ge(xn_ready, 1)
            sp.dma_start(x_in, x_t[1, :, :]).then_inc(x_loaded, 16)
            sp.dma_start(dskip, Dskip[None, :].broadcast_to([P, D])).then_inc(dskip_loaded, 16)

            def next_tile(it):
                sp.wait_ge(a_free, NA0 + PER_TILE * it + PER_TILE)
                sp.wait_ge(b_free, NB0 + PER_TILE * it + PER_TILE)
                load_ctx(it + 1)
                load_prep(it + 1)
                sp.wait_ge(xn_ready, it + 2)

            with sp.Fori(0, G - 2) as it:
                next_tile(it)
                sp.dma_start(x_in, x_t[it + 2, :, :]).then_inc(x_loaded, 16)
            next_tile(G - 2)
            sp.dma_start(x_in, x_t[0, :, :]).then_inc(x_loaded, 16)

            for name, w in (("in_g", in_gamma), ("in_b", in_beta), ("agg_b", agg_b), ("pn_g", pn_gamma),
                            ("pn_b", pn_beta), ("d2_b", d2_b), ("bc_b", bc_b)):
                for j in range(NJ):
                    sp.dma_start(packed[name][32 * j:32 * j + 32, :],
                                 w[None, j * W4:(j + 1) * W4].broadcast_to([32, W4])).then_inc(par_loaded, 16)

            agg_v = agg_w.rearrange("(n j p) d -> n p j d", j=2, p=P)
            bc_v = bc_w.rearrange("(n j p) d -> n p j d", j=2, p=P)
            sp.wait_ge(o_full, 2 * G)
            for r in range(3):
                sp.dma_start(as_piece(resident[r], RESIDENT_Q[r]), piece_source(RESIDENT_Q[r])).then_inc(res_in, 16)
            for m in range(RING):
                sp.dma_start(shaped(ring[m], j=2, n=D), agg_v[m, :, :, :]).then_inc(slot_in[m], 16)
            with sp.Fori(1, G) as g:
                sp.wait_ge(y_read, 2 * g)
                sp.dma_start(x_in, x_t[g, :, :]).then_inc(x_loaded, 16)
            sp.wait_ge(y_full, 2 * G)
            sp.dma_start(gw, gate_w.rearrange("(k p) n -> p k n", p=P)).then_inc(gw_loaded, 16)
            sp.wait_ge(c_full, 2 * G)
            sp.wait_ge(xd_ready, G)
            sp.dma_start(gate_bias, gate_b[None, :].broadcast_to([P, D])).then_inc(gbias_loaded, 16)
            for j in range(NJ):
                sp.dma_start(d1_bias[32 * j:32 * j + 32, :],
                             d1_b[None, j * H4:(j + 1) * H4].broadcast_to([32, H4])).then_inc(gbias_loaded, 16)
            for r in range(3, RES):
                sp.dma_start(as_piece(resident[r], RESIDENT_Q[r]), piece_source(RESIDENT_Q[r])).then_inc(res_in, 16)

            sp.wait_ge(slot_used, 1)
            sp.dma_start(shaped(ring[0], j=2, n=D), agg_v[RING, :, :, :]).then_inc(slot_in[0], 16)
            with sp.Fori(0, STEPS) as step:
                m = 0
                for q in range(PIECES):
                    if q in RESIDENT_Q:
                        continue
                    s = (AGG + m) % RING
                    sp.wait_ge(slot_used, N_RING * step + AGG + m - RING + 1)
                    sp.dma_start(as_piece(ring[s], q), piece_source(q)).then_inc(slot_in[s], 16)
                    m += 1
            for n in range(AGG):
                m = AGG + STEPS * N_RING + n
                sp.wait_ge(slot_used, m - RING + 1)
                sp.dma_start(shaped(ring[m % RING], j=2, n=D), bc_v[n, :, :, :]).then_inc(slot_in[m % RING], 16)
            sp.wait_ge(p_full, 1 + STEPS)
            sp.dma_start(t_gamma, out_gamma[None, :].broadcast_to([P, D])).then_inc(tail_in, 16)
            sp.dma_start(t_beta, out_beta[None, :].broadcast_to([P, D])).then_inc(tail_in, 16)
            with sp.Fori(0, G // 2) as i:
                for e in range(2):
                    sp.wait_ge(fin_ready, 2 * i + e + 1)
                    sp.dma_start(out_t[2 * i + e, :, :], t_out[e]).then_inc(out_done[e], 16)
            for e in range(2):
                sp.wait_ge(out_done[e], 16 * (G // 2))

        @block.gpsimd
        def _(pool):
            chain = Count(pool_chain)

            def then(instruction):
                pool.wait_ge(pool_chain, chain.one(instruction))

            def ones_where_zero(ap, base, pattern):
                return nc.gpsimd.affine_select(out=ap, in_=ap, compare_op=ALU.not_equal, fill=1.0, base=base,
                                               pattern=pattern, channel_multiplier=1)

            then(nc.gpsimd.memset(ident, 0.0))
            then(ones_where_zero(ident, 0, [[-1, P]]))
            then(nc.gpsimd.memset(power, -0.5))
            then(nc.gpsimd.memset(powers8, -0.5))
            then(nc.gpsimd.memset(half, 0.5))
            quad = shaped(probsT[:, 0, :], j=BT, k=SQ)
            then(nc.gpsimd.memset(quad, 0.0))
            then(nc.gpsimd.affine_select(out=quad, in_=quad, compare_op=ALU.is_ge, fill=MASKED, base=0,
                                         pattern=[[-SQ, BT], [-1, SQ]], channel_multiplier=1))
            for j in range(BT):
                then(nc.gpsimd.tensor_copy(causal[32 * j:32 * j + 32, :], quad[32 * j:32 * j + 32, j, :]))
            then(nc.gpsimd.memset(probsT, 0.0))
            for u in state:
                then(nc.gpsimd.memset(u, 0.0))
            nc.gpsimd.memset(group_mask, 0.0).then_inc(const_ready, 1)

            def power_of(dst, src, exponent):
                return nc.gpsimd.tensor_tensor(dst, src, exponent, ALU.pow)

            pool.wait_ge(var_ready, 1)
            power_of(rstd, veps, power).then_inc(rstd_ready, 1)
            pool.wait_ge(ssm_pool, 1)
            power_of(gam, ssm[:, 12:13], half).then_inc(gam_ready, 1)
            pool.wait_ge(const_ready, 1)
            for j in range(NJ):
                then(nc.gpsimd.memset(group_mask[32 * j:32 * j + 32, j:j + 1], 1.0))
            then(nc.gpsimd.memset(same_row, 0.0))
            for m in range(1 - NJ, NJ):
                then(ones_where_zero(same_row, 32 * m, [[-1, P]]))
            then(nc.gpsimd.memset(last_rows, 0.0))
            ones_where_zero(shaped(last_rows, g=G, c=36)[:, :, 0:BT], 1 - SQ, [[0, G], [-SQ, BT]])\
                .then_inc(const_ready, 1)

            with pool.Fori(1, G) as g:
                pool.wait_ge(var_ready, g + 1)
                power_of(rstd, veps, power).then_inc(rstd_ready, 1)

            def load_o(g):
                nc.gpsimd.tensor_copy(o_st, o_all[:, g, :]).then_inc(ost_ready, 1)

            def residual(g):
                pool.wait_ge(var_ready, G + g + 1)
                power_of(rstd, veps, power).then_inc(rstd_ready, 1)
                pool.wait_ge(x1n_ready, g + 1)
                tile = x_all[:, g, :]
                nc.gpsimd.tensor_tensor(tile, x1n, dskip, ALU.mult).then_inc(xd_half, 1)
                pool.wait_ge(xd_half, g + 1)
                pool.sem_inc(passed_pool, 1)
                nc.gpsimd.tensor_tensor(tile, tile, x1, ALU.add).then_inc(xd_ready, 1)

            pool.wait_ge(dskip_loaded, 16)
            pool.wait_ge(o_evac, 2 * G)
            load_o(0)
            pool.wait_ge(b_full, NB1 + 1)
            load_o(1)
            residual(0)
            with pool.Fori(1, G - 1) as g:
                pool.wait_ge(b_full, NB1 + 2 * g)
                load_o(g + 1)
                residual(g)
            residual(G - 1)

            pool.wait_ge(zv_ready, 1)
            power_of(zscale, vz, powers8).then_inc(zr_ready, 1)
            pool.wait_ge(c_full, 2 * G)
            then(nc.gpsimd.memset(spread, 0.0))
            for j in range(NJ):
                then(ones_where_zero(spread.rearrange("p g (q s) -> p g q s", q=BT), -32 * j,
                                     [[-BT, G], [-1, BT], [0, SQ]]))
            nc.gpsimd.memset(bcast, 0.0).then_inc(bzero, 1)
            pool.wait_ge(var_ready, 2 * G + 1)
            power_of(rstd, veps, power).then_inc(rstd_ready, 1)
            pool.wait_ge(var_ready, 2 * G + 2)
            power_of(rstd, veps, power).then_inc(rstd_ready, 1)
            with pool.Fori(0, STEPS) as step:
                pool.wait_ge(var_ready, step + (2 * G + 3))
                power_of(rstd, veps, power).then_inc(rstd_ready, 1)
            pool.wait_ge(tail_in, 32)

            def finish(t, e):
                pool.wait_ge(var_ready, t + (2 * G + STEPS + 3))
                power_of(rstd, veps, power).then_inc(rstd_ready, 1)
                pool.wait_ge(tsum_ready, t + 1)
                nc.gpsimd.tensor_tensor(t_out[e], t_mul[e], t_beta, ALU.add).then_inc(fin_ready, 1)

            for e in range(2):
                finish(e, e)
            with pool.Fori(1, G // 2) as i:
                for e in range(2):
                    pool.wait_ge(out_done[e], 16 * i)
                    finish(2 * i + e, e)

        @block.scalar
        def _(act):
            A = Count(a_free)
            qk, vv = Count(qk_evac), Count(v_evac)

            def copy(dst, src):
                return nc.scalar.activation(dst, src, ACT.Copy)

            def bank_a(dst, src=None):
                act.wait_ge(a_full, A.term + A.n + 1)
                A.one(copy(dst, shaped(TA, k=4, n=P) if src is None else src))

            act.dma_start(ssm[:, 0:1], nu_log[:, None]).then_inc(ssm_in, 16)
            act.dma_start(ssm[:, 1:2], theta_log[:, None]).then_inc(ssm_in, 16)
            act.wait_ge(ssm_in, 32)
            nc.scalar.activation(ssm[:, 2:4], ssm[:, 0:2], ACT.Exp).then_inc(ssm_act, 1)
            act.wait_ge(ssm_arg, 1)
            nc.scalar.activation(ssm[:, 7:8], ssm[:, 4:5], ACT.Exp)
            nc.scalar.activation(ssm[:, 8:9], ssm[:, 5:6], ACT.Sin)
            nc.scalar.activation(ssm[:, 9:10], ssm[:, 5:6], ACT.Sin, scale=0.5).then_inc(ssm_act, 1)

            for m in range(4):
                for r in range(2):
                    n = 4 * m + r
                    if r == 0:
                        act.wait_ge(a_full, A.n + 1)
                        copy(wkvT[:, :, n * P:(n + 1) * P], shaped(TA[:, 0:2 * P], k=KL, n=P))
                    else:
                        A.one(copy(wkvT[:, :, n * P:(n + 1) * P], shaped(TA[:, 2 * P:4 * P], k=KL, n=P)))
            with act.Fori(0, KD // 4) as i:
                A.enter(i, 4)
                for s in range(4):
                    bank_a(wqT[:, 0:4, bass.ds(i * 4 * P + s * P, P)])
                A.leave(KD // 4)

            def transposed(g):
                bank_a(xnT[:, 0:4, :])
                bank_a(ctxT, shaped(TA[:, 0:L], k=KL, n=P))
                bank_a(woT[:, 4:8, bass.ts(g, P)])

            def projected(g):
                for dst in (qT, kT):
                    for f in range(2):
                        act.wait_ge(qk_full, qk.term + qk.n + 1)
                        qk.one(copy(dst[:, 4 * f:4 * f + 4, :], shaped(bank(2 + f), c=4, t=P)))
                for n in range(2):
                    act.wait_ge(v_full, vv.term + vv.n + 1)
                    vv.one(copy(v[:, n * BANK:(n + 1) * BANK], bank(4 + n)))

            def exponentials(g):
                act.wait_ge(shifted_ready, g + 1)
                nc.scalar.activation(probs, scores.rearrange("p h k -> p (h k)"), ACT.Exp,
                                     scale=float(HD) ** -0.5).then_inc(exp_ready, 1)

            transposed(0)
            projected(0)
            with act.Fori(0, G - 1) as it:
                A.enter(it, PER_TILE), qk.enter(it, 4), vv.enter(it, 2)
                transposed(it + 1)
                exponentials(it)
                projected(it + 1)
                A.leave(G - 1), qk.leave(G - 1), vv.leave(G - 1)
            exponentials(G - 1)

            def bu(g):
                act.wait_ge(bu_full, g + 1)
                for c in range(2):
                    last = nc.scalar.activation(state[0][:, c, :, 16:16 + SQ],
                                                shaped(bank(6)[:, c * P:(c + 1) * P], b=BT, t=SQ),
                                                ACT.Copy, scale=gam)
                last.then_inc(bu_evac, 1)

            act.wait_ge(gam_ready, 1)
            act.sem_inc(bu_evac, 1)
            bank_a(oT[:, 0:4, :])
            bank_a(oT[:, 0:4, :])
            with act.Fori(1, G - 1) as g:
                A.enter(g - 1, 2)
                bank_a(x1nT[:, 0:4, :])
                bu(g - 1)
                bank_a(oT[:, 0:4, :])
                A.leave(G - 2)
            for g in (G - 1, G):
                bank_a(x1nT[:, 0:4, :])
                bu(g - 1)

            def z_tile(dst, t):
                return nc.scalar.activation(dst, x_all[:, t, :], ACT.Identity, scale=zscale[:, bass.ds(t, 1)],
                                            bias=zshift[:, bass.ds(t, 1)])

            act.wait_ge(zshift_ready, 1)
            bank_a(tT, shaped(TA[:, 0:2 * P], c=2, m=P))
            with act.Fori(0, STEPS) as step:
                A.enter(step, 4)
                act.wait_ge(b_full, NB2 + 3 * step)
                z_tile(zst, 2 * step).then_inc(z_ready, 1)
                bank_a(zT[:, 0:4, :])
                bank_a(tT, shaped(TA[:, 0:2 * P], c=2, m=P))
                act.wait_ge(b_full, NB2 + 3 * step + 1)
                z_tile(zst, 2 * step + 1).then_inc(z_ready, 1)
                bank_a(zT[:, 0:4, :])
                for i in range(2):
                    act.wait_ge(hsum_ready, 2 * step + i + 1)
                    part = hid[:, i * BANK:(i + 1) * BANK]
                    nc.scalar.activation(part, part, ACT.Gelu).then_inc(hid_ready, 1)
                bank_a(hidT[:, 0:4, :])
                A.leave(STEPS)
            act.wait_ge(g_read, 2 * G + 2)
            with act.Fori(0, G) as g:
                nc.scalar.activation(gate_all[:, g, :], gate_all[:, g, :], ACT.Sigmoid).then_inc(sig_ready, 1)
            bank_a(tT, shaped(TA[:, 0:2 * P], c=2, m=P))
            act.wait_ge(slot_used, BC_DONE)
            for e in range(2):
                z_tile(t_z[e], e).then_inc(tz_ready, 1)
            with act.Fori(1, G // 2) as i:
                for e in range(2):
                    act.wait_ge(tz_used, 2 * i + e - 1)
                    z_tile(t_z[e], 2 * i + e).then_inc(tz_ready, 1)

        @block.vector
        def _(dve):
            chain = Count(dve_chain)
            B = Count(b_free)

            def then(instruction):
                dve.wait_ge(dve_chain, chain.one(instruction))

            def bank_b(dst, src=None):
                dve.wait_ge(b_full, B.term + B.n + 1)
                B.one(nc.vector.tensor_copy(dst, shaped(TB, k=4, n=P) if src is None else src))

            def settled():
                dve.sem_inc(passed_dve, 1)

            def moments(src, eps):
                for i in range(2):
                    ins = nc.vector.bn_stats(s6[:, i, :], src[:, i * BANK:(i + 1) * BANK])
                    chain.one(ins) if i == 0 else then(ins)
                settled()
                then(nc.vector.bn_aggr(mv, s6))
                nc.vector.tensor_scalar_add(veps, mv[:, 1:2], eps).then_inc(var_ready, 1)

            def norm(dst, src, n):
                dve.wait_ge(rstd_ready, n + 1)
                return nc.vector.tensor_scalar(dst, src, mv[:, 0:1], rstd, ALU.subtract, ALU.mult)

            def layer_norm(g):
                dve.wait_ge(x_loaded, 16 * g + 16)
                moments(x_in, LN_EPS)
                norm(xn, x_in, g).then_inc(xn_ready, 1)

            layer_norm(0)

            col = [ssm[:, i:i + 1] for i in range(20)]
            ts, tt, stt = nc.vector.tensor_scalar, nc.vector.tensor_tensor, nc.vector.scalar_tensor_tensor
            dve.wait_ge(ssm_act, 1)
            then(ts(col[4], col[2], 1.0, -1.0, ALU.add, ALU.mult))
            then(ts(col[10], col[3], 1.0 / TWO_PI, None, ALU.mult))
            turns = ssmk[:, 0:1].bitcast(I32)
            then(nc.vector.tensor_copy(turns, col[10]))
            then(nc.vector.tensor_copy(col[10], turns))
            then(stt(col[5], col[10], -6.28125, col[3], ALU.mult, ALU.add))
            then(stt(col[5], col[10], -(TWO_PI - 6.28125), col[5], ALU.mult, ALU.add))
            then(ts(col[11], col[5], TWO_PI / 2, -TWO_PI, ALU.is_gt, ALU.mult))
            then(tt(col[5], col[5], col[11], ALU.add))
            then(ts(col[11], col[5], -TWO_PI / 2, TWO_PI, ALU.is_lt, ALU.mult))
            then(tt(col[5], col[5], col[11], ALU.add))
            ts(col[5], col[5], 3.1415925, -3.1415925, ALU.min, ALU.max).then_inc(ssm_arg, 1)
            dve.wait_ge(ssm_act, 2)
            then(tt(col[11], col[9], col[9], ALU.mult))
            then(ts(col[11], col[11], -2.0, 1.0, ALU.mult, ALU.add))
            then(tt(col[12], col[7], col[7], ALU.mult))
            then(ts(col[12], col[12], -1.0, 1.0, ALU.mult, ALU.add))
            ts(col[12], col[12], 0.0, None, ALU.max).then_inc(ssm_pool, 1)
            then(tt(apow[:, 0, 0:1], col[7], col[11], ALU.mult))
            then(tt(apow[:, 0, 1:2], col[7], col[8], ALU.mult))
            then(ts(apow[:, 0, 2:3], apow[:, 0, 1:2], -1.0, None, ALU.mult))
            for l in range(1, 5):
                re, im = apow[:, l - 1, 0:1], apow[:, l - 1, 1:2]
                then(tt(col[13], im, im, ALU.mult))
                then(tt(col[14], re, re, ALU.mult))
                then(tt(apow[:, l, 0:1], col[14], col[13], ALU.subtract))
                then(tt(col[13], re, im, ALU.mult))
                then(ts(apow[:, l, 1:2], col[13], 2.0, None, ALU.mult))
                then(ts(apow[:, l, 2:3], col[13], -2.0, None, ALU.mult))

            for m in range(4):
                dve.wait_ge(b_full, B.n + 1)
                for r in range(2):
                    n = 4 * m + 2 + r
                    ins = nc.vector.tensor_copy(wkvT[:, :, n * P:(n + 1) * P],
                                                shaped(TB[:, r * 2 * P:(r + 1) * 2 * P], k=KL, n=P))
                B.one(ins)
            with dve.Fori(0, KD // 4) as i:
                B.enter(i, 4)
                for s in range(4):
                    bank_b(wqT[:, 4:8, bass.ds(i * 4 * P + s * P, P)])
                B.leave(KD // 4)

            def transposed(g):
                bank_b(xnT[:, 4:8, :])
                bank_b(woT[:, 0:4, bass.ts(g, P)])
                dve.wait_ge(b_full, B.term + B.n + 1)
                nc.vector.tensor_copy(cT[:, 0, bass.ts(g, P)], TB[:, 0:P])
                nc.vector.tensor_scalar_mul(cT[:, 1, bass.ts(g, P)], TB[:, P:2 * P], -1.0)
                B.one(nc.vector.tensor_copy(bT[:, :, g, :], shaped(TB[:, 2 * P:4 * P], c=2, n=P)))

            def softmax(g):
                dve.wait_ge(s_full, g + 1)
                mask = causal[:, None, :].broadcast_to([P, HEADS // 2, SQ])
                for e in range(2):
                    ins = tt(scores[:, e::2, :], shaped(bank(6 + e)[:, 0:BANK // 2], h=HEADS // 2, k=SQ), mask, ALU.add)
                    chain.one(ins) if e == 0 else ins.then_inc(s_read, 1)
                dve.wait_ge(s_read, g + 2)
                then(nc.vector.reduce_max(mx, scores, axis=AX.X))
                tt(scores, scores, mx[:, :, None].broadcast_to([P, HEADS, SQ]), ALU.subtract)\
                    .then_inc(shifted_ready, 1)
                dve.wait_ge(exp_ready, g + 1)
                then(nc.vector.reduce_sum(rs, shaped(probs, h=HEADS, k=SQ), axis=AX.X))
                then(nc.vector.reciprocal(ri, rs))
                for j in range(BT):
                    r = slice(32 * j, 32 * j + 32)
                    last = nc.vector.transpose(probsT[r, :, 32 * j:32 * j + SQ], probs[r, :])
                last.then_inc(pT_ready, 1)

            def attention_out(g):
                for n in range(2):
                    dve.wait_ge(o_full, 2 * g + n + 1)
                    tt(o_all[:, g, n * BANK:(n + 1) * BANK], bank(4 + n), ri[:, 8 * n:8 * n + 8, None].broadcast_to([P, 8, HD]), ALU.mult)\
                        .then_inc(o_evac, 1)

            transposed(0)
            layer_norm(1)
            dve.wait_ge(const_ready, 1)
            dve.sem_inc(s_read, 1)

            def attend(it, more):
                transposed(it + 1)
                softmax(it)
                if more:
                    layer_norm(it + 2)
                attention_out(it)

            with dve.Fori(0, G - 2) as it:
                B.enter(it, PER_TILE), chain.enter(it, 7)
                attend(it, True)
                B.leave(G - 2), chain.leave(G - 2)
            attend(G - 2, False)
            softmax(G - 1)
            attention_out(G - 1)

            def residual(g):
                dve.wait_ge(x_loaded, 16 * g + 16 * (G + 1))
                for n in range(2):
                    h = slice(n * BANK, (n + 1) * BANK)
                    dve.wait_ge(y_full, 2 * g + n + 1)
                    tt(x1[:, h], x_in[:, h], bank(2 + n), ALU.add).then_inc(y_read, 1)
                dve.wait_ge(y_read, 2 * g + 2)
                moments(x1, LN_EPS)
                norm(x1n, x1, G + g).then_inc(x1n_ready, 1)

            def recurrence(g):
                dve.wait_ge(bu_evac, g + 2)
                for l in range(5):
                    s, src, dst = 2 ** l, state[l % 2], state[(l + 1) % 2]
                    a, b, nb = (apow[:, l, i:i + 1] for i in range(3))
                    now, old = slice(16, 16 + SQ), slice(16 - s, 16 - s + SQ)
                    to = dst[:, :, :, now] if l < 4 else hT
                    then(stt(stmp.rearrange("p c b t -> p (c b) t"),
                             src.rearrange("p c b t -> p (c b) t")[:, :, old], a,
                             src.rearrange("p c b t -> p (c b) t")[:, :, now], ALU.mult, ALU.add))
                    chain.one(stt(to[:, 0], src[:, 1, :, old], nb, stmp[:, 0], ALU.mult, ALU.add))
                    ins = stt(to[:, 1], src[:, 0, :, old], b, stmp[:, 1], ALU.mult, ALU.add)
                    then(ins) if l < 4 else ins.then_inc(h_ready, 1)

            def add_states(g):
                dve.wait_ge(xd_ready, g + 1)
                for n in range(2):
                    h = slice(n * BANK, (n + 1) * BANK)
                    dve.wait_ge(c_full, 2 * g + n + 1)
                    tt(x_all[:, g, h], x_all[:, g, h], bank(4 + n), ALU.add).then_inc(c_read, 1)
                dve.wait_ge(c_read, 2 * g + 2)
                settled()
                for i in range(2):
                    ins = nc.vector.bn_stats(s6[:, i, :], x_all[:, g, i * BANK:(i + 1) * BANK])
                    chain.one(ins) if i == 0 else then(ins)
                settled()
                then(nc.vector.bn_aggr(mv, s6))
                chain.one(nc.vector.tensor_copy(mvz[:, g, :], mv))

            bank_b(oT[:, 4:8, :])
            residual(0)
            bank_b(oT[:, 4:8, :])

            def turn(g, more):
                bank_b(x1nT[:, 4:8, :])
                recurrence(g - 1)
                dve.wait_ge(xd_ready, g)
                residual(g)
                add_states(g - 1)
                if more:
                    bank_b(oT[:, 4:8, :])

            with dve.Fori(1, G - 1) as g:
                B.enter(g - 1, 2), chain.enter(g - 1, 21)
                turn(g, True)
                B.leave(G - 2), chain.leave(G - 2)
            turn(G - 1, False)
            bank_b(x1nT[:, 4:8, :])
            recurrence(G - 1)
            add_states(G - 1)

            dve.wait_ge(dve_chain, chain.n)
            ts(vz, mvz[:, :, 1], LN_EPS, None, ALU.add).then_inc(zv_ready, 1)
            dve.wait_ge(zr_ready, 1)
            then(tt(zshift, mvz[:, :, 0], zscale, ALU.mult))
            ts(zshift, zshift, -1.0, None, ALU.mult).then_inc(zshift_ready, 1)

            st_n, p_n = Count(st_in), Count(p_read)

            def packed_norm(dst, src, eps, n):
                then(nc.vector.bn_stats(s6f, src))
                st_n.one(tt(s24, s6f[:, None, :].broadcast_to([P, NJ, 6]),
                            group_mask[:, :, None].broadcast_to([P, NJ, 6]), ALU.mult))
                dve.wait_ge(st_full, st_n.term + st_n.n)
                settled()
                then(nc.vector.bn_aggr(mv, bank(7)[:, 0:24]))
                nc.vector.tensor_scalar_add(veps, mv[:, 1:2], eps).then_inc(var_ready, 1)
                then(norm(dst, src, n))

            dve.wait_ge(par_loaded, 16 * 7 * NJ)
            dve.wait_ge(p_full, 1)
            dve.wait_ge(const_ready, 1)
            then(nc.vector.tensor_copy(th, bank(6)[:, 0:W4]))
            packed_norm(tn, th, LN_EPS, 2 * G)
            packed_norm(thb, tn, FFN_EPS, 2 * G + 1)
            then(tt(thb, thb, packed["in_g"], ALU.mult))
            tt(tn, thb, packed["in_b"], ALU.add).then_inc(tn_ready, 1)
            dve.wait_ge(slot_used, AGG)
            then(tt(th, bank(6)[:, 0:W4], packed["agg_b"], ALU.add))

            dve.wait_ge(gbias_loaded, 16 * (1 + NJ))
            dve.sem_inc(g_read, 2)

            def gate_sum(t, n):
                h = slice(n * BANK, (n + 1) * BANK)
                dve.wait_ge(g_full, 2 * t + n + 1)
                tt(gate_all[:, t, h], bank(4 + n), gate_bias[:, h], ALU.add).then_inc(g_read, 1)

            def hidden_sum(step, i):
                h = slice(i * BANK, (i + 1) * BANK)
                dve.wait_ge(hp_full, 2 * step + i + 1)
                tt(hid[:, h], bank(2 + i), d1_bias[:, h], ALU.add).then_inc(hsum_ready, 1)

            with dve.Fori(0, STEPS) as step:
                B.enter(step, 3), chain.enter(step, 6), st_n.enter(step, 1)
                bank_b(zT[:, 4:8, :])
                packed_norm(tn, th, FFN_EPS, step + 2 * G + 2)
                then(tt(tn, tn, packed["pn_g"], ALU.mult))
                tt(tn, tn, packed["pn_b"], ALU.add).then_inc(tn_ready, 1)
                then(tt(thb, th, packed["d2_b"], ALU.add))
                for i in range(2):
                    hidden_sum(step, i)
                    gate_sum(2 * step, i)
                bank_b(zT[:, 4:8, :])
                bank_b(hidT[:, 4:8, :])
                for i in range(2):
                    gate_sum(2 * step + 1, i)
                dve.wait_ge(p_full, step + 2)
                then(tt(th, bank(6)[:, 0:W4], thb, ALU.add))
                B.leave(STEPS), chain.leave(STEPS), st_n.leave(STEPS)
            nc.vector.tensor_copy(tn, th).then_inc(tn_ready, 1)

            dve.wait_ge(slot_used, BC_DONE)
            dve.wait_ge(bzero, 1)
            for j in range(NJ):
                r = slice(32 * j, 32 * j + 32)
                last = tt(bcast[r, j, :], bank(6)[r, 0:W4], packed["bc_b"][r, :], ALU.add)
            last.then_inc(bc_ready, 1)

            def finish(t, e):
                mul, z = t_mul[e], t_z[e]
                for n in range(2):
                    h = slice(n * BANK, (n + 1) * BANK)
                    dve.wait_ge(bb_full, 2 * t + n + 1)
                    tt(mul[:, h], bank(2 + 2 * e + n), gate_all[:, t, h], ALU.mult).then_inc(bb_read, 1)
                dve.wait_ge(bb_read, 2 * t + 2)
                dve.wait_ge(tz_ready, t + 1)
                tt(mul, mul, z, ALU.add).then_inc(tz_used, 1)
                dve.wait_ge(tz_used, t + 1)
                moments(mul, FFN_EPS)
                then(stt(mul, mul, mv[:, 0:1], t_gamma, ALU.subtract, ALU.mult))
                dve.wait_ge(rstd_ready, t + (2 * G + STEPS + 3))
                stt(mul, mul, rstd, x_all[:, t, :], ALU.mult, ALU.add).then_inc(tsum_ready, 1)

            dve.wait_ge(tail_in, 32)
            dve.wait_ge(sig_ready, G)
            for e in range(2):
                finish(e, e)
            with dve.Fori(1, G // 2) as i:
                chain.enter(i - 1, 8)
                for e in range(2):
                    t = 2 * i + e
                    dve.wait_ge(fin_ready, t - 1)
                    finish(t, e)
                chain.leave(G // 2 - 1)

        @block.tensor
        def _(pe):
            A, B = Count(a_full), Count(b_full)

            def four(fulls, free, dst, blocks):
                if not (isinstance(fulls.term, int) and fulls.term + fulls.n == 0):
                    pe.wait_ge(free, fulls.term + fulls.n)
                for i, b in enumerate(blocks):
                    last = nc.tensor.transpose(dst[:, i * P:(i + 1) * P], b, ident)
                fulls.one(last)

            def bank_a(*blocks):
                four(A, a_free, TA, blocks)

            def bank_b(*blocks):
                four(B, b_free, TB, blocks)

            def cols(ap, *ks):
                return [ap[:, k * P:(k + 1) * P] for k in ks]

            def product(dst, lhsTs, rhss):
                for k, (l, r) in enumerate(zip(lhsTs, rhss)):
                    last = nc.tensor.matmul(dst, l, r, start=(k == 0), stop=(k == len(lhsTs) - 1))
                return last

            pe.wait_ge(const_ready, 1)
            for s in range(4):
                pe.wait_ge(raw_in[s], 16)
                bank_a(*cols(raw[s], 0, 1, 2, 3))
                bank_b(*cols(raw[s], 4, 5, 6, 7))
            with pe.Fori(0, KD // 4) as i:
                A.enter(i, 4), B.enter(i, 4)
                for s in range(4):
                    pe.wait_ge(raw_in[s], 16 * i + 32)
                    bank_a(*cols(raw[s], 0, 1, 2, 3))
                    bank_b(*cols(raw[s], 4, 5, 6, 7))
                A.leave(KD // 4), B.leave(KD // 4)

            def transposes(g):
                pe.wait_ge(xn_ready, g + 1)
                bank_a(*cols(xn, 0, 1, 2, 3))
                bank_b(*cols(xn, 4, 5, 6, 7))
                pe.wait_ge(ctx_loaded, 16 * BT * g + 16 * BT)
                bank_a(*cols(ctx_in, 0, 1))
                pe.wait_ge(wo_loaded, 16 * g + 16)
                bank_b(*cols(raw_wo, 0, 1, 2, 3))
                bank_a(*cols(raw_wo, 4, 5, 6, 7))
                pe.wait_ge(bc_loaded, 64 * g + 64)
                bank_b(*cols(raw_bc, 0, 1, 2, 3))

            def heads_product(g, f, w, acts, ks, w0, fulls):
                for c in range(4 * (f % 2), 4 * (f % 2) + 4):
                    last = product(bank(2 + f % 2)[:, (c % 4) * P:(c % 4 + 1) * P],
                                   [w[:, k, w0 + c * P:w0 + (c + 1) * P] for k in range(ks)],
                                   [acts[:, k, :] for k in range(ks)])
                last.then_inc(qk_full, 1)

            def queries(g, first):
                pe.wait_ge(a_free, A.term + A.n)
                pe.wait_ge(b_free, B.term + B.n)
                for f in range(2):
                    if not first:
                        pe.wait_ge(qk_evac, 4 * g - 1 + f)
                    heads_product(g, f, wqT, xnT, KD, 0, None)

            def keys(g):
                for f in range(2):
                    pe.wait_ge(qk_evac, 4 * g + f + 1)
                    heads_product(g, 2 + f, wkvT, ctxT, KL, 0, None)

            def values(g, first):
                for n in range(2):
                    if not first:
                        pe.wait_ge(o_evac, 2 * g - 1 + n)
                    product(bank(4 + n), [ctxT[:, k, :] for k in range(KL)],
                            [wkvT[:, k, D + n * BANK:D + (n + 1) * BANK] for k in range(KL)]).then_inc(v_full, 1)

            def score(g):
                pe.wait_ge(qk_evac, 4 * g + 4)
                pe.wait_ge(s_read, g + 1)
                pe.sem_inc(passed_pe, 1)
                for c in range(KD):
                    for e in range(2):
                        for j in range(BT):
                            r, t = slice(64 * e, 64 * e + HD), slice(32 * j, 32 * j + SQ)
                            last = nc.tensor.matmul(bank(6 + e)[t, c * SQ:(c + 1) * SQ], qT[r, c, t], kT[r, c, t],
                                                    start=True, stop=True)
                last.then_inc(s_full, 1)

            def weighted(g):
                pe.wait_ge(pT_ready, g + 1)
                pe.wait_ge(v_evac, 2 * g + 2)
                for n in range(2):
                    for h in range(8 * n, 8 * n + 8):
                        last = nc.tensor.matmul(bank(4 + n)[:, (h % 8) * HD:(h % 8 + 1) * HD], probsT[:, h, :],
                                                v[:, h * HD:(h + 1) * HD], start=True, stop=True)
                    last.then_inc(o_full, 1)

            transposes(0)
            queries(0, True)
            keys(0)
            values(0, True)
            with pe.Fori(0, G - 1) as it:
                A.enter(it, PER_TILE), B.enter(it, PER_TILE)
                score(it)
                transposes(it + 1)
                queries(it + 1, False)
                weighted(it)
                keys(it + 1)
                values(it + 1, False)
                A.leave(G - 1), B.leave(G - 1)
            score(G - 1)
            weighted(G - 1)

            def load_o(g):
                pe.wait_ge(ost_ready, g + 1)
                bank_a(*cols(o_st, 0, 1, 2, 3))
                bank_b(*cols(o_st, 4, 5, 6, 7))

            def project(g, first):
                for n in range(2):
                    if not first:
                        pe.wait_ge(y_read, 2 * g - 1 + n)
                    product(bank(2 + n), [oT[:, k, :] for k in range(KD)],
                            [woT[:, k, n * BANK:(n + 1) * BANK] for k in range(KD)]).then_inc(y_full, 1)

            def inputs(g):
                pe.wait_ge(x1n_ready, g + 1)
                bank_a(*cols(x1n, 0, 1, 2, 3))
                bank_b(*cols(x1n, 4, 5, 6, 7))
                pe.wait_ge(bu_evac, g + 1)
                pe.wait_ge(a_free, A.term + A.n)
                pe.wait_ge(b_free, B.term + B.n)
                for c in range(2):
                    last = product(bank(6)[:, c * P:(c + 1) * P], [bT[:, c, k, :] for k in range(KD)],
                                   [x1nT[:, k, :] for k in range(KD)])
                last.then_inc(bu_full, 1)

            def outputs(g, first):
                pe.wait_ge(h_ready, g + 1)
                for n in range(2):
                    if not first:
                        pe.wait_ge(c_read, 2 * g - 1 + n)
                    product(bank(4 + n), [hT[:, c].rearrange("p b t -> p (b t)") for c in range(2)],
                            [cT[:, c, n * BANK:(n + 1) * BANK] for c in range(2)]).then_inc(c_full, 1)

            load_o(0)
            pe.wait_ge(a_free, A.n)
            pe.wait_ge(b_free, B.n)
            project(0, True)
            load_o(1)

            def turn(g, first, more):
                inputs(g - 1)
                project(g, False)
                outputs(g - 1, first)
                if more:
                    load_o(g + 1)

            turn(1, True, True)
            with pe.Fori(2, G - 1) as g:
                A.enter(g - 2, 2), B.enter(g - 2, 2)
                turn(g, False, True)
                A.leave(G - 3), B.leave(G - 3)
            turn(G - 1, False, False)
            inputs(G - 1)
            outputs(G - 1, False)

            pe.wait_ge(const_ready, 1)
            pe.wait_ge(c_read, 2 * G)
            for g in range(G):
                for j in range(NJ):
                    last = nc.tensor.matmul(bank(6)[32 * j:32 * j + 32, 0:W4], last_rows[:, g * NB:(g + 1) * NB],
                                            x_all[:, g, j * W4:(j + 1) * W4], start=(g == 0), stop=(g == G - 1))
            last.then_inc(p_full, 1)

            fills = [Count(s) for s in slot_in]
            used = Count(slot_used)

            def stats(n):
                pe.wait_ge(st_in, n)
                nc.tensor.matmul(bank(7)[:, 0:24], same_row, small[:, 107:131], start=True, stop=True)\
                    .then_inc(st_full, 1)

            def transposed_thought(n):
                pe.wait_ge(tn_ready, n)
                bank_a(*cols(tn, 0, 1))
                pe.wait_ge(a_free, A.term + A.n)

            def streamed(s):
                fills[s].n += 16
                pe.wait_ge(slot_in[s], fills[s].term + fills[s].n)

            def rows_product(n0):
                for n in range(AGG):
                    s = (n0 + n) % RING
                    streamed(s)
                    piece = shaped(ring[s], j=2, n=D)
                    for c in range(2):
                        k = 2 * n + c
                        for j in range(NJ):
                            last = nc.tensor.matmul(bank(6)[32 * j:32 * j + 32, 0:W4],
                                                    tT[:, k % 2, 32 * (k // 2):32 * (k // 2) + 32],
                                                    piece[:, c, j * W4:(j + 1) * W4],
                                                    start=(k == 0), stop=(k == KD - 1))
                    used.one(last)

            stats(1)
            stats(2)
            transposed_thought(1)
            rows_product(0)
            pe.wait_ge(res_in, 16 * RES)
            pe.wait_ge(gw_loaded, 16)

            def z_transposes(t):
                pe.wait_ge(z_ready, t + 1)
                bank_a(*cols(zst, 0, 1, 2, 3))
                bank_b(*cols(zst, 4, 5, 6, 7))

            def gate_product(t, u):
                n, k = divmod(u, KD)
                if k == 0:
                    pe.wait_ge(g_read, 2 * t + n + 1)
                last = nc.tensor.matmul(bank(4 + n), zT[:, k, :], gw[:, k, n * BANK:(n + 1) * BANK],
                                        start=(k == 0), stop=(k == KD - 1))
                if k == KD - 1:
                    last.then_inc(g_full, 1)

            def next_piece(q, m):
                if q in RESIDENT_Q:
                    return as_piece(resident[RESIDENT_Q.index(q)], q), m
                streamed((AGG + m) % RING)
                return as_piece(ring[(AGG + m) % RING], q), m + 1

            with pe.Fori(0, STEPS) as step:
                A.enter(step, 4), B.enter(step, 3), used.enter(step, N_RING)
                for f in fills:
                    f.enter(step, 16 * N_RING // RING)
                m = 0
                z_transposes(2 * step)
                stats(step + 3)
                transposed_thought(step + 2)
                pe.wait_ge(b_free, B.term + B.n)
                for q in range(D1P):
                    i, k = divmod(q, KD)
                    piece, m = next_piece(q, m)
                    for j in range(NJ):
                        last = nc.tensor.matmul(bank(2 + i)[32 * j:32 * j + 32, :],
                                                tT[:, k % 2, 32 * (k // 2):32 * (k // 2) + 32],
                                                piece[:, j, :], start=(k == 0), stop=(k == KD - 1))
                    if k == KD - 1:
                        last.then_inc(hp_full, 1)
                    else:
                        used.one(last) if q not in RESIDENT_Q else None
                    gate_product(2 * step, q)
                z_transposes(2 * step + 1)
                pe.wait_ge(hid_ready, 2 * step + 1)
                bank_a(*cols(hid, 0, 1, 2, 3))
                pe.wait_ge(hid_ready, 2 * step + 2)
                bank_b(*cols(hid, 4, 5, 6, 7))
                pe.wait_ge(a_free, A.term + A.n)
                for q in range(D1P, PIECES):
                    c, jp = divmod(q - D1P, 2)
                    if c == H4 // P // 2 and jp == 0:
                        pe.wait_ge(b_free, B.term + B.n)
                    piece, m = next_piece(q, m)
                    for jj in range(2):
                        j = 2 * jp + jj
                        for n in range(NJ):
                            last = nc.tensor.matmul(bank(6)[32 * n:32 * n + 32, 0:W4],
                                                    hidT[:, c, 32 * j:32 * j + 32],
                                                    piece[:, jj, n * W4:(n + 1) * W4],
                                                    start=(c == 0 and j == 0), stop=(q == PIECES - 1 and jj == 1))
                    if q == PIECES - 1:
                        last.then_inc(p_full, 1)
                    elif q not in RESIDENT_Q:
                        used.one(last)
                    gate_product(2 * step + 1, q - D1P)
                A.leave(STEPS), B.leave(STEPS), used.leave(STEPS)
                for f in fills:
                    f.leave(STEPS)
            transposed_thought(STEPS + 2)
            rows_product(AGG + STEPS * N_RING)

            pe.wait_ge(bc_ready, 1)
            pe.wait_ge(g_read, 2 * G + 2)
            for t in range(G):
                for n in range(2):
                    if t >= 2:
                        pe.wait_ge(bb_read, 2 * t - 3 + n)
                    nc.tensor.matmul(bank(2 + 2 * (t % 2) + n), spread[:, t, :],
                                     bcast.rearrange("p j n -> p (j n)")[:, n * BANK:(n + 1) * BANK],
                                     start=True, stop=True).then_inc(bb_full, 1)


_INS = ["x", "ctx_512", "L0_xattn_Wq", "L0_xattn_Wkv_expand", "L0_xattn_Wout", "L0_attn_nu_log",
        "L0_attn_theta_log", "L0_attn_B_re", "L0_attn_B_im", "L0_attn_C_re", "L0_attn_C_im", "L0_attn_D",
        "L0_ffn_in_gamma", "L0_ffn_in_beta", "L0_ffn_agg_w", "L0_ffn_agg_b", "L0_ffn_pn_gamma",
        "L0_ffn_pn_beta", "L0_ffn_d1_w", "L0_ffn_d1_b", "L0_ffn_d2_w", "L0_ffn_d2_b", "L0_ffn_bc_w",
        "L0_ffn_bc_b", "L0_ffn_gate_w", "L0_ffn_gate_b", "L0_ffn_out_gamma", "L0_ffn_out_beta"]


def kernel(**inputs):
    import numpy as _np
    import concourse.bacc as _bacc
    from concourse import mybir as _mybir
    from concourse.bass_utils import run_bass_kernel_spmd as _run

    nc = _bacc.Bacc("TRN2", target_bir_lowering=False, num_devices=1)
    arrays, args = {}, []
    for name in _INS:
        a = _np.ascontiguousarray(inputs[name])
        arrays[f"in_{name}_dram"] = a
        args.append(nc.dram_tensor(f"in_{name}_dram", a.shape, _mybir.dt.from_np(a.dtype), kind="ExternalInput").ap())
    shape = inputs["x"].shape
    args.append(nc.dram_tensor("out_0_dram", shape, _mybir.dt.float32, kind="ExternalOutput").ap())
    build(nc, *args)
    r = _run(nc, [arrays], core_ids=[0])
    return r.results[0]["out_0_dram"]
```

```python
from contextlib import ExitStack

import concourse.bass as bass
from concourse import mybir

F32 = mybir.dt.float32
I32 = mybir.dt.int32
ALU = mybir.AluOpType
ACT = mybir.ActivationFunctionType
AX = mybir.AxisListType

P = 128
BANK = 512
TWO_PI = 6.283185307179586
MASKED = -1.0e38
LN_EPS = 1e-5
FFN_EPS = 1e-6


class Count:

    def __init__(self, sem):
        self.sem, self.n, self.term = sem, 0, 0

    def one(self, instruction, by=1):
        instruction.then_inc(self.sem, by)
        self.n += by
        return self.term + self.n

    def enter(self, turn, per_turn):
        self.start, self.per_turn, self.term = self.n, per_turn, turn * per_turn

    def leave(self, turns):
        assert self.n - self.start == self.per_turn, (self.n - self.start, self.per_turn)
        self.n, self.term = self.start + turns * self.per_turn, 0


def build(nc, x, ctx_512, Wq, Wkv, Wout, nu_log, theta_log, B_re, B_im, C_re, C_im, Dskip,
          in_gamma, in_beta, agg_w, agg_b, pn_gamma, pn_beta, d1_w, d1_b, d2_w, d2_b,
          bc_w, bc_b, gate_w, gate_b, out_gamma, out_beta, out):
    NB, SQ, D = x.shape
    L = ctx_512.shape[2]
    HEADS = 16
    HD = D // HEADS
    KD, KL = D // P, L // P
    BT = P // SQ
    G = NB // BT
    NST = nu_log.shape[0]
    HID = d1_w.shape[1]
    NJ = 4
    W4 = D // NJ
    H4 = HID // NJ
    STEPS = 4
    assert SQ == 32 and P == NST and L == 2 * P and W4 == 256 and H4 == 2 * BANK

    x_t = x.rearrange("b s d -> (b s) d").rearrange("(g p) d -> g p d", p=P)
    out_t = out.rearrange("b s d -> (b s) d").rearrange("(g p) d -> g p d", p=P)
    wo_t = Wout.rearrange("(g p) d -> g p d", p=P)

    with ExitStack() as ctx:
        mem = ctx.enter_context(nc.sbuf_tensor("mem", [P, 53200], F32))
        ps = ctx.enter_context(nc.psum_tensor("ps", [P, 8 * BANK], F32))
        top = [0]

        def take(cols, at=None):
            lo = top[0] if at is None else at
            if at is None:
                top[0] += cols
            assert lo + cols <= 53200, lo + cols
            return mem[:, lo:lo + cols]

        def shaped(ap, **dims):
            return ap.rearrange("p (" + " ".join(dims) + ") -> p " + " ".join(dims), **dims)

        R_WQ = 0
        R_WKV = KD * D
        R_O = R_WKV + KL * 2 * D
        R_WO = R_O + G * D
        R_BC = R_WO + KD * D
        R_T = R_BC + 4 * D
        wqT = shaped(take(KD * D, R_WQ), k=KD, n=D)
        wkvT = shaped(take(KL * 2 * D, R_WKV), k=KL, n=2 * D)
        o_all = shaped(take(G * D, R_O), g=G, n=D)
        woT = shaped(take(KD * D, R_WO), k=KD, n=D)
        bT = shaped(take(2 * D, R_BC), c=2, k=KD, n=NST)
        cT = shaped(take(2 * D, R_BC + 2 * D), c=2, n=D)
        gw = shaped(take(KD * D, R_WO), k=KD, n=D)
        raw = [take(D, R_T + i * D) for i in range(4)]
        qT = shaped(take(D, R_T + 4 * D), c=KD, t=P)
        kT = shaped(take(D, R_T + 5 * D), c=KD, t=P)
        v = take(D, R_T + 6 * D)
        ctx_in = take(L, R_T + 7 * D)
        ctxT = shaped(take(L, R_T + 7 * D + L), k=KL, t=P)
        raw_bc = take(4 * P, R_T + 7 * D + 2 * L)
        top[0] = R_T + 8 * D
        R_U = top[0]
        x_in = take(D)
        xn = take(D)
        xnT = shaped(take(D), k=KD, t=P)
        raw_wo = take(D)
        scores = shaped(take(HEADS * SQ), h=HEADS, k=SQ)
        probs = take(HEADS * SQ)
        probsT = shaped(take(HEADS * P), h=HEADS, q=P)
        o_st = take(D, R_T)
        oT = shaped(take(D, R_T + D), k=KD, t=P)
        xd = take(D, R_U + D)
        x2 = take(D, R_U + 2 * D)
        xd_last = take(D, R_U + 3 * D)
        x2_last = xd
        x1 = take(D, R_U + 4 * D)
        x1n = take(D, R_U + 5 * D)
        x1nT = shaped(take(D, R_U + 6 * D), k=KD, t=P)
        top[0] = R_U + 7 * D
        R_STATE = top[0]
        state = [shaped(take(2 * BT * 48), c=2, b=BT, t=48) for _ in range(2)]
        stmp = shaped(take(2 * P), c=2, b=BT, t=SQ)
        R_H = top[0]
        hT = shaped(take(2 * P), c=2, b=BT, t=SQ)
        R_SKIP = top[0]
        dskip = take(D)
        zst = take(D, R_U)
        zT = shaped(take(D, R_U + D), k=KD, t=P)
        hid = take(H4, R_T)
        hidT = shaped(take(H4, R_T + D), c=H4 // P, m=P)
        th = take(W4, R_U + 4 * D)
        thb = take(W4, R_U + 4 * D + W4)
        tn = take(W4, R_U + 4 * D + 2 * W4)
        bcast = shaped(take(D, R_U + 5 * D), j=NJ, n=W4)
        gate_out = take(D, R_U + 5 * D)
        gate_bias = take(D, R_U + 6 * D)
        d1_bias = take(H4, R_SKIP)
        spread = shaped(take(G * P, R_STATE), g=G, t=P)
        tT = shaped(take(2 * P, R_H), c=2, m=P)
        back = shaped(take(G * 2 * D, R_WQ), t=G, w=2 * D)
        x_back, gate_back = back[:, :, 0:D], back[:, :, D:2 * D]
        t_z = [take(D, R_WO + i * D) for i in range(6)] + [take(D, R_O + (4 + i) * D) for i in range(2)]
        t_gamma = take(D, R_WO + 6 * D)
        t_beta = take(D, R_WO + 7 * D)
        packed_names = ["in_g", "in_b", "agg_b", "pn_g", "pn_b", "d2_b", "bc_b"]
        packed = {n: take(W4) for n in packed_names}
        ident = take(P)
        same_row = take(P)
        causal = take(SQ)
        group_mask = take(NJ)
        small = take(176)
        mvz = shaped(take(2 * G), g=G, c=2)
        zscale = take(G)
        zshift = take(G)

        SLOT = 2 * D
        ring = [take(SLOT, R_T + (1 + i) * SLOT) for i in range(3)] + [take(SLOT, R_WKV + SLOT)]
        resident = [take(SLOT, R_WQ + i * SLOT) for i in range(4)] + [take(SLOT, R_WKV), take(SLOT, R_U + 2 * D)] \
            + [take(SLOT, R_O + i * SLOT) for i in range(4)] + [take(SLOT, R_BC + i * SLOT) for i in range(2)]
        RING, RES = len(ring), len(resident)
        EARLY = 5
        D1P = 2 * KD
        D2P = HID // P // 2
        PIECES = D1P + D2P
        assert (PIECES - RES) % RING == 0

        s6 = shaped(small[:, 0:12], a=2, c=6)
        mv = small[:, 12:14]
        veps = small[:, 14:15]
        rstd = small[:, 15:16]
        power = small[:, 16:17]
        mx = small[:, 17:33]
        rs = small[:, 33:49]
        ri = small[:, 49:65]
        ssm = small[:, 65:85]
        apow = shaped(small[:, 85:100], l=5, c=3)
        gam = small[:, 100:101]
        s6x = shaped(small[:, 160:172], a=2, c=6)
        mvx = small[:, 172:174]
        s6f = small[:, 101:107]
        s24 = shaped(small[:, 107:131], j=NJ, c=6)
        ssmk = small[:, 131:133]
        powers8 = small[:, 133:141]
        half = small[:, 141:142]
        vz = small[:, 142:150]
        t_mv = [small[:, 152 + 2 * e:154 + 2 * e] for e in range(2)]
        t_rstd = [small[:, 156 + e:157 + e] for e in range(2)]
        t_shift = [small[:, 158 + e:159 + e] for e in range(2)]

        x2_d = nc.dram_tensor("x2_spill", [G, P, D], F32, kind="Internal").ap()
        gate_d = nc.dram_tensor("gate_spill", [G, P, D], F32, kind="Internal").ap()

        def bank(i, cols=BANK):
            return ps[:, i * BANK:i * BANK + cols]

        TA, TB = bank(0), bank(1)

        def sem(name):
            return ctx.enter_context(nc.semaphore(name))

        const_ready = sem("const_ready")
        ssm_in = sem("ssm_in")
        gam_ready = sem("gam_ready")
        ssm_pool = sem("ssm_pool")
        ssm_act = sem("ssm_act")
        ssm_arg = sem("ssm_arg")
        dve_chain = sem("dve_chain")
        act_chain = sem("act_chain")
        pool_chain = sem("pool_chain")
        raw_in = [sem(f"raw_in{i}") for i in range(4)]
        x_loaded = sem("x_loaded")
        ctx_loaded = sem("ctx_loaded")
        wo_loaded = sem("wo_loaded")
        bc_loaded = sem("bc_loaded")
        dskip_loaded = sem("dskip_loaded")
        a_full, a_free = sem("a_full"), sem("a_free")
        b_full, b_free = sem("b_full"), sem("b_free")
        var_ready = sem("var_ready")
        rstd_ready = sem("rstd_ready")
        xn_ready = sem("xn_ready")
        qk_full, qk_evac = sem("qk_full"), sem("qk_evac")
        v_full, v_evac = sem("v_full"), sem("v_evac")
        o_full, o_evac = sem("o_full"), sem("o_evac")
        s_full, s_read = sem("s_full"), sem("s_read")
        shifted_ready = sem("shifted_ready")
        exp_ready = sem("exp_ready")
        pT_ready = sem("pT_ready")
        ost_ready = sem("ost_ready")
        y_full, y_read = sem("y_full"), sem("y_read")
        x1_ready = sem("x1_ready")
        x1n_ready = sem("x1n_ready")
        xd_ready = sem("xd_ready")
        bu_full, bu_evac = sem("bu_full"), sem("bu_evac")
        h_ready = sem("h_ready")
        c_full, c_read = sem("c_full"), sem("c_read")
        par_loaded = sem("par_loaded")
        gbias_loaded = sem("gbias_loaded")
        gw_loaded = sem("gw_loaded")
        slot_in = [sem(f"slot_in{i}") for i in range(RING)]
        slot_used = sem("slot_used")
        res_in = sem("res_in")
        zv_ready, zr_ready = sem("zv_ready"), sem("zr_ready")
        st_in, st_full = sem("st_in"), sem("st_full")
        tn_ready = sem("tn_ready")
        z_ready = sem("z_ready")
        p_full, p_read = sem("p_full"), sem("p_read")
        hp_full, hp_read = sem("hp_full"), sem("hp_read")
        hsum_ready, hid_ready = sem("hsum_ready"), sem("hid_ready")
        g_full, g_read = sem("g_full"), sem("g_read")
        sig_ready = sem("sig_ready")
        x2_stored = sem("x2_stored")
        res_late = sem("res_late")
        th_loaded, zx_loaded = sem("th_loaded"), sem("zx_loaded")
        gate_stored = sem("gate_stored")
        back_in = [sem(f"back_in{i}") for i in range(2)]
        norm_arg, normed, scaled, skip_ready = sem("norm_arg"), sem("normed"), sem("scaled"), sem("skip_ready")
        bc_ready = sem("bc_ready")
        tail_in = sem("tail_in")
        bb_full, bb_read = sem("bb_full"), sem("bb_read")
        tz_ready = sem("tz_ready")
        fin_ready = sem("fin_ready")
        xd_half, bzero, tsum_ready = sem("xd_half"), sem("bzero"), sem("tsum_ready")
        zshift_ready, tz_used = sem("zshift_ready"), sem("tz_used")
        passed_dve, passed_pool, passed_pe = sem("passed_dve"), sem("passed_pool"), sem("passed_pe")
        out_done = sem("out_done")
        z_added, centred = sem("z_added"), sem("centred")

        block = ctx.enter_context(nc.Block())

        NA0 = NB0 = KD + 4
        PER_TILE = 3
        NB1 = NB0 + PER_TILE * G
        N_RING = PIECES - RES
        RESIDENT_Q = [1, 4, 7, 10, 12, 15, 18, 20, 22, 24, 28, 31]
        BC_DONE = 2 * (KD // 2) + STEPS * N_RING
        NB2 = NB1 + 2 * G
        AGG = KD // 2
        chunk_of = [(j, c) for j in range(NJ) for c in range(2)]

        def piece_source(q):
            if q < D1P:
                i, k = divmod(q, KD)
                return d1_w[k * P:(k + 1) * P, :].rearrange("p (j n) -> p j n", j=NJ)[:, :, i * BANK:(i + 1) * BANK]
            c, jp = divmod(q - D1P, 2)
            return d2_w.rearrange("(j c p) n -> p c j n", j=NJ, c=H4 // P)[:, c, 2 * jp:2 * jp + 2, :]

        def as_piece(slot, q):
            return shaped(slot, j=NJ, n=BANK) if q < D1P else shaped(slot, j=2, n=D)

        @block.sync
        def _(sp):
            def load_ctx(g):
                for j in range(BT):
                    sp.dma_start(ctx_in[32 * j:32 * j + SQ, :], ctx_512[g * BT + j, 0:SQ, :])\
                      .then_inc(ctx_loaded, 16)

            def load_prep(g):
                sp.dma_start(raw_wo, wo_t[g, :, :]).then_inc(wo_loaded, 16)
                for n, w in enumerate((C_re, C_im)):
                    sp.dma_start(raw_bc[:, n * P:(n + 1) * P], w[bass.ts(g, P), :]).then_inc(bc_loaded, 16)
                for n, w in enumerate((B_re, B_im)):
                    sp.dma_start(raw_bc[:, (2 + n) * P:(3 + n) * P], w[:, bass.ts(g, P)])\
                      .then_inc(bc_loaded, 16)

            sp.dma_start(x_in, x_t[0, :, :]).then_inc(x_loaded, 16)
            for n in range(KD + 4):
                s = n % 4
                if n >= 4:
                    sp.wait_ge(a_free, n - 3)
                    sp.wait_ge(b_free, n - 3)
                if n >= 4:
                    sp.dma_start(raw[s], Wq[(n - 4) * P:(n - 3) * P, :]).then_inc(raw_in[s], 16)
                else:
                    sp.dma_start(shaped(raw[s], r=4, n=L),
                                 Wkv[4 * n * P:4 * (n + 1) * P, :].rearrange("(r p) n -> p r n", p=P))\
                      .then_inc(raw_in[s], 16)
                if n == 3:
                    load_ctx(0)
            load_prep(0)
            sp.wait_ge(xn_ready, 1)
            sp.dma_start(x_in, x_t[1, :, :]).then_inc(x_loaded, 16)
            sp.dma_start(dskip, Dskip[None, :].broadcast_to([P, D])).then_inc(dskip_loaded, 16)

            def next_tile(it):
                sp.wait_ge(a_free, NA0 + PER_TILE * it + PER_TILE)
                sp.wait_ge(b_free, NB0 + PER_TILE * it + PER_TILE)
                load_ctx(it + 1)
                load_prep(it + 1)
                sp.wait_ge(xn_ready, it + 2)

            with sp.Fori(0, G - 2) as it:
                next_tile(it)
                sp.dma_start(x_in, x_t[it + 2, :, :]).then_inc(x_loaded, 16)
            next_tile(G - 2)
            sp.dma_start(x_in, x_t[0, :, :]).then_inc(x_loaded, 16)

            for name, w in (("in_g", in_gamma), ("in_b", in_beta), ("agg_b", agg_b), ("pn_g", pn_gamma),
                            ("pn_b", pn_beta), ("d2_b", d2_b), ("bc_b", bc_b)):
                for j in range(NJ):
                    sp.dma_start(packed[name][32 * j:32 * j + 32, :],
                                 w[None, j * W4:(j + 1) * W4].broadcast_to([32, W4])).then_inc(par_loaded, 16)

            bc_v = bc_w.rearrange("(n j p) d -> n p j d", j=2, p=P)

            def store_x2(g, x2=x2):
                sp.wait_ge(c_read, 2 * g + 3)
                sp.dma_start(x2_d[g, :, :], x2).then_inc(x2_stored, 16)

            def next_x(g):
                sp.wait_ge(y_read, 2 * g)
                sp.dma_start(x_in, x_t[g, :, :]).then_inc(x_loaded, 16)

            def load_resident(r):
                sp.dma_start(as_piece(resident[r], RESIDENT_Q[r]), piece_source(RESIDENT_Q[r])).then_inc(res_late, 16)

            next_x(1)
            d2_v = d2_w.rearrange("(j c p) n -> p c j n", j=NJ, c=H4 // P)
            with sp.Fori(1, G // 2) as i:
                next_x(2 * i)
                store_x2(2 * i - 2)
                next_x(2 * i + 1)
                store_x2(2 * i - 1)
                sp.wait_ge(ost_ready, 2 * i)
                sp.dma_start(shaped(mem[:, bass.ds(i * SLOT + (R_O - SLOT), SLOT)], j=2, n=D),
                             d2_v[:, bass.ds(i, 1), 0:2, :].rearrange("p c j n -> p (c j) n")).then_inc(res_late, 16)
            sp.wait_ge(ost_ready, G)
            load_resident(EARLY + 4)
            sp.wait_ge(y_full, 2 * G)
            sp.dma_start(gw, gate_w.rearrange("(k p) n -> p k n", p=P)).then_inc(gw_loaded, 16)
            last = x2_d.rearrange("g (b s) d -> (g b) s d", s=SQ)
            old = NB - 2 * BT
            sp.wait_ge(xd_ready, G)
            sp.wait_ge(x2_stored, 16 * (G - 2))
            for j in range(NJ):
                sp.dma_start(th[32 * j:32 * j + old, :], last[0:old, SQ - 1, j * W4:(j + 1) * W4])\
                  .then_inc(th_loaded, 16)
            sp.wait_ge(bu_full, G)
            load_resident(RES - 2)
            sp.dma_start(gate_bias, gate_b[None, :].broadcast_to([P, D])).then_inc(gbias_loaded, 16)
            for j in range(NJ):
                sp.dma_start(d1_bias[32 * j:32 * j + 32, :],
                             d1_b[None, j * H4:(j + 1) * H4].broadcast_to([32, H4])).then_inc(gbias_loaded, 16)
            for g, tile in ((G - 2, x2), (G - 1, x2_last)):
                sp.wait_ge(c_read, 2 * g + 3)
                for j in range(NJ):
                    sp.dma_start(th[32 * j + g * BT:32 * j + (g + 1) * BT, :],
                                 tile[SQ - 1::SQ, j * W4:(j + 1) * W4]).then_inc(th_loaded, 16)
            store_x2(G - 2)
            store_x2(G - 1, x2_last)
            sp.wait_ge(c_full, 2 * G)
            load_resident(RES - 1)
            sp.wait_ge(zv_ready, 1)
            sp.wait_ge(th_loaded, 48 * NJ)
            sp.wait_ge(x2_stored, 16 * G)
            load_resident(EARLY)

            with sp.Fori(0, STEPS) as step:
                m = 0
                for q in range(PIECES):
                    if q in RESIDENT_Q:
                        continue
                    s = (AGG + m) % RING
                    sp.wait_ge(slot_used, N_RING * step + AGG + m - RING + 1)
                    sp.dma_start(as_piece(ring[s], q), piece_source(q)).then_inc(slot_in[s], 16)
                    m += 1
            for n in range(AGG):
                m = AGG + STEPS * N_RING + n
                sp.wait_ge(slot_used, m - RING + 1)
                sp.dma_start(shaped(ring[m % RING], j=2, n=D), bc_v[n, :, :, :]).then_inc(slot_in[m % RING], 16)
            sp.wait_ge(g_read, 2 * G + 2)
            sp.dma_start(t_gamma, out_gamma[None, :].broadcast_to([P, D])).then_inc(tail_in, 16)
            sp.dma_start(t_beta, out_beta[None, :].broadcast_to([P, D])).then_inc(tail_in, 16)
            sp.wait_ge(gate_stored, 16 * (G + 1))
            sp.wait_ge(p_full, STEPS)
            for t in range(G):
                if t == 5:
                    sp.wait_ge(slot_used, BC_DONE)
                if t >= 2:
                    sp.wait_ge(back_in[t % 2], 32 * (t // 2))
                sp.dma_start(x_back[:, t, :], x2_d[t, :, :]).then_inc(back_in[t % 2], 16)
                sp.dma_start(gate_back[:, t, :], gate_d[t, :, :]).then_inc(back_in[t % 2], 16)
            for t in range(G):
                sp.wait_ge(fin_ready, t + 1)
                sp.dma_start(out_t[t, :, :], x_back[:, t, :]).then_inc(out_done, 16)
            sp.wait_ge(out_done, 16 * G)

        @block.gpsimd
        def _(pool):
            chain = Count(pool_chain)

            def then(instruction):
                pool.wait_ge(pool_chain, chain.one(instruction))

            def ones_where_zero(ap, base, pattern):
                return nc.gpsimd.affine_select(out=ap, in_=ap, compare_op=ALU.not_equal, fill=1.0, base=base,
                                               pattern=pattern, channel_multiplier=1)

            then(nc.gpsimd.memset(ident, 0.0))
            then(ones_where_zero(ident, 0, [[-1, P]]))
            then(nc.gpsimd.memset(power, -0.5))
            then(nc.gpsimd.memset(powers8, -0.5))
            then(nc.gpsimd.memset(half, 0.5))
            quad = shaped(probsT[:, 0, :], j=BT, k=SQ)
            then(nc.gpsimd.memset(quad, 0.0))
            then(nc.gpsimd.affine_select(out=quad, in_=quad, compare_op=ALU.is_ge, fill=MASKED, base=0,
                                         pattern=[[-SQ, BT], [-1, SQ]], channel_multiplier=1))
            for j in range(BT):
                then(nc.gpsimd.tensor_copy(causal[32 * j:32 * j + 32, :], quad[32 * j:32 * j + 32, j, :]))
            then(nc.gpsimd.memset(probsT, 0.0))
            for u in state:
                then(nc.gpsimd.memset(u, 0.0))
            nc.gpsimd.memset(group_mask, 0.0).then_inc(const_ready, 1)

            def power_of(dst, src, exponent):
                return nc.gpsimd.tensor_tensor(dst, src, exponent, ALU.pow)

            pool.wait_ge(var_ready, 1)
            power_of(rstd, veps, power).then_inc(rstd_ready, 1)
            pool.wait_ge(const_ready, 1)
            for j in range(NJ):
                then(nc.gpsimd.memset(group_mask[32 * j:32 * j + 32, j:j + 1], 1.0))
            then(nc.gpsimd.memset(same_row, 0.0))
            for m in range(1 - NJ, NJ - 1):
                then(ones_where_zero(same_row, 32 * m, [[-1, P]]))
            ones_where_zero(same_row, 32 * (NJ - 1), [[-1, P]]).then_inc(const_ready, 1)

            pool.wait_ge(ssm_pool, 1)
            power_of(gam, ssm[:, 12:13], half).then_inc(gam_ready, 1)

            with pool.Fori(1, G) as g:
                pool.wait_ge(var_ready, g + 1)
                power_of(rstd, veps, power).then_inc(rstd_ready, 1)

            def load_o(g):
                nc.gpsimd.tensor_copy(o_st, o_all[:, g, :]).then_inc(ost_ready, 1)

            def residual(g, xd=xd):
                pool.wait_ge(var_ready, G + g + 1)
                power_of(rstd, veps, power).then_inc(rstd_ready, 1)
                if xd is not xd_last:
                    pool.wait_ge(c_read, 2 * g + 1)
                pool.wait_ge(x1n_ready, g + 1)
                nc.gpsimd.tensor_tensor(xd, x1n, dskip, ALU.mult).then_inc(xd_half, 1)
                pool.wait_ge(xd_half, g + 1)
                nc.gpsimd.tensor_tensor(xd, xd, x1, ALU.add).then_inc(xd_ready, 1)

            pool.wait_ge(dskip_loaded, 16)
            pool.wait_ge(o_evac, 2)
            load_o(0)
            pool.wait_ge(b_full, NB1 + 1)
            load_o(1)
            residual(0)
            with pool.Fori(1, G - 1) as g:
                pool.wait_ge(b_full, NB1 + 2 * g)
                pool.wait_ge(o_evac, 2 * G)
                load_o(g + 1)
                residual(g)
            residual(G - 1, xd_last)

            pool.wait_ge(zv_ready, 1)
            power_of(zscale, vz, powers8).then_inc(zr_ready, 1)
            pool.wait_ge(var_ready, 2 * G + 1)
            power_of(rstd, veps, power).then_inc(rstd_ready, 1)
            pool.wait_ge(var_ready, 2 * G + 2)
            power_of(rstd, veps, power).then_inc(rstd_ready, 1)
            pool.wait_ge(c_full, 2 * G)
            then(nc.gpsimd.memset(spread, 0.0))
            for j in range(NJ):
                then(ones_where_zero(spread.rearrange("p g (q s) -> p g q s", q=BT), -32 * j,
                                     [[-BT, G], [-1, BT], [0, SQ]]))
            with pool.Fori(0, STEPS) as step:
                pool.wait_ge(var_ready, step + (2 * G + 3))
                power_of(rstd, veps, power).then_inc(rstd_ready, 1)
            pool.wait_ge(gate_stored, 16 * (G + 1))
            nc.gpsimd.memset(bcast, 0.0).then_inc(bzero, 1)

            def skipped(t):
                pool.wait_ge(tz_ready, t + 1)
                nc.gpsimd.tensor_tensor(x_back[:, t, :], x_back[:, t, :], t_beta, ALU.add).then_inc(skip_ready, 1)

            pool.wait_ge(tail_in, 32)
            for t in range(G):
                if t + 1 < G:
                    pool.wait_ge(bb_read, 2 * t + 4)
                    pool.wait_ge(tz_ready, t + 2)
                    nc.gpsimd.tensor_tensor(gate_back[:, t + 1, :], gate_back[:, t + 1, :], t_z[t + 1], ALU.add)\
                        .then_inc(z_added, 1)
                skipped(t)
                pool.wait_ge(var_ready, t + (2 * G + STEPS + 3))
                power_of(t_rstd[t % 2], t_rstd[t % 2], power).then_inc(rstd_ready, 1)

        @block.scalar
        def _(act):
            A = Count(a_free)
            qk, vv = Count(qk_evac), Count(v_evac)

            def copy(dst, src):
                return nc.scalar.activation(dst, src, ACT.Copy)

            def bank_a(dst, src=None):
                act.wait_ge(a_full, A.term + A.n + 1)
                A.one(copy(dst, shaped(TA, k=4, n=P) if src is None else src))

            act.dma_start(ssm[:, 0:1], nu_log[:, None]).then_inc(ssm_in, 16)
            act.dma_start(ssm[:, 1:2], theta_log[:, None]).then_inc(ssm_in, 16)
            act.wait_ge(ssm_in, 32)
            nc.scalar.activation(ssm[:, 2:4], ssm[:, 0:2], ACT.Exp).then_inc(ssm_act, 1)

            for m in range(4):
                for r in range(2):
                    n = 4 * m + r
                    if r == 0:
                        act.wait_ge(a_full, A.n + 1)
                        copy(wkvT[:, :, n * P:(n + 1) * P], shaped(TA[:, 0:2 * P], k=KL, n=P))
                    else:
                        A.one(copy(wkvT[:, :, n * P:(n + 1) * P], shaped(TA[:, 2 * P:4 * P], k=KL, n=P)))
            with act.Fori(0, KD // 4) as i:
                A.enter(i, 4)
                for s in range(4):
                    bank_a(wqT[:, 0:4, bass.ds(i * 4 * P + s * P, P)])
                A.leave(KD // 4)

            def transposed(g):
                bank_a(xnT[:, 0:4, :])
                bank_a(ctxT, shaped(TA[:, 0:L], k=KL, n=P))

            def projected(g):
                for dst in (qT, kT):
                    for f in range(2):
                        act.wait_ge(qk_full, qk.term + qk.n + 1)
                        qk.one(copy(dst[:, 4 * f:4 * f + 4, :], shaped(bank(2 + f), c=4, t=P)))
                    if dst is qT:
                        bank_a(woT[:, 4:8, bass.ts(g, P)])
                for n in range(2):
                    act.wait_ge(v_full, vv.term + vv.n + 1)
                    vv.one(copy(v[:, n * BANK:(n + 1) * BANK], bank(4 + n)))

            def exponentials(g):
                act.wait_ge(shifted_ready, g + 1)
                nc.scalar.activation(probs, scores.rearrange("p h k -> p (h k)"), ACT.Exp,
                                     scale=float(HD) ** -0.5).then_inc(exp_ready, 1)

            transposed(0)
            act.wait_ge(ssm_arg, 1)
            nc.scalar.activation(ssm[:, 7:8], ssm[:, 4:5], ACT.Exp)
            nc.scalar.activation(ssm[:, 8:9], ssm[:, 5:6], ACT.Sin)
            nc.scalar.activation(ssm[:, 9:10], ssm[:, 5:6], ACT.Sin, scale=0.5).then_inc(ssm_act, 1)
            projected(0)
            transposed(1)
            with act.Fori(0, G - 2) as it:
                A.enter(it, PER_TILE), qk.enter(it, 4), vv.enter(it, 2)
                exponentials(it)
                projected(it + 1)
                transposed(it + 2)
                A.leave(G - 2), qk.leave(G - 2), vv.leave(G - 2)
            exponentials(G - 2)
            projected(G - 1)

            for r in range(EARLY):
                act.dma_start(as_piece(resident[r], RESIDENT_Q[r]), piece_source(RESIDENT_Q[r])).then_inc(res_in, 16)
            agg_v = agg_w.rearrange("(n j p) d -> n p j d", j=2, p=P)
            for m in (3, 0):
                act.dma_start(shaped(ring[m], j=2, n=D), agg_v[m, :, :, :]).then_inc(slot_in[m], 16)
            bank_a(oT[:, 0:4, :])
            exponentials(G - 1)
            act.wait_ge(o_full, 2 * G)
            for m in (1, 2):
                act.dma_start(shaped(ring[m], j=2, n=D), agg_v[m, :, :, :]).then_inc(slot_in[m], 16)

            def bu(g):
                act.wait_ge(bu_full, g + 1)
                for c in range(2):
                    last = nc.scalar.activation(state[0][:, c, :, 16:16 + SQ],
                                                shaped(bank(6)[:, c * P:(c + 1) * P], b=BT, t=SQ),
                                                ACT.Copy, scale=gam)
                last.then_inc(bu_evac, 1)

            act.wait_ge(gam_ready, 1)
            act.sem_inc(bu_evac, 1)
            bank_a(oT[:, 0:4, :])
            with act.Fori(1, G - 1) as g:
                A.enter(g - 1, 2)
                bank_a(x1nT[:, 0:4, :])
                bu(g - 1)
                bank_a(oT[:, 0:4, :])
                A.leave(G - 2)
            bank_a(x1nT[:, 0:4, :])
            bu(G - 2)
            bank_a(x1nT[:, 0:4, :])
            act.wait_ge(h_ready, G - 1)
            bu(G - 1)

            def z_tile(dst, src, t):
                at = slice(t, t + 1) if isinstance(t, int) else bass.ds(t, 1)
                return nc.scalar.activation(dst, src, ACT.Identity, scale=zscale[:, at], bias=zshift[:, at])

            def z_load(t, transposed_before):
                act.wait_ge(b_full, transposed_before)
                act.dma_start(zst, x2_d[t, :, :]).then_inc(zx_loaded, 16)

            def z_norm(t):
                act.wait_ge(zx_loaded, 16 * t + 16)
                z_tile(zst, zst, t).then_inc(z_ready, 1)

            def gate_store(t):
                act.wait_ge(g_read, 2 * t + 4)
                act.dma_start(gate_d[t, :, :], gate_out).then_inc(gate_stored, 16)

            def before_hidden(step):
                bank_a(zT[:, 0:4, :])
                z_load(2 * step + 1, NB2 + 3 * step + 1)
                bank_a(tT, shaped(TA[:, 0:2 * P], c=2, m=P))
                z_norm(2 * step + 1)
                bank_a(zT[:, 0:4, :])
                gate_store(2 * step)

            def hidden(step, more):
                if more:
                    z_load(2 * step + 2, NB2 + 3 * step + 2)
                for i in range(2):
                    act.wait_ge(hsum_ready, 2 * step + i + 1)
                    part = hid[:, i * BANK:(i + 1) * BANK]
                    nc.scalar.activation(part, part, ACT.Gelu).then_inc(hid_ready, 1)
                bank_a(hidT[:, 0:4, :])
                if more:
                    z_norm(2 * step + 2)
                gate_store(2 * step + 1)

            act.wait_ge(x2_stored, 16 * (G - 2))
            act.wait_ge(y_read, 2 * G)
            z_load(0, NB2)
            act.wait_ge(zshift_ready, 1)
            z_norm(0)
            bank_a(tT, shaped(TA[:, 0:2 * P], c=2, m=P))
            act.wait_ge(x2_stored, 16 * G)
            before_hidden(0)
            with act.Fori(0, STEPS - 1) as step:
                A.enter(step, 4)
                hidden(step, True)
                before_hidden(step + 1)
                A.leave(STEPS - 1)
            hidden(STEPS - 1, False)
            bank_a(tT, shaped(TA[:, 0:2 * P], c=2, m=P))

            def sigmoid_and_z(t):
                act.wait_ge(back_in[t % 2], 32 * (t // 2 + 1))
                nc.scalar.activation(gate_back[:, t, :], gate_back[:, t, :], ACT.Sigmoid).then_inc(sig_ready, 1)
                z_tile(t_z[t], x_back[:, t, :], t).then_inc(tz_ready, 1)

            act.wait_ge(g_read, 2 * G + 2)
            for t in range(G):
                sigmoid_and_z(t)

        @block.vector
        def _(dve):
            chain = Count(dve_chain)
            B = Count(b_free)

            def then(instruction):
                dve.wait_ge(dve_chain, chain.one(instruction))

            def bank_b(dst, src=None):
                dve.wait_ge(b_full, B.term + B.n + 1)
                B.one(nc.vector.tensor_copy(dst, shaped(TB, k=4, n=P) if src is None else src))

            def settled():
                dve.sem_inc(passed_dve, 1)

            def moments(src, eps):
                for i in range(2):
                    ins = nc.vector.bn_stats(s6[:, i, :], src[:, i * BANK:(i + 1) * BANK])
                    chain.one(ins) if i == 0 else then(ins)
                settled()
                then(nc.vector.bn_aggr(mv, s6))
                nc.vector.tensor_scalar_add(veps, mv[:, 1:2], eps).then_inc(var_ready, 1)

            def norm(dst, src, n):
                dve.wait_ge(rstd_ready, n + 1)
                return nc.vector.tensor_scalar(dst, src, mv[:, 0:1], rstd, ALU.subtract, ALU.mult)

            def layer_norm(g):
                dve.wait_ge(x_loaded, 16 * g + 16)
                moments(x_in, LN_EPS)
                norm(xn, x_in, g).then_inc(xn_ready, 1)

            layer_norm(0)

            col = [ssm[:, i:i + 1] for i in range(20)]
            ts, tt, stt = nc.vector.tensor_scalar, nc.vector.tensor_tensor, nc.vector.scalar_tensor_tensor

            def angles():
                dve.wait_ge(ssm_act, 1)
                then(ts(col[4], col[2], 1.0, -1.0, ALU.add, ALU.mult))
                then(ts(col[10], col[3], 1.0 / TWO_PI, None, ALU.mult))
                turns = ssmk[:, 0:1].bitcast(I32)
                then(nc.vector.tensor_copy(turns, col[10]))
                then(nc.vector.tensor_copy(col[10], turns))
                then(stt(col[5], col[10], -6.28125, col[3], ALU.mult, ALU.add))
                then(stt(col[5], col[10], -(TWO_PI - 6.28125), col[5], ALU.mult, ALU.add))
                then(ts(col[11], col[5], TWO_PI / 2, -TWO_PI, ALU.is_gt, ALU.mult))
                then(tt(col[5], col[5], col[11], ALU.add))
                then(ts(col[11], col[5], -TWO_PI / 2, TWO_PI, ALU.is_lt, ALU.mult))
                then(tt(col[5], col[5], col[11], ALU.add))
                ts(col[5], col[5], 3.1415925, -3.1415925, ALU.min, ALU.max).then_inc(ssm_arg, 1)

            def powers():
                dve.wait_ge(ssm_act, 2)
                then(tt(col[11], col[9], col[9], ALU.mult))
                then(ts(col[11], col[11], -2.0, 1.0, ALU.mult, ALU.add))
                then(tt(col[12], col[7], col[7], ALU.mult))
                then(ts(col[12], col[12], -1.0, 1.0, ALU.mult, ALU.add))
                ts(col[12], col[12], 0.0, None, ALU.max).then_inc(ssm_pool, 1)
                then(tt(apow[:, 0, 0:1], col[7], col[11], ALU.mult))
                then(tt(apow[:, 0, 1:2], col[7], col[8], ALU.mult))
                then(ts(apow[:, 0, 2:3], apow[:, 0, 1:2], -1.0, None, ALU.mult))
                for l in range(1, 5):
                    re, im = apow[:, l - 1, 0:1], apow[:, l - 1, 1:2]
                    then(tt(col[13], im, im, ALU.mult))
                    then(tt(col[14], re, re, ALU.mult))
                    then(tt(apow[:, l, 0:1], col[14], col[13], ALU.subtract))
                    then(tt(col[13], re, im, ALU.mult))
                    then(ts(apow[:, l, 1:2], col[13], 2.0, None, ALU.mult))
                    then(ts(apow[:, l, 2:3], col[13], -2.0, None, ALU.mult))


            for m in range(4):
                dve.wait_ge(b_full, B.n + 1)
                for r in range(2):
                    n = 4 * m + 2 + r
                    ins = nc.vector.tensor_copy(wkvT[:, :, n * P:(n + 1) * P],
                                                shaped(TB[:, r * 2 * P:(r + 1) * 2 * P], k=KL, n=P))
                B.one(ins)
            with dve.Fori(0, KD // 4) as i:
                B.enter(i, 4)
                for s in range(4):
                    bank_b(wqT[:, 4:8, bass.ds(i * 4 * P + s * P, P)])
                B.leave(KD // 4)

            def prepared_o(g):
                bank_b(woT[:, 0:4, bass.ts(g, P)])

            def prepared_bc(g):
                dve.wait_ge(b_full, B.term + B.n + 1)
                nc.vector.tensor_copy(cT[:, 0, bass.ts(g, P)], TB[:, 0:P])
                nc.vector.tensor_scalar_mul(cT[:, 1, bass.ts(g, P)], TB[:, P:2 * P], -1.0)
                B.one(nc.vector.tensor_copy(bT[:, :, g, :], shaped(TB[:, 2 * P:4 * P], c=2, n=P)))

            def softmax(g):
                dve.wait_ge(s_full, g + 1)
                mask = causal[:, None, :].broadcast_to([P, HEADS // 2, SQ])
                for e in range(2):
                    ins = tt(scores[:, e::2, :], shaped(bank(6 + e)[:, 0:BANK // 2], h=HEADS // 2, k=SQ), mask, ALU.add)
                    chain.one(ins) if e == 0 else ins.then_inc(s_read, 1)
                dve.wait_ge(s_read, g + 2)
                then(nc.vector.reduce_max(mx, scores, axis=AX.X))
                tt(scores, scores, mx[:, :, None].broadcast_to([P, HEADS, SQ]), ALU.subtract)\
                    .then_inc(shifted_ready, 1)
                dve.wait_ge(exp_ready, g + 1)
                then(nc.vector.reduce_sum(rs, shaped(probs, h=HEADS, k=SQ), axis=AX.X))
                then(nc.vector.reciprocal(ri, rs))
                for j in range(BT):
                    r = slice(32 * j, 32 * j + 32)
                    last = nc.vector.transpose(probsT[r, :, 32 * j:32 * j + SQ], probs[r, :])
                last.then_inc(pT_ready, 1)

            def attention_out(g):
                for n in range(2):
                    dve.wait_ge(o_full, 2 * g + n + 1)
                    tt(o_all[:, g, n * BANK:(n + 1) * BANK], bank(4 + n), ri[:, 8 * n:8 * n + 8, None].broadcast_to([P, 8, HD]), ALU.mult)\
                        .then_inc(o_evac, 1)

            bank_b(xnT[:, 4:8, :])
            angles()
            prepared_o(0)
            powers()
            prepared_bc(0)
            layer_norm(1)
            dve.wait_ge(const_ready, 1)
            dve.sem_inc(s_read, 1)

            def attend(it, more):
                bank_b(xnT[:, 4:8, :])
                softmax(it)
                prepared_o(it + 1)
                if more:
                    layer_norm(it + 2)
                attention_out(it)
                prepared_bc(it + 1)

            with dve.Fori(0, G - 2) as it:
                B.enter(it, PER_TILE), chain.enter(it, 7)
                attend(it, True)
                B.leave(G - 2), chain.leave(G - 2)
            attend(G - 2, False)
            bank_b(oT[:, 4:8, :])
            softmax(G - 1)

            def residual(g, n, meanwhile=None):
                h = slice(n * BANK, (n + 1) * BANK)
                if n == 0:
                    dve.wait_ge(x_loaded, 16 * g + 16 * (G + 1))
                dve.wait_ge(y_full, 2 * g + n + 1)
                tt(x1[:, h], x_in[:, h], bank(2 + n), ALU.add).then_inc(y_read, 1)
                dve.wait_ge(y_read, 2 * g + n + 1)
                settled()
                ins = nc.vector.bn_stats(s6[:, n, :], x1[:, h])
                if n == 0:
                    chain.one(ins)
                    return
                then(ins)
                settled()
                then(nc.vector.bn_aggr(mv, s6))
                nc.vector.tensor_scalar_add(veps, mv[:, 1:2], LN_EPS).then_inc(var_ready, 1)
                if meanwhile:
                    meanwhile()
                norm(x1n, x1, G + g).then_inc(x1n_ready, 1)

            def recurrence(g, before=()):
                dve.wait_ge(bu_evac, g + 2)
                for l in range(5):
                    if l in before:
                        before[l]()
                    s, src, dst = 2 ** l, state[l % 2], state[(l + 1) % 2]
                    a, b, nb = (apow[:, l, i:i + 1] for i in range(3))
                    now, old = slice(16, 16 + SQ), slice(16 - s, 16 - s + SQ)
                    to = dst[:, :, :, now] if l < 4 else hT
                    then(stt(stmp.rearrange("p c b t -> p (c b) t"),
                             src.rearrange("p c b t -> p (c b) t")[:, :, old], a,
                             src.rearrange("p c b t -> p (c b) t")[:, :, now], ALU.mult, ALU.add))
                    chain.one(stt(to[:, 0], src[:, 1, :, old], nb, stmp[:, 0], ALU.mult, ALU.add))
                    ins = stt(to[:, 1], src[:, 0, :, old], b, stmp[:, 1], ALU.mult, ALU.add)
                    then(ins) if l < 4 else ins.then_inc(h_ready, 1)

            def add_states(g, first, more, xd=xd, at=4, x2=x2):
                dve.wait_ge(xd_ready, g + 1)
                if not first and x2 is not x2_last:
                    dve.wait_ge(x2_stored, 16 * g)
                for n in range(2):
                    h = slice(n * BANK, (n + 1) * BANK)
                    dve.wait_ge(c_full, 2 * g + n + 1)
                    tt(x2[:, h], xd[:, h], bank(at + n), ALU.add).then_inc(c_read, 1)
                if more:
                    bank_b(oT[:, 4:8, :])
                dve.wait_ge(c_read, 2 * g + 3)
                settled()
                for i in range(2):
                    ins = nc.vector.bn_stats(s6x[:, i, :], x2[:, i * BANK:(i + 1) * BANK])
                    chain.one(ins) if i == 0 else then(ins)
                settled()
                then(nc.vector.bn_aggr(mvx, s6x))
                chain.one(nc.vector.tensor_copy(mvz[:, g, :], mvx))

            dve.sem_inc(c_read, 1)
            residual(0, 0)
            attention_out(G - 1)
            residual(0, 1, lambda: bank_b(oT[:, 4:8, :]))

            def turn(g, first, more):
                bank_b(x1nT[:, 4:8, :])
                dve.wait_ge(xd_ready, g)
                residual(g, 0)
                recurrence(g - 1)
                residual(g, 1)
                add_states(g - 1, first, more)

            turn(1, True, True)
            with dve.Fori(2, G - 1) as g:
                B.enter(g - 2, 2), chain.enter(g - 2, 21)
                turn(g, False, True)
                B.leave(G - 3), chain.leave(G - 3)
            bank_b(x1nT[:, 4:8, :])
            dve.wait_ge(xd_ready, G - 1)
            residual(G - 1, 0)
            residual(G - 1, 1)
            recurrence(G - 2, {1: lambda: bank_b(x1nT[:, 4:8, :])})
            recurrence(G - 1, {4: lambda: dve.wait_ge(c_full, 2 * G - 2)})
            add_states(G - 2, False, False)
            add_states(G - 1, False, False, xd_last, 2, x2_last)

            dve.wait_ge(dve_chain, chain.n)
            ts(vz, mvz[:, :, 1], LN_EPS, None, ALU.add).then_inc(zv_ready, 1)
            dve.wait_ge(zr_ready, 1)
            then(tt(zshift, mvz[:, :, 0], zscale, ALU.mult))
            ts(zshift, zshift, -1.0, None, ALU.mult).then_inc(zshift_ready, 1)

            st_n, p_n = Count(st_in), Count(p_read)

            def packed_norm(dst, src, eps, n, meanwhile=None):
                then(nc.vector.bn_stats(s6f, src))
                st_n.one(tt(s24, s6f[:, None, :].broadcast_to([P, NJ, 6]),
                            group_mask[:, :, None].broadcast_to([P, NJ, 6]), ALU.mult))
                if meanwhile:
                    meanwhile()
                dve.wait_ge(st_full, st_n.term + st_n.n)
                settled()
                then(nc.vector.bn_aggr(mv, bank(7)[:, 0:24]))
                nc.vector.tensor_scalar_add(veps, mv[:, 1:2], eps).then_inc(var_ready, 1)
                then(norm(dst, src, n))

            dve.wait_ge(par_loaded, 16 * 7 * NJ)
            dve.wait_ge(th_loaded, 48 * NJ)
            dve.wait_ge(const_ready, 2)
            packed_norm(tn, th, LN_EPS, 2 * G)
            packed_norm(thb, tn, FFN_EPS, 2 * G + 1)
            then(tt(thb, thb, packed["in_g"], ALU.mult))
            tt(tn, thb, packed["in_b"], ALU.add).then_inc(tn_ready, 1)
            dve.wait_ge(slot_used, AGG)
            then(tt(th, bank(6)[:, 0:W4], packed["agg_b"], ALU.add))

            dve.wait_ge(gbias_loaded, 16 * (1 + NJ))
            dve.wait_ge(x2_stored, 16 * G)
            dve.sem_inc(g_read, 2)
            dve.sem_inc(gate_stored, 16)

            def gate_sum(t, n):
                h = slice(n * BANK, (n + 1) * BANK)
                dve.wait_ge(g_full, 2 * t + n + 1)
                if n == 0:
                    dve.wait_ge(gate_stored, 16 * t + 16)
                tt(gate_out[:, h], bank(4 + n), gate_bias[:, h], ALU.add).then_inc(g_read, 1)

            def hidden_sum(step, i):
                h = slice(i * BANK, (i + 1) * BANK)
                dve.wait_ge(hp_full, 2 * step + i + 1)
                tt(hid[:, h], bank(2 + i), d1_bias[:, h], ALU.add).then_inc(hsum_ready, 1)

            with dve.Fori(0, STEPS) as step:
                B.enter(step, 3), chain.enter(step, 6), st_n.enter(step, 1)
                packed_norm(tn, th, FFN_EPS, step + 2 * G + 2, lambda: bank_b(zT[:, 4:8, :]))
                then(tt(tn, tn, packed["pn_g"], ALU.mult))
                tt(tn, tn, packed["pn_b"], ALU.add).then_inc(tn_ready, 1)
                then(tt(thb, th, packed["d2_b"], ALU.add))
                gate_sum(2 * step, 0)
                hidden_sum(step, 0)
                gate_sum(2 * step, 1)
                bank_b(zT[:, 4:8, :])
                hidden_sum(step, 1)
                bank_b(hidT[:, 4:8, :])
                for i in range(2):
                    gate_sum(2 * step + 1, i)
                dve.wait_ge(p_full, step + 1)
                then(tt(th, bank(6)[:, 0:W4], thb, ALU.add))
                B.leave(STEPS), chain.leave(STEPS), st_n.leave(STEPS)
            nc.vector.tensor_copy(tn, th).then_inc(tn_ready, 1)

            dve.wait_ge(slot_used, BC_DONE)
            dve.wait_ge(bzero, 1)
            for j in range(NJ):
                r = slice(32 * j, 32 * j + 32)
                last = tt(bcast[r, j, :], bank(6)[r, 0:W4], packed["bc_b"][r, :], ALU.add)
            last.then_inc(bc_ready, 1)

            def gated(t):
                dve.wait_ge(sig_ready, t + 1)
                for n in range(2):
                    h = slice(n * BANK, (n + 1) * BANK)
                    dve.wait_ge(bb_full, 2 * t + n + 1)
                    tt(gate_back[:, t, h], bank(2 + 2 * (t % 2) + n), gate_back[:, t, h], ALU.mult).then_inc(bb_read, 1)

            def finish(t):
                dve.wait_ge(rstd_ready, t + (2 * G + STEPS + 3))
                dve.wait_ge(skip_ready, t + 1)
                dve.wait_ge(centred, t + 1)
                stt(x_back[:, t, :], gate_back[:, t, :], t_rstd[t % 2], x_back[:, t, :], ALU.mult, ALU.add)\
                    .then_inc(fin_ready, 1)

            dve.wait_ge(tail_in, 32)
            gated(0)
            for t in range(G):
                e, total = t % 2, gate_back[:, t, :]
                if t == 0:
                    dve.wait_ge(tz_ready, 1)
                    dve.wait_ge(bb_read, 2)
                    chain.one(tt(total, total, t_z[t], ALU.add))
                if t + 1 < G:
                    gated(t + 1)
                if t == 0:
                    dve.wait_ge(dve_chain, chain.n)
                else:
                    dve.wait_ge(z_added, t)
                for i in range(2):
                    ins = nc.vector.bn_stats(s6[:, i, :], total[:, i * BANK:(i + 1) * BANK])
                    chain.one(ins) if i == 0 else then(ins)
                then(nc.vector.bn_aggr(t_mv[e], s6))
                if t >= 2:
                    dve.wait_ge(fin_ready, t - 1)
                nc.vector.tensor_scalar_add(t_rstd[e], t_mv[e][:, 1:2], FFN_EPS).then_inc(var_ready, 1)
                stt(total, total, t_mv[e][:, 0:1], t_gamma, ALU.subtract, ALU.mult).then_inc(centred, 1)
                if t >= 1:
                    finish(t - 1)
            finish(G - 1)

        @block.tensor
        def _(pe):
            A, B = Count(a_full), Count(b_full)

            def four(fulls, free, dst, blocks):
                if not (isinstance(fulls.term, int) and fulls.term + fulls.n == 0):
                    pe.wait_ge(free, fulls.term + fulls.n)
                for i, b in enumerate(blocks):
                    last = nc.tensor.transpose(dst[:, i * P:(i + 1) * P], b, ident)
                fulls.one(last)

            def bank_a(*blocks):
                four(A, a_free, TA, blocks)

            def bank_b(*blocks):
                four(B, b_free, TB, blocks)

            def cols(ap, *ks):
                return [ap[:, k * P:(k + 1) * P] for k in ks]

            def product(dst, lhsTs, rhss):
                for k, (l, r) in enumerate(zip(lhsTs, rhss)):
                    last = nc.tensor.matmul(dst, l, r, start=(k == 0), stop=(k == len(lhsTs) - 1))
                return last

            pe.wait_ge(const_ready, 1)
            for s in range(4):
                pe.wait_ge(raw_in[s], 16)
                bank_a(*cols(raw[s], 0, 1, 2, 3))
                bank_b(*cols(raw[s], 4, 5, 6, 7))
            with pe.Fori(0, KD // 4) as i:
                A.enter(i, 4), B.enter(i, 4)
                for s in range(4):
                    pe.wait_ge(raw_in[s], 16 * i + 32)
                    bank_a(*cols(raw[s], 0, 1, 2, 3))
                    bank_b(*cols(raw[s], 4, 5, 6, 7))
                A.leave(KD // 4), B.leave(KD // 4)

            def transposes(g):
                pe.wait_ge(xn_ready, g + 1)
                bank_a(*cols(xn, 0, 1, 2, 3))
                bank_b(*cols(xn, 4, 5, 6, 7))
                pe.wait_ge(ctx_loaded, 16 * BT * g + 16 * BT)
                bank_a(*cols(ctx_in, 0, 1))

            def prepare_bc(g):
                pe.wait_ge(bc_loaded, 64 * g + 64)
                bank_b(*cols(raw_bc, 0, 1, 2, 3))

            def heads_product(f, w, acts, ks):
                for c in range(4 * f, 4 * f + 4):
                    last = product(bank(2 + f)[:, (c % 4) * P:(c % 4 + 1) * P],
                                   [w[:, k, c * P:(c + 1) * P] for k in range(ks)],
                                   [acts[:, k, :] for k in range(ks)])
                last.then_inc(qk_full, 1)

            def queries(g, first):
                pe.wait_ge(a_free, A.term + A.n)
                pe.wait_ge(b_free, B.term + B.n)
                for f in range(2):
                    if not first:
                        pe.wait_ge(qk_evac, 4 * g - 1 + f)
                    heads_product(f, wqT, xnT, KD)
                    if f == 0:
                        pe.wait_ge(wo_loaded, 16 * g + 16)
                        bank_b(*cols(raw_wo, 0, 1, 2, 3))
                bank_a(*cols(raw_wo, 4, 5, 6, 7))

            def keys(g):
                for f in range(2):
                    pe.wait_ge(qk_evac, 4 * g + f + 1)
                    heads_product(f, wkvT, ctxT, KL)

            def values(g, first):
                for n in range(2):
                    if not first:
                        pe.wait_ge(o_evac, 2 * g - 1 + n)
                    product(bank(4 + n), [ctxT[:, k, :] for k in range(KL)],
                            [wkvT[:, k, D + n * BANK:D + (n + 1) * BANK] for k in range(KL)]).then_inc(v_full, 1)

            def score(g):
                pe.wait_ge(qk_evac, 4 * g + 4)
                pe.wait_ge(s_read, g + 1)
                pe.sem_inc(passed_pe, 1)
                for c in range(KD):
                    for e in range(2):
                        for j in range(BT):
                            r, t = slice(64 * e, 64 * e + HD), slice(32 * j, 32 * j + SQ)
                            last = nc.tensor.matmul(bank(6 + e)[t, c * SQ:(c + 1) * SQ], qT[r, c, t], kT[r, c, t],
                                                    start=True, stop=True)
                last.then_inc(s_full, 1)

            def weighted(g):
                pe.wait_ge(pT_ready, g + 1)
                pe.wait_ge(v_evac, 2 * g + 2)
                for n in range(2):
                    for h in range(8 * n, 8 * n + 8):
                        last = nc.tensor.matmul(bank(4 + n)[:, (h % 8) * HD:(h % 8 + 1) * HD], probsT[:, h, :],
                                                v[:, h * HD:(h + 1) * HD], start=True, stop=True)
                    last.then_inc(o_full, 1)

            transposes(0)
            queries(0, True)
            prepare_bc(0)
            keys(0)
            values(0, True)
            with pe.Fori(0, G - 1) as it:
                A.enter(it, PER_TILE), B.enter(it, PER_TILE)
                transposes(it + 1)
                score(it)
                queries(it + 1, False)
                weighted(it)
                prepare_bc(it + 1)
                keys(it + 1)
                values(it + 1, False)
                A.leave(G - 1), B.leave(G - 1)

            def load_o(g):
                pe.wait_ge(ost_ready, g + 1)
                bank_a(*cols(o_st, 0, 1, 2, 3))
                bank_b(*cols(o_st, 4, 5, 6, 7))

            def project(g, n, first=False):
                if not first:
                    pe.wait_ge(y_read, 2 * g - 1 + n)
                product(bank(2 + n), [oT[:, k, :] for k in range(KD)],
                        [woT[:, k, n * BANK:(n + 1) * BANK] for k in range(KD)]).then_inc(y_full, 1)

            def transpose_x1n(g):
                pe.wait_ge(x1n_ready, g + 1)
                bank_a(*cols(x1n, 0, 1, 2, 3))
                bank_b(*cols(x1n, 4, 5, 6, 7))

            def inputs(g):
                pe.wait_ge(bu_evac, g + 1)
                pe.wait_ge(a_free, A.term + A.n)
                pe.wait_ge(b_free, B.term + B.n)
                for c in range(2):
                    last = product(bank(6)[:, c * P:(c + 1) * P], [bT[:, c, k, :] for k in range(KD)],
                                   [x1nT[:, k, :] for k in range(KD)])
                last.then_inc(bu_full, 1)

            def outputs(g, first, at=4):
                pe.wait_ge(h_ready, g + 1)
                for n in range(2):
                    if not first:
                        pe.wait_ge(c_read, 2 * g + n)
                    product(bank(at + n), [hT[:, c].rearrange("p b t -> p (b t)") for c in range(2)],
                            [cT[:, c, n * BANK:(n + 1) * BANK] for c in range(2)]).then_inc(c_full, 1)

            score(G - 1)
            load_o(0)
            pe.wait_ge(a_free, A.n)
            pe.wait_ge(b_free, B.n)
            project(0, 0, True)
            weighted(G - 1)
            project(0, 1, True)
            load_o(1)
            pe.wait_ge(a_free, A.n)
            pe.wait_ge(b_free, B.n)
            project(1, 0)
            transpose_x1n(0)
            inputs(0)
            project(1, 1)
            outputs(0, True)
            load_o(2)

            def turn(g):
                transpose_x1n(g - 1)
                project(g, 0)
                inputs(g - 1)
                project(g, 1)
                outputs(g - 1, False)
                load_o(g + 1)

            with pe.Fori(2, G - 1) as g:
                A.enter(g - 2, 2), B.enter(g - 2, 2)
                turn(g)
                A.leave(G - 3), B.leave(G - 3)
            transpose_x1n(G - 2)
            project(G - 1, 0)
            project(G - 1, 1)
            inputs(G - 2)
            transpose_x1n(G - 1)
            inputs(G - 1)
            outputs(G - 2, False)
            pe.wait_ge(y_read, 2 * G)
            outputs(G - 1, True, 2)

            pe.wait_ge(const_ready, 2)
            fills = [Count(s) for s in slot_in]
            used = Count(slot_used)

            def stats(n):
                pe.wait_ge(st_in, n)
                nc.tensor.matmul(bank(7)[:, 0:24], same_row, small[:, 107:131], start=True, stop=True)\
                    .then_inc(st_full, 1)

            def transposed_thought(n):
                pe.wait_ge(tn_ready, n)
                bank_a(*cols(tn, 0, 1))

            def streamed(s):
                fills[s].n += 16
                pe.wait_ge(slot_in[s], fills[s].term + fills[s].n)

            def rows_product(n0):
                for n in range(AGG):
                    s = (n0 + n) % RING
                    streamed(s)
                    piece = shaped(ring[s], j=2, n=D)
                    for c in range(2):
                        k = 2 * n + c
                        for j in range(NJ):
                            last = nc.tensor.matmul(bank(6)[32 * j:32 * j + 32, 0:W4],
                                                    tT[:, k % 2, 32 * (k // 2):32 * (k // 2) + 32],
                                                    piece[:, c, j * W4:(j + 1) * W4],
                                                    start=(k == 0), stop=(k == KD - 1))
                    used.one(last)

            stats(1)
            stats(2)
            transposed_thought(1)
            pe.wait_ge(a_free, A.n)
            rows_product(0)
            pe.wait_ge(res_in, 16 * EARLY)
            pe.wait_ge(gw_loaded, 16)

            def z_transposes(t):
                pe.wait_ge(z_ready, t + 1)
                bank_a(*cols(zst, 0, 1, 2, 3))
                bank_b(*cols(zst, 4, 5, 6, 7))

            def gate_product(t, u):
                n, k = divmod(u, KD)
                if k == 0:
                    pe.wait_ge(g_read, 2 * t + n + 1)
                last = nc.tensor.matmul(bank(4 + n), zT[:, k, :], gw[:, k, n * BANK:(n + 1) * BANK],
                                        start=(k == 0), stop=(k == KD - 1))
                if k == KD - 1:
                    last.then_inc(g_full, 1)

            def gates(t, lo, hi):
                for u in range(lo, hi):
                    gate_product(t, u)

            def next_piece(q, m):
                if q in RESIDENT_Q:
                    return as_piece(resident[RESIDENT_Q.index(q)], q), m
                streamed((AGG + m) % RING)
                return as_piece(ring[(AGG + m) % RING], q), m + 1

            with pe.Fori(0, STEPS) as step:
                A.enter(step, 4), B.enter(step, 3), used.enter(step, N_RING)
                for f in fills:
                    f.enter(step, 16 * N_RING // RING)
                m = 0
                z_transposes(2 * step)
                stats(step + 3)
                pe.wait_ge(a_free, A.term + A.n)
                pe.wait_ge(b_free, B.term + B.n)
                gates(2 * step, 0, 4)
                transposed_thought(step + 2)
                gates(2 * step, 4, 5)
                pe.wait_ge(a_free, A.term + A.n)
                for q in range(D1P):
                    i, k = divmod(q, KD)
                    if q == RESIDENT_Q[EARLY]:
                        pe.wait_ge(res_late, 16 * (RES - EARLY))
                    piece, m = next_piece(q, m)
                    for j in range(NJ):
                        last = nc.tensor.matmul(bank(2 + i)[32 * j:32 * j + 32, :],
                                                tT[:, k % 2, 32 * (k // 2):32 * (k // 2) + 32],
                                                piece[:, j, :], start=(k == 0), stop=(k == KD - 1))
                    if k == KD - 1:
                        last.then_inc(hp_full, 1)
                    else:
                        used.one(last) if q not in RESIDENT_Q else None
                    if q < 11:
                        gate_product(2 * step, 5 + q)
                    if q == 10:
                        z_transposes(2 * step + 1)
                    if q >= 14:
                        if q == 14:
                            pe.wait_ge(a_free, A.term + A.n)
                            pe.wait_ge(b_free, B.term + B.n)
                        gate_product(2 * step + 1, q - 14)
                gates(2 * step + 1, 2, 4)
                pe.wait_ge(hid_ready, 2 * step + 1)
                bank_a(*cols(hid, 0, 1, 2, 3))
                gates(2 * step + 1, 4, 5)
                pe.wait_ge(hid_ready, 2 * step + 2)
                bank_b(*cols(hid, 4, 5, 6, 7))
                gates(2 * step + 1, 5, 8)
                pe.wait_ge(a_free, A.term + A.n)
                for q in range(D1P, PIECES):
                    c, jp = divmod(q - D1P, 2)
                    if c == H4 // P // 2 and jp == 0:
                        pe.wait_ge(b_free, B.term + B.n)
                    piece, m = next_piece(q, m)
                    for jj in range(2):
                        j = 2 * jp + jj
                        for n in range(NJ):
                            last = nc.tensor.matmul(bank(6)[32 * n:32 * n + 32, 0:W4],
                                                    hidT[:, c, 32 * j:32 * j + 32],
                                                    piece[:, jj, n * W4:(n + 1) * W4],
                                                    start=(c == 0 and j == 0), stop=(q == PIECES - 1 and jj == 1))
                    if q == PIECES - 1:
                        last.then_inc(p_full, 1)
                    elif q not in RESIDENT_Q:
                        used.one(last)
                    if q % 2:
                        gate_product(2 * step + 1, 8 + (q - D1P) // 2)
                A.leave(STEPS), B.leave(STEPS), used.leave(STEPS)
                for f in fills:
                    f.leave(STEPS)
            transposed_thought(STEPS + 2)
            pe.wait_ge(a_free, A.n)
            rows_product(AGG + STEPS * N_RING)

            pe.wait_ge(bc_ready, 1)
            pe.wait_ge(g_read, 2 * G + 2)
            for t in range(G):
                for n in range(2):
                    if t >= 2:
                        pe.wait_ge(bb_read, 2 * t - 3 + n)
                    nc.tensor.matmul(bank(2 + 2 * (t % 2) + n), spread[:, t, :],
                                     bcast.rearrange("p j n -> p (j n)")[:, n * BANK:(n + 1) * BANK],
                                     start=True, stop=True).then_inc(bb_full, 1)


_INS = ["x", "ctx_512", "L0_xattn_Wq", "L0_xattn_Wkv_expand", "L0_xattn_Wout", "L0_attn_nu_log",
        "L0_attn_theta_log", "L0_attn_B_re", "L0_attn_B_im", "L0_attn_C_re", "L0_attn_C_im", "L0_attn_D",
        "L0_ffn_in_gamma", "L0_ffn_in_beta", "L0_ffn_agg_w", "L0_ffn_agg_b", "L0_ffn_pn_gamma",
        "L0_ffn_pn_beta", "L0_ffn_d1_w", "L0_ffn_d1_b", "L0_ffn_d2_w", "L0_ffn_d2_b", "L0_ffn_bc_w",
        "L0_ffn_bc_b", "L0_ffn_gate_w", "L0_ffn_gate_b", "L0_ffn_out_gamma", "L0_ffn_out_beta"]


def kernel(**inputs):
    import numpy as _np
    import concourse.bacc as _bacc
    from concourse import mybir as _mybir
    from concourse.bass_utils import run_bass_kernel_spmd as _run

    nc = _bacc.Bacc("TRN2", target_bir_lowering=False, num_devices=1)
    arrays, args = {}, []
    for name in _INS:
        a = _np.ascontiguousarray(inputs[name])
        arrays[f"in_{name}_dram"] = a
        args.append(nc.dram_tensor(f"in_{name}_dram", a.shape, _mybir.dt.from_np(a.dtype), kind="ExternalInput").ap())
    shape = inputs["x"].shape
    args.append(nc.dram_tensor("out_0_dram", shape, _mybir.dt.float32, kind="ExternalOutput").ap())
    build(nc, *args)
    r = _run(nc, [arrays], core_ids=[0])
    return r.results[0]["out_0_dram"]
```

```python
from contextlib import ExitStack

import concourse.bass as bass
from concourse import mybir

F32 = mybir.dt.float32
I32 = mybir.dt.int32
ALU = mybir.AluOpType
ACT = mybir.ActivationFunctionType
AX = mybir.AxisListType

P = 128
BANK = 512
TWO_PI = 6.283185307179586
MASKED = -1.0e38
LN_EPS = 1e-5
FFN_EPS = 1e-6


class Count:

    def __init__(self, sem):
        self.sem, self.n, self.term = sem, 0, 0

    def one(self, instruction, by=1):
        instruction.then_inc(self.sem, by)
        self.n += by
        return self.term + self.n

    def enter(self, turn, per_turn):
        self.start, self.per_turn, self.term = self.n, per_turn, turn * per_turn

    def leave(self, turns):
        assert self.n - self.start == self.per_turn, (self.n - self.start, self.per_turn)
        self.n, self.term = self.start + turns * self.per_turn, 0


def build(nc, x, ctx_512, Wq, Wkv, Wout, nu_log, theta_log, B_re, B_im, C_re, C_im, Dskip,
          in_gamma, in_beta, agg_w, agg_b, pn_gamma, pn_beta, d1_w, d1_b, d2_w, d2_b,
          bc_w, bc_b, gate_w, gate_b, out_gamma, out_beta, out):
    NB, SQ, D = x.shape
    L = ctx_512.shape[2]
    HEADS = 16
    HD = D // HEADS
    KD, KL = D // P, L // P
    BT = P // SQ
    G = NB // BT
    NST = nu_log.shape[0]
    HID = d1_w.shape[1]
    NJ = 4
    W4 = D // NJ
    H4 = HID // NJ
    STEPS = 4
    assert SQ == 32 and P == NST and L == 2 * P and W4 == 256 and H4 == 2 * BANK

    x_t = x.rearrange("b s d -> (b s) d").rearrange("(g p) d -> g p d", p=P)
    out_t = out.rearrange("b s d -> (b s) d").rearrange("(g p) d -> g p d", p=P)
    wo_t = Wout.rearrange("(g p) d -> g p d", p=P)

    with ExitStack() as ctx:
        mem = ctx.enter_context(nc.sbuf_tensor("mem", [P, 53200], F32))
        ps = ctx.enter_context(nc.psum_tensor("ps", [P, 8 * BANK], F32))
        top = [0]

        def take(cols, at=None):
            lo = top[0] if at is None else at
            if at is None:
                top[0] += cols
            assert lo + cols <= 53200, lo + cols
            return mem[:, lo:lo + cols]

        def shaped(ap, **dims):
            return ap.rearrange("p (" + " ".join(dims) + ") -> p " + " ".join(dims), **dims)

        SLOT = 2 * D

        R_WQ = 0
        R_WKV = KD * D
        R_O = R_WKV + KL * 2 * D
        R_WO = R_O + G * D
        R_BC = R_WO + KD * D
        R_T = R_BC + 4 * D
        wqT = shaped(take(KD * D, R_WQ), k=KD, n=D)
        wkvT = shaped(take(KL * 2 * D, R_WKV), k=KL, n=2 * D)
        o_all = shaped(take(G * D, R_O), g=G, n=D)
        woT = shaped(take(KD * D, R_WO), k=KD, n=D)
        bT = shaped(take(2 * D, R_BC), c=2, k=KD, n=NST)
        cT = shaped(take(2 * D, R_BC + 2 * D), c=2, n=D)
        gw = shaped(take(KD * D, R_WO), k=KD, n=D)
        raw = [take(D, R_T + i * D) for i in range(4)]
        qT = shaped(take(D, R_T + 4 * D), c=KD, t=P)
        kT = shaped(take(D, R_T + 5 * D), c=KD, t=P)
        v = take(D, R_T + 6 * D)
        ctx_in = take(L, R_T + 7 * D)
        ctxT = shaped(take(L, R_T + 7 * D + L), k=KL, t=P)
        raw_bc = take(4 * P, R_T + 7 * D + 2 * L)
        top[0] = R_T + 8 * D
        R_U = top[0]
        x_in = take(D)
        xn = take(D)
        xnT = shaped(take(D), k=KD, t=P)
        raw_wo = take(D)
        scores = shaped(take(HEADS * SQ), h=HEADS, k=SQ)
        probs = take(HEADS * SQ)
        probsT = shaped(take(HEADS * P), h=HEADS, q=P)
        o_st = take(D, R_T)
        oT = shaped(take(D, R_T + D), k=KD, t=P)
        xd = take(D, R_U + D)
        x2 = take(D, R_U + 2 * D)
        xd_last = take(D, R_U + 3 * D)
        x2_last = xd
        x1 = take(D, R_U + 4 * D)
        x1n = take(D, R_U + 5 * D)
        x1nT = shaped(take(D, R_U + 6 * D), k=KD, t=P)
        top[0] = R_U + 7 * D
        R_STATE = top[0]
        state = [shaped(take(2 * BT * 48), c=2, b=BT, t=48) for _ in range(2)]
        stmp = shaped(take(2 * P), c=2, b=BT, t=SQ)
        R_H = top[0]
        hT = shaped(take(2 * P), c=2, b=BT, t=SQ)
        R_SKIP = top[0]
        dskip = take(D)
        zst = take(D, R_U)
        zT = shaped(take(D, R_U + D), k=KD, t=P)
        hid = take(H4, R_U)
        hidT = shaped(take(H4, R_T + D), c=H4 // P, m=P)
        th = take(W4, R_U + 4 * D)
        thb = take(W4, R_U + 4 * D + W4)
        tn = take(W4, R_U + 4 * D + 2 * W4)
        bcast = shaped(take(D, R_U + 5 * D), j=NJ, n=W4)
        gate_out = take(D, R_U + 5 * D)
        gate_bias = take(D, R_T)
        agg_last = [take(D, R_T + D), take(D, R_U + 6 * D)]
        d1_bias = take(H4, R_SKIP)
        spread = shaped(take(G * P, R_U), g=G, t=P)
        tT = shaped(take(2 * P, R_H), c=2, m=P)
        back = shaped(take(G * 2 * D, R_WQ), t=G, w=2 * D)
        x_back, gate_back = back[:, :, 0:D], back[:, :, D:2 * D]
        t_z = [take(D, R_WO + i * D) for i in range(6)] + [take(D, R_O + (4 + i) * D) for i in range(2)]
        t_gamma = take(D, R_WO + 6 * D)
        t_beta = take(D, R_WO + 7 * D)
        packed_names = ["in_g", "in_b", "agg_b", "pn_g", "pn_b", "d2_b", "bc_b"]
        packed = {n: take(W4) for n in packed_names}
        ident = take(P)
        same_row = take(P)
        causal = take(SQ)
        group_mask = take(NJ)
        small = take(176)
        mvz = shaped(take(2 * G), g=G, c=2)
        zscale = take(G)
        zshift = take(G)

        ring = [take(SLOT, R_T + (1 + i) * SLOT) for i in range(3)]
        resident = [take(SLOT, R_WQ + i * SLOT) for i in range(4)] \
            + [take(SLOT, R_WKV + i * SLOT) for i in range(2)] \
            + [take(SLOT, R_U + 2 * D)] + [take(SLOT, R_O + i * SLOT) for i in range(4)] \
            + [take(SLOT, R_BC + i * SLOT) for i in range(2)] + [take(SLOT, R_U + 6 * D)]
        RING, RES = len(ring), len(resident)
        EARLY = 6
        assert R_STATE + 2 * 2 * BT * 48 + 2 * P == R_U + 8 * D
        D1P = 2 * KD
        D2P = HID // P // 2
        PIECES = D1P + D2P
        assert (PIECES - RES) % RING == 0

        s6 = shaped(small[:, 0:12], a=2, c=6)
        mv = small[:, 12:14]
        veps = small[:, 14:15]
        rstd = small[:, 15:16]
        power = small[:, 16:17]
        mx = small[:, 17:33]
        rs = small[:, 33:49]
        ri = small[:, 49:65]
        ssm = small[:, 65:85]
        apow = shaped(small[:, 85:100], l=5, c=3)
        gam = small[:, 100:101]
        s6x = shaped(small[:, 160:172], a=2, c=6)
        mvx = small[:, 172:174]
        s6f = small[:, 101:107]
        s24 = shaped(small[:, 107:131], j=NJ, c=6)
        ssmk = small[:, 131:133]
        powers8 = small[:, 133:141]
        half = small[:, 141:142]
        scratch = small[:, 142:143]
        vz = small[:, 144:152]
        t_mv = [small[:, 152 + 2 * e:154 + 2 * e] for e in range(2)]
        t_rstd = [small[:, 156 + e:157 + e] for e in range(2)]

        x2_d = nc.dram_tensor("x2_spill", [G, P, D], F32, kind="Internal").ap()
        gate_d = nc.dram_tensor("gate_spill", [G, P, D], F32, kind="Internal").ap()

        def bank(i, cols=BANK):
            return ps[:, i * BANK:i * BANK + cols]

        TA, TB = bank(0), bank(1)

        def sem(name):
            return ctx.enter_context(nc.semaphore(name))

        const_ready = sem("const_ready")
        ssm_in = sem("ssm_in")
        gam_ready = sem("gam_ready")
        ssm_pool = sem("ssm_pool")
        ssm_act = sem("ssm_act")
        ssm_arg = sem("ssm_arg")
        dve_chain = sem("dve_chain")
        pool_chain = sem("pool_chain")
        raw_in = [sem(f"raw_in{i}") for i in range(4)]
        x_loaded = sem("x_loaded")
        ctx_loaded = sem("ctx_loaded")
        wo_loaded = sem("wo_loaded")
        bc_loaded = sem("bc_loaded")
        dskip_loaded = sem("dskip_loaded")
        a_full, a_free = sem("a_full"), sem("a_free")
        b_full, b_free = sem("b_full"), sem("b_free")
        var_ready = sem("var_ready")
        rstd_ready = sem("rstd_ready")
        xn_ready = sem("xn_ready")
        qk_full, qk_evac = sem("qk_full"), sem("qk_evac")
        v_full, v_evac = sem("v_full"), sem("v_evac")
        o_full, o_evac = sem("o_full"), sem("o_evac")
        s_full, s_read = sem("s_full"), sem("s_read")
        shifted_ready = sem("shifted_ready")
        exp_ready = sem("exp_ready")
        pT_ready = sem("pT_ready")
        ost_ready = sem("ost_ready")
        y_full, y_read = sem("y_full"), sem("y_read")
        x1n_ready = sem("x1n_ready")
        xd_ready = sem("xd_ready")
        bu_full, bu_evac = sem("bu_full"), sem("bu_evac")
        h_ready = sem("h_ready")
        c_full, c_read = sem("c_full"), sem("c_read")
        par_loaded = sem("par_loaded")
        gbias_loaded = sem("gbias_loaded")
        gw_loaded = sem("gw_loaded")
        slot_in = [sem(f"slot_in{i}") for i in range(RING)]
        slot_used = sem("slot_used")
        res_in = sem("res_in")
        zv_ready, zr_ready = sem("zv_ready"), sem("zr_ready")
        st_in, st_full = sem("st_in"), sem("st_full")
        tn_ready = sem("tn_ready")
        z_ready = sem("z_ready")
        p_full = sem("p_full")
        hp_full = sem("hp_full")
        hsum_ready, hid_ready = sem("hsum_ready"), sem("hid_ready")
        g_full, g_read = sem("g_full"), sem("g_read")
        sig_ready = sem("sig_ready")
        x2_stored = sem("x2_stored")
        res_late = sem("res_late")
        agg_loaded = sem("agg_loaded")
        th_loaded, zx_loaded = sem("th_loaded"), sem("zx_loaded")
        gate_stored = sem("gate_stored")
        gate_in, x2_in = ([sem(f"{name}{i}") for i in range(2)] for name in ("gate_in", "x2_in"))
        skip_ready = sem("skip_ready")
        bc_ready = sem("bc_ready")
        tail_in = sem("tail_in")
        bb_full, bb_read = sem("bb_full"), sem("bb_read")
        tz_ready = sem("tz_ready")
        fin_ready = sem("fin_ready")
        xd_half, bzero = sem("xd_half"), sem("bzero")
        zshift_ready = sem("zshift_ready")
        passed_dve, passed_pe = sem("passed_dve"), sem("passed_pe")
        out_done = sem("out_done")
        z_added, centred = sem("z_added"), sem("centred")

        block = ctx.enter_context(nc.Block())

        NA0 = NB0 = KD + 4
        PER_TILE = 3
        NB1 = NB0 + PER_TILE * G
        N_RING = PIECES - RES
        RESIDENT_Q = [1, 3, 5, 7, 10, 12, 15, 18, 20, 22, 24, 27, 29, 31]
        BC_DONE = 2 * (KD // 2) + STEPS * N_RING
        NB2 = NB1 + 2 * G
        AGG = KD // 2

        def piece_source(q):
            if q < D1P:
                i, k = divmod(q, KD)
                return d1_w[k * P:(k + 1) * P, :].rearrange("p (j n) -> p j n", j=NJ)[:, :, i * BANK:(i + 1) * BANK]
            c, jp = divmod(q - D1P, 2)
            return d2_w.rearrange("(j c p) n -> p c j n", j=NJ, c=H4 // P)[:, c, 2 * jp:2 * jp + 2, :]

        def as_piece(slot, q):
            return shaped(slot, j=NJ, n=BANK) if q < D1P else shaped(slot, j=2, n=D)

        @block.sync
        def _(sp):
            def load_ctx(g):
                for j in range(BT):
                    sp.dma_start(ctx_in[32 * j:32 * j + SQ, :], ctx_512[g * BT + j, 0:SQ, :])\
                      .then_inc(ctx_loaded, 16)

            def load_prep(g):
                sp.dma_start(raw_wo, wo_t[g, :, :]).then_inc(wo_loaded, 16)
                for n, w in enumerate((C_re, C_im)):
                    sp.dma_start(raw_bc[:, n * P:(n + 1) * P], w[bass.ts(g, P), :]).then_inc(bc_loaded, 16)
                for n, w in enumerate((B_re, B_im)):
                    sp.dma_start(raw_bc[:, (2 + n) * P:(3 + n) * P], w[:, bass.ts(g, P)])\
                      .then_inc(bc_loaded, 16)

            sp.dma_start(x_in, x_t[0, :, :]).then_inc(x_loaded, 16)
            for n in range(KD + 4):
                s = n % 4
                if n >= 4:
                    sp.wait_ge(a_free, n - 3 if n < 8 else n - 2)
                    sp.wait_ge(b_free, n - 3)
                if n >= 4:
                    sp.dma_start(raw[s], Wq[(n - 4) * P:(n - 3) * P, :]).then_inc(raw_in[s], 16)
                else:
                    sp.dma_start(shaped(raw[s], r=4, n=L),
                                 Wkv[4 * n * P:4 * (n + 1) * P, :].rearrange("(r p) n -> p r n", p=P))\
                      .then_inc(raw_in[s], 16)
                if n == 3:
                    load_ctx(0)
            load_prep(0)
            load_ctx(1)
            sp.wait_ge(xn_ready, 1)
            sp.dma_start(x_in, x_t[1, :, :]).then_inc(x_loaded, 16)
            sp.dma_start(dskip, Dskip[None, :].broadcast_to([P, D])).then_inc(dskip_loaded, 16)

            def next_tile(it, more):
                sp.wait_ge(a_free, NA0 + PER_TILE * it + PER_TILE)
                sp.wait_ge(b_free, NB0 + PER_TILE * it + PER_TILE)
                load_prep(it + 1)
                sp.wait_ge(xn_ready, it + 2)
                if more:
                    sp.dma_start(x_in, x_t[it + 2, :, :]).then_inc(x_loaded, 16)
                    sp.wait_ge(a_free, NA0 + PER_TILE * it + PER_TILE + 2)
                    load_ctx(it + 2)

            with sp.Fori(0, G - 2) as it:
                next_tile(it, True)
            next_tile(G - 2, False)
            sp.dma_start(x_in, x_t[0, :, :]).then_inc(x_loaded, 16)

            for name, w in (("in_g", in_gamma), ("in_b", in_beta), ("agg_b", agg_b), ("pn_g", pn_gamma),
                            ("pn_b", pn_beta), ("d2_b", d2_b), ("bc_b", bc_b)):
                for j in range(NJ):
                    sp.dma_start(packed[name][32 * j:32 * j + 32, :],
                                 w[None, j * W4:(j + 1) * W4].broadcast_to([32, W4])).then_inc(par_loaded, 16)

            bc_v = bc_w.rearrange("(n j p) d -> n p j d", j=2, p=P)

            def store_x2(g, x2=x2):
                sp.wait_ge(c_read, 2 * g + 3)
                sp.dma_start(x2_d[g, :, :], x2).then_inc(x2_stored, 16)

            def next_x(g):
                sp.wait_ge(y_read, 2 * g)
                sp.dma_start(x_in, x_t[g, :, :]).then_inc(x_loaded, 16)

            def load_resident(r):
                sp.dma_start(as_piece(resident[r], RESIDENT_Q[r]), piece_source(RESIDENT_Q[r])).then_inc(res_late, 16)

            next_x(1)
            d2_v = d2_w.rearrange("(j c p) n -> p c j n", j=NJ, c=H4 // P)
            with sp.Fori(1, G // 2) as i:
                next_x(2 * i)
                store_x2(2 * i - 2)
                next_x(2 * i + 1)
                store_x2(2 * i - 1)
                sp.wait_ge(ost_ready, 2 * i)
                sp.dma_start(shaped(mem[:, bass.ds(i * SLOT + (R_O - SLOT), SLOT)], j=2, n=D),
                             d2_v[:, bass.ds(i, 1), 0:2, :].rearrange("p c j n -> p (c j) n")).then_inc(res_late, 16)
            sp.wait_ge(ost_ready, G)
            load_resident(EARLY + 4)
            sp.wait_ge(y_full, 2 * G)
            sp.dma_start(gate_bias, gate_b[None, :].broadcast_to([P, D])).then_inc(gbias_loaded, 16)
            sp.dma_start(agg_last[0], agg_w[(KD - 2) * P:(KD - 1) * P, :]).then_inc(agg_loaded, 16)
            sp.dma_start(gw, gate_w.rearrange("(k p) n -> p k n", p=P)).then_inc(gw_loaded, 16)
            last = x2_d.rearrange("g (b s) d -> (g b) s d", s=SQ)
            old = NB - 2 * BT
            sp.wait_ge(xd_ready, G)
            sp.wait_ge(x2_stored, 16 * (G - 2))
            for j in range(NJ):
                sp.dma_start(th[32 * j:32 * j + old, :], last[0:old, SQ - 1, j * W4:(j + 1) * W4])\
                  .then_inc(th_loaded, 16)
            sp.wait_ge(bu_full, G)
            load_resident(EARLY + 5)
            sp.dma_start(agg_last[1], agg_w[(KD - 1) * P:KD * P, :]).then_inc(agg_loaded, 16)
            for j in range(NJ):
                sp.dma_start(d1_bias[32 * j:32 * j + 32, :],
                             d1_b[None, j * H4:(j + 1) * H4].broadcast_to([32, H4])).then_inc(gbias_loaded, 16)
            for g, tile in ((G - 2, x2), (G - 1, x2_last)):
                sp.wait_ge(c_read, 2 * g + 3)
                for j in range(NJ):
                    sp.dma_start(th[32 * j + g * BT:32 * j + (g + 1) * BT, :],
                                 tile[SQ - 1::SQ, j * W4:(j + 1) * W4]).then_inc(th_loaded, 16)
            store_x2(G - 2)
            store_x2(G - 1, x2_last)
            sp.wait_ge(c_full, 2 * G)
            load_resident(EARLY + 6)
            sp.wait_ge(zv_ready, 1)
            sp.wait_ge(th_loaded, 48 * NJ)
            sp.wait_ge(x2_stored, 16 * G)
            load_resident(EARLY)

            sp.wait_ge(slot_used, AGG)
            load_resident(EARLY + 7)
            with sp.Fori(0, STEPS) as step:
                m = 0
                for q in range(PIECES):
                    if q in RESIDENT_Q:
                        continue
                    s = m % RING
                    sp.wait_ge(slot_used, N_RING * step + AGG + m - RING + 1)
                    sp.dma_start(as_piece(ring[s], q), piece_source(q)).then_inc(slot_in[s], 16)
                    m += 1
            for n in range(AGG):
                m = AGG + STEPS * N_RING + n
                sp.wait_ge(slot_used, m - RING + 1)
                sp.dma_start(shaped(ring[n % RING], j=2, n=D), bc_v[n, :, :, :]).then_inc(slot_in[n % RING], 16)
            sp.wait_ge(g_read, 2 * G + 2)
            sp.dma_start(t_gamma, out_gamma[None, :].broadcast_to([P, D])).then_inc(tail_in, 16)
            sp.dma_start(t_beta, out_beta[None, :].broadcast_to([P, D])).then_inc(tail_in, 16)
            sp.wait_ge(gate_stored, 16 * (G + 1))
            sp.wait_ge(p_full, STEPS)
            for t in range(G):
                if t >= 2:
                    sp.wait_ge(gate_in[t % 2], 16 * (t // 2))
                    sp.wait_ge(x2_in[t % 2], 16 * (t // 2))
                sp.dma_start(gate_back[:, t, :], gate_d[t, :, :]).then_inc(gate_in[t % 2], 16)
                sp.dma_start(x_back[:, t, :], x2_d[t, :, :]).then_inc(x2_in[t % 2], 16)
            for t in range(G):
                sp.wait_ge(fin_ready, t + 1)
                sp.dma_start(out_t[t, :, :], x_back[:, t, :]).then_inc(out_done, 16)
            sp.wait_ge(out_done, 16 * G)

        @block.gpsimd
        def _(pool):
            chain = Count(pool_chain)

            def then(instruction):
                pool.wait_ge(pool_chain, chain.one(instruction))

            def ones_where_zero(ap, base, pattern):
                return nc.gpsimd.affine_select(out=ap, in_=ap, compare_op=ALU.not_equal, fill=1.0, base=base,
                                               pattern=pattern, channel_multiplier=1)

            then(nc.gpsimd.memset(ident, 0.0))
            then(ones_where_zero(ident, 0, [[-1, P]]))
            then(nc.gpsimd.memset(power, -0.5))
            then(nc.gpsimd.memset(powers8, -0.5))
            then(nc.gpsimd.memset(half, 0.5))
            quad = shaped(probsT[:, 0, :], j=BT, k=SQ)
            then(nc.gpsimd.memset(quad, 0.0))
            then(nc.gpsimd.affine_select(out=quad, in_=quad, compare_op=ALU.is_ge, fill=MASKED, base=0,
                                         pattern=[[-SQ, BT], [-1, SQ]], channel_multiplier=1))
            for j in range(BT):
                then(nc.gpsimd.tensor_copy(causal[32 * j:32 * j + 32, :], quad[32 * j:32 * j + 32, j, :]))
            then(nc.gpsimd.memset(probsT, 0.0))
            for u in state:
                then(nc.gpsimd.memset(u, 0.0))
            nc.gpsimd.memset(group_mask, 0.0).then_inc(const_ready, 1)

            def power_of(dst, src, exponent):
                return nc.gpsimd.tensor_tensor(dst, src, exponent, ALU.pow)

            pool.wait_ge(var_ready, 1)
            power_of(rstd, veps, power).then_inc(rstd_ready, 1)
            pool.wait_ge(const_ready, 1)
            for j in range(NJ):
                then(nc.gpsimd.memset(group_mask[32 * j:32 * j + 32, j:j + 1], 1.0))
            then(nc.gpsimd.memset(same_row, 0.0))
            for m in range(1 - NJ, NJ - 1):
                then(ones_where_zero(same_row, 32 * m, [[-1, P]]))
            ones_where_zero(same_row, 32 * (NJ - 1), [[-1, P]]).then_inc(const_ready, 1)

            with pool.Fori(1, G) as g:
                pool.wait_ge(var_ready, g + 1)
                power_of(rstd, veps, power).then_inc(rstd_ready, 1)
            pool.wait_ge(ssm_pool, 1)
            power_of(gam, ssm[:, 12:13], half).then_inc(gam_ready, 1)

            def load_o(g):
                nc.gpsimd.tensor_copy(o_st, o_all[:, g, :]).then_inc(ost_ready, 1)

            def residual(g, xd=xd):
                pool.wait_ge(var_ready, G + g + 1)
                power_of(rstd, veps, power).then_inc(rstd_ready, 1)
                if xd is not xd_last:
                    pool.wait_ge(c_read, 2 * g + 1)
                pool.wait_ge(x1n_ready, g + 1)
                nc.gpsimd.tensor_tensor(xd, x1n, dskip, ALU.mult).then_inc(xd_half, 1)
                pool.wait_ge(xd_half, g + 1)
                nc.gpsimd.tensor_tensor(xd, xd, x1, ALU.add).then_inc(xd_ready, 1)

            pool.wait_ge(dskip_loaded, 16)
            pool.wait_ge(o_evac, 2)
            load_o(0)
            pool.wait_ge(b_full, NB1 + 1)
            load_o(1)
            residual(0)
            with pool.Fori(1, G - 1) as g:
                pool.wait_ge(b_full, NB1 + 2 * g)
                pool.wait_ge(o_evac, 2 * G)
                load_o(g + 1)
                residual(g)
            residual(G - 1, xd_last)

            pool.wait_ge(zv_ready, 1)
            power_of(zscale, vz, powers8).then_inc(zr_ready, 1)
            pool.wait_ge(var_ready, 2 * G + 1)
            power_of(rstd, veps, power).then_inc(rstd_ready, 1)
            pool.wait_ge(var_ready, 2 * G + 2)
            power_of(rstd, veps, power).then_inc(rstd_ready, 1)
            with pool.Fori(0, STEPS) as step:
                pool.wait_ge(var_ready, step + (2 * G + 3))
                power_of(rstd, veps, power).then_inc(rstd_ready, 1)
            pool.wait_ge(b_full, NB2 + 3 * STEPS)
            then(nc.gpsimd.memset(spread, 0.0))
            for j in range(NJ):
                then(ones_where_zero(spread.rearrange("p g (q s) -> p g q s", q=BT), -32 * j,
                                     [[-BT, G], [-1, BT], [0, SQ]]))
            pool.wait_ge(gate_stored, 16 * (G + 1))
            nc.gpsimd.memset(bcast, 0.0).then_inc(bzero, 1)

            def skipped(t):
                pool.wait_ge(tz_ready, t + 1)
                nc.gpsimd.tensor_tensor(x_back[:, t, :], x_back[:, t, :], t_beta, ALU.add).then_inc(skip_ready, 1)

            pool.wait_ge(tail_in, 32)
            for t in range(G):
                if t + 1 < G:
                    pool.wait_ge(bb_read, 2 * t + 4)
                    pool.wait_ge(tz_ready, t + 2)
                    nc.gpsimd.tensor_tensor(gate_back[:, t + 1, :], gate_back[:, t + 1, :], t_z[t + 1], ALU.add)\
                        .then_inc(z_added, 1)
                skipped(t)
                pool.wait_ge(var_ready, t + (2 * G + STEPS + 3))
                power_of(t_rstd[t % 2], t_rstd[t % 2], power).then_inc(rstd_ready, 1)

        @block.scalar
        def _(act):
            A = Count(a_free)
            qk, vv = Count(qk_evac), Count(v_evac)

            def copy(dst, src):
                return nc.scalar.activation(dst, src, ACT.Copy)

            def bank_a(dst, src=None):
                act.wait_ge(a_full, A.term + A.n + 1)
                A.one(copy(dst, shaped(TA, k=4, n=P) if src is None else src))

            act.dma_start(ssm[:, 0:1], nu_log[:, None]).then_inc(ssm_in, 16)
            act.dma_start(ssm[:, 1:2], theta_log[:, None]).then_inc(ssm_in, 16)
            act.wait_ge(ssm_in, 32)
            nc.scalar.activation(ssm[:, 2:4], ssm[:, 0:2], ACT.Exp).then_inc(ssm_act, 1)

            for m in range(4):
                for r in range(2):
                    n = 4 * m + r
                    if r == 0:
                        act.wait_ge(a_full, A.n + 1)
                        copy(wkvT[:, :, n * P:(n + 1) * P], shaped(TA[:, 0:2 * P], k=KL, n=P))
                    else:
                        A.one(copy(wkvT[:, :, n * P:(n + 1) * P], shaped(TA[:, 2 * P:4 * P], k=KL, n=P)))

            def into(dst, f):
                act.wait_ge(qk_full, qk.term + qk.n + 1)
                qk.one(copy(dst[:, 4 * f:4 * f + 4, :], shaped(bank(2 + f), c=4, t=P)))

            def into_v(n):
                act.wait_ge(v_full, vv.term + vv.n + 1)
                vv.one(copy(v[:, n * BANK:(n + 1) * BANK], bank(4 + n)))

            bank_a(ctxT, shaped(TA[:, 0:L], k=KL, n=P))
            for n in range(KD):
                bank_a(wqT[:, 0:4, n * P:(n + 1) * P])
                if n < 2:
                    into(kT, n)
                elif n < 4:
                    into_v(n - 2)

            def transposed(g):
                bank_a(xnT[:, 0:4, :])
                bank_a(ctxT, shaped(TA[:, 0:L], k=KL, n=P))

            def projected(g):
                into(qT, 0)
                into(qT, 1)
                bank_a(woT[:, 4:8, bass.ts(g, P)])
                into(kT, 0)
                into(kT, 1)
                into_v(0)
                into_v(1)

            def exponentials(g):
                act.wait_ge(shifted_ready, g + 1)
                nc.scalar.activation(probs, scores.rearrange("p h k -> p (h k)"), ACT.Exp,
                                     scale=float(HD) ** -0.5).then_inc(exp_ready, 1)

            bank_a(xnT[:, 0:4, :])
            act.wait_ge(ssm_arg, 1)
            nc.scalar.activation(ssm[:, 7:8], ssm[:, 4:5], ACT.Exp)
            nc.scalar.activation(ssm[:, 8:9], ssm[:, 5:6], ACT.Sin)
            nc.scalar.activation(ssm[:, 9:10], ssm[:, 5:6], ACT.Sin, scale=0.5).then_inc(ssm_act, 1)
            into(qT, 0)
            into(qT, 1)
            bank_a(woT[:, 4:8, 0:P])
            transposed(1)
            with act.Fori(0, G - 2) as it:
                A.enter(it, PER_TILE), qk.enter(it, 4), vv.enter(it, 2)
                exponentials(it)
                projected(it + 1)
                transposed(it + 2)
                A.leave(G - 2), qk.leave(G - 2), vv.leave(G - 2)
            exponentials(G - 2)
            projected(G - 1)

            bank_a(oT[:, 0:4, :])
            for r in range(EARLY):
                act.dma_start(as_piece(resident[r], RESIDENT_Q[r]), piece_source(RESIDENT_Q[r])).then_inc(res_in, 16)
            agg_v = agg_w.rearrange("(n j p) d -> n p j d", j=2, p=P)
            act.dma_start(shaped(ring[0], j=2, n=D), agg_v[0, :, :, :]).then_inc(slot_in[0], 16)
            exponentials(G - 1)
            act.wait_ge(o_full, 2 * G)
            for m in (1, 2):
                act.dma_start(shaped(ring[m], j=2, n=D), agg_v[m, :, :, :]).then_inc(slot_in[m], 16)

            def bu(g):
                act.wait_ge(bu_full, g + 1)
                for c in range(2):
                    last = nc.scalar.activation(state[0][:, c, :, 16:16 + SQ],
                                                shaped(bank(6)[:, c * P:(c + 1) * P], b=BT, t=SQ),
                                                ACT.Copy, scale=gam)
                last.then_inc(bu_evac, 1)

            act.wait_ge(gam_ready, 1)
            act.sem_inc(bu_evac, 1)
            bank_a(oT[:, 0:4, :])
            with act.Fori(1, G - 1) as g:
                A.enter(g - 1, 2)
                bank_a(x1nT[:, 0:4, :])
                bu(g - 1)
                bank_a(oT[:, 0:4, :])
                A.leave(G - 2)
            bank_a(x1nT[:, 0:4, :])
            bu(G - 2)
            bank_a(x1nT[:, 0:4, :])
            act.wait_ge(h_ready, G - 1)
            bu(G - 1)

            def z_tile(dst, src, t):
                at = slice(t, t + 1) if isinstance(t, int) else bass.ds(t, 1)
                return nc.scalar.activation(dst, src, ACT.Identity, scale=zscale[:, at], bias=zshift[:, at])

            def z_load(t, transposed_before):
                act.wait_ge(b_full, transposed_before)
                act.dma_start(zst, x2_d[t, :, :]).then_inc(zx_loaded, 16)

            def z_norm(t):
                act.wait_ge(zx_loaded, 16 * t + 16)
                z_tile(zst, zst, t).then_inc(z_ready, 1)

            def gate_store(t):
                act.wait_ge(g_read, 2 * t + 4)
                act.dma_start(gate_d[t, :, :], gate_out).then_inc(gate_stored, 16)

            def before_hidden(step):
                bank_a(tT, shaped(TA[:, 0:2 * P], c=2, m=P))
                bank_a(zT[:, 0:4, :])
                gate_store(2 * step)

            def hidden(step, more):
                for i in range(2):
                    act.wait_ge(hsum_ready, 2 * step + i + 1)
                    part = hid[:, i * BANK:(i + 1) * BANK]
                    nc.scalar.activation(part, part, ACT.Gelu).then_inc(hid_ready, 1)
                bank_a(hidT[:, 0:4, :])
                if more:
                    z_load(2 * step + 2, NB2 + 3 * step + 3)
                    z_norm(2 * step + 2)
                gate_store(2 * step + 1)
                if more:
                    bank_a(zT[:, 0:4, :])
                    z_load(2 * step + 3, NB2 + 3 * step + 4)
                    z_norm(2 * step + 3)

            act.wait_ge(x2_stored, 16 * (G - 2))
            act.wait_ge(y_read, 2 * G)
            z_load(0, NB2)
            act.wait_ge(zshift_ready, 1)
            z_norm(0)
            act.wait_ge(x2_stored, 16 * G)
            act.wait_ge(th_loaded, 48 * NJ)
            bank_a(zT[:, 0:4, :])
            z_load(1, NB2 + 1)
            bank_a(tT, shaped(TA[:, 0:2 * P], c=2, m=P))
            z_norm(1)
            before_hidden(0)
            with act.Fori(0, STEPS - 1) as step:
                A.enter(step, 4)
                hidden(step, True)
                before_hidden(step + 1)
                A.leave(STEPS - 1)
            hidden(STEPS - 1, False)
            bank_a(tT, shaped(TA[:, 0:2 * P], c=2, m=P))

            def sigmoid_and_z(t):
                act.wait_ge(gate_in[t % 2], 16 * (t // 2 + 1))
                nc.scalar.activation(gate_back[:, t, :], gate_back[:, t, :], ACT.Sigmoid).then_inc(sig_ready, 1)
                act.wait_ge(x2_in[t % 2], 16 * (t // 2 + 1))
                z_tile(t_z[t], x_back[:, t, :], t).then_inc(tz_ready, 1)

            act.wait_ge(g_read, 2 * G + 2)
            nc.scalar.activation(scratch, zshift[:, 0:1], ACT.Sigmoid)
            for t in range(G):
                sigmoid_and_z(t)

        @block.vector
        def _(dve):
            chain = Count(dve_chain)
            B = Count(b_free)

            def then(instruction):
                dve.wait_ge(dve_chain, chain.one(instruction))

            def bank_b(dst, src=None):
                dve.wait_ge(b_full, B.term + B.n + 1)
                B.one(nc.vector.tensor_copy(dst, shaped(TB, k=4, n=P) if src is None else src))

            def settled():
                dve.sem_inc(passed_dve, 1)

            def moments(src, eps):
                for i in range(2):
                    ins = nc.vector.bn_stats(s6[:, i, :], src[:, i * BANK:(i + 1) * BANK])
                    chain.one(ins) if i == 0 else then(ins)
                settled()
                then(nc.vector.bn_aggr(mv, s6))
                nc.vector.tensor_scalar_add(veps, mv[:, 1:2], eps).then_inc(var_ready, 1)

            def norm(dst, src, n):
                dve.wait_ge(rstd_ready, n + 1)
                return nc.vector.tensor_scalar(dst, src, mv[:, 0:1], rstd, ALU.subtract, ALU.mult)

            def layer_norm(g):
                dve.wait_ge(x_loaded, 16 * g + 16)
                moments(x_in, LN_EPS)
                norm(xn, x_in, g).then_inc(xn_ready, 1)

            layer_norm(0)

            col = [ssm[:, i:i + 1] for i in range(20)]
            ts, tt, stt = nc.vector.tensor_scalar, nc.vector.tensor_tensor, nc.vector.scalar_tensor_tensor

            def angles():
                dve.wait_ge(ssm_act, 1)
                then(ts(col[4], col[2], 1.0, -1.0, ALU.add, ALU.mult))
                then(ts(col[10], col[3], 1.0 / TWO_PI, None, ALU.mult))
                turns = ssmk[:, 0:1].bitcast(I32)
                then(nc.vector.tensor_copy(turns, col[10]))
                then(nc.vector.tensor_copy(col[10], turns))
                then(stt(col[5], col[10], -6.28125, col[3], ALU.mult, ALU.add))
                then(stt(col[5], col[10], -(TWO_PI - 6.28125), col[5], ALU.mult, ALU.add))
                then(ts(col[11], col[5], TWO_PI / 2, -TWO_PI, ALU.is_gt, ALU.mult))
                then(tt(col[5], col[5], col[11], ALU.add))
                then(ts(col[11], col[5], -TWO_PI / 2, TWO_PI, ALU.is_lt, ALU.mult))
                then(tt(col[5], col[5], col[11], ALU.add))
                ts(col[5], col[5], 3.1415925, -3.1415925, ALU.min, ALU.max).then_inc(ssm_arg, 1)

            def powers():
                dve.wait_ge(ssm_act, 2)
                then(tt(col[11], col[9], col[9], ALU.mult))
                then(ts(col[11], col[11], -2.0, 1.0, ALU.mult, ALU.add))
                then(tt(col[12], col[7], col[7], ALU.mult))
                then(ts(col[12], col[12], -1.0, 1.0, ALU.mult, ALU.add))
                ts(col[12], col[12], 0.0, None, ALU.max).then_inc(ssm_pool, 1)
                then(tt(apow[:, 0, 0:1], col[7], col[11], ALU.mult))
                then(tt(apow[:, 0, 1:2], col[7], col[8], ALU.mult))
                then(ts(apow[:, 0, 2:3], apow[:, 0, 1:2], -1.0, None, ALU.mult))
                for l in range(1, 5):
                    re, im = apow[:, l - 1, 0:1], apow[:, l - 1, 1:2]
                    then(tt(col[13], im, im, ALU.mult))
                    then(tt(col[14], re, re, ALU.mult))
                    then(tt(apow[:, l, 0:1], col[14], col[13], ALU.subtract))
                    then(tt(col[13], re, im, ALU.mult))
                    then(ts(apow[:, l, 1:2], col[13], 2.0, None, ALU.mult))
                    then(ts(apow[:, l, 2:3], col[13], -2.0, None, ALU.mult))


            for m in range(4):
                dve.wait_ge(b_full, B.n + 1)
                for r in range(2):
                    n = 4 * m + 2 + r
                    ins = nc.vector.tensor_copy(wkvT[:, :, n * P:(n + 1) * P],
                                                shaped(TB[:, r * 2 * P:(r + 1) * 2 * P], k=KL, n=P))
                B.one(ins)
            with dve.Fori(0, KD // 4) as i:
                B.enter(i, 4)
                for s in range(4):
                    bank_b(wqT[:, 4:8, bass.ds(i * 4 * P + s * P, P)])
                B.leave(KD // 4)

            def prepared_o(g):
                bank_b(woT[:, 0:4, bass.ts(g, P)])

            def prepared_bc(g):
                dve.wait_ge(b_full, B.term + B.n + 1)
                nc.vector.tensor_copy(cT[:, 0, bass.ts(g, P)], TB[:, 0:P])
                nc.vector.tensor_scalar_mul(cT[:, 1, bass.ts(g, P)], TB[:, P:2 * P], -1.0)
                B.one(nc.vector.tensor_copy(bT[:, :, g, :], shaped(TB[:, 2 * P:4 * P], c=2, n=P)))

            def softmax(g):
                dve.wait_ge(s_full, g + 1)
                mask = causal[:, None, :].broadcast_to([P, HEADS // 2, SQ])
                for e in range(2):
                    ins = tt(scores[:, e::2, :], shaped(bank(6 + e)[:, 0:BANK // 2], h=HEADS // 2, k=SQ), mask, ALU.add)
                    chain.one(ins) if e == 0 else ins.then_inc(s_read, 1)
                dve.wait_ge(s_read, g + 2)
                then(nc.vector.reduce_max(mx, scores, axis=AX.X))
                tt(scores, scores, mx[:, :, None].broadcast_to([P, HEADS, SQ]), ALU.subtract)\
                    .then_inc(shifted_ready, 1)
                dve.wait_ge(exp_ready, g + 1)
                then(nc.vector.reduce_sum(rs, shaped(probs, h=HEADS, k=SQ), axis=AX.X))
                then(nc.vector.reciprocal(ri, rs))
                for j in range(BT):
                    r = slice(32 * j, 32 * j + 32)
                    last = nc.vector.transpose(probsT[r, :, 32 * j:32 * j + SQ], probs[r, :])
                last.then_inc(pT_ready, 1)

            def attention_out(g):
                for n in range(2):
                    dve.wait_ge(o_full, 2 * g + n + 1)
                    tt(o_all[:, g, n * BANK:(n + 1) * BANK], bank(4 + n), ri[:, 8 * n:8 * n + 8, None].broadcast_to([P, 8, HD]), ALU.mult)\
                        .then_inc(o_evac, 1)

            bank_b(xnT[:, 4:8, :])
            angles()
            layer_norm(1)
            prepared_o(0)
            powers()
            prepared_bc(0)
            dve.wait_ge(const_ready, 1)
            dve.sem_inc(s_read, 1)

            def attend(it, more):
                bank_b(xnT[:, 4:8, :])
                softmax(it)
                prepared_o(it + 1)
                if more:
                    layer_norm(it + 2)
                attention_out(it)
                prepared_bc(it + 1)

            with dve.Fori(0, G - 2) as it:
                B.enter(it, PER_TILE), chain.enter(it, 7)
                attend(it, True)
                B.leave(G - 2), chain.leave(G - 2)
            attend(G - 2, False)
            bank_b(oT[:, 4:8, :])
            softmax(G - 1)

            def residual(g, n, meanwhile=None):
                h = slice(n * BANK, (n + 1) * BANK)
                if n == 0:
                    dve.wait_ge(x_loaded, 16 * g + 16 * (G + 1))
                dve.wait_ge(y_full, 2 * g + n + 1)
                tt(x1[:, h], x_in[:, h], bank(2 + n), ALU.add).then_inc(y_read, 1)
                dve.wait_ge(y_read, 2 * g + n + 1)
                settled()
                ins = nc.vector.bn_stats(s6[:, n, :], x1[:, h])
                if n == 0:
                    chain.one(ins)
                    return
                then(ins)
                settled()
                then(nc.vector.bn_aggr(mv, s6))
                nc.vector.tensor_scalar_add(veps, mv[:, 1:2], LN_EPS).then_inc(var_ready, 1)
                if meanwhile:
                    meanwhile()
                norm(x1n, x1, G + g).then_inc(x1n_ready, 1)

            def recurrence(g, before=()):
                dve.wait_ge(bu_evac, g + 2)
                for l in range(5):
                    if l in before:
                        before[l]()
                    s, src, dst = 2 ** l, state[l % 2], state[(l + 1) % 2]
                    a, b, nb = (apow[:, l, i:i + 1] for i in range(3))
                    now, old = slice(16, 16 + SQ), slice(16 - s, 16 - s + SQ)
                    to = dst[:, :, :, now] if l < 4 else hT
                    then(stt(stmp.rearrange("p c b t -> p (c b) t"),
                             src.rearrange("p c b t -> p (c b) t")[:, :, old], a,
                             src.rearrange("p c b t -> p (c b) t")[:, :, now], ALU.mult, ALU.add))
                    chain.one(stt(to[:, 0], src[:, 1, :, old], nb, stmp[:, 0], ALU.mult, ALU.add))
                    ins = stt(to[:, 1], src[:, 0, :, old], b, stmp[:, 1], ALU.mult, ALU.add)
                    then(ins) if l < 4 else ins.then_inc(h_ready, 1)

            def add_states(g, first, xd=xd, at=4, x2=x2):
                dve.wait_ge(xd_ready, g + 1)
                if not first and x2 is not x2_last:
                    dve.wait_ge(x2_stored, 16 * g)
                for n in range(2):
                    h = slice(n * BANK, (n + 1) * BANK)
                    dve.wait_ge(c_full, 2 * g + n + 1)
                    tt(x2[:, h], xd[:, h], bank(at + n), ALU.add).then_inc(c_read, 1)
                dve.wait_ge(c_read, 2 * g + 3)
                settled()
                for i in range(2):
                    ins = nc.vector.bn_stats(s6x[:, i, :], x2[:, i * BANK:(i + 1) * BANK])
                    chain.one(ins) if i == 0 else then(ins)
                settled()
                then(nc.vector.bn_aggr(mvx, s6x))
                chain.one(nc.vector.tensor_copy(mvz[:, g, :], mvx))

            dve.sem_inc(c_read, 1)
            residual(0, 0)
            attention_out(G - 1)
            residual(0, 1, lambda: bank_b(oT[:, 4:8, :]))

            def turn(g, first):
                bank_b(x1nT[:, 4:8, :])
                dve.wait_ge(xd_ready, g)
                residual(g, 0)
                recurrence(g - 1)
                residual(g, 1, lambda: bank_b(oT[:, 4:8, :]))
                add_states(g - 1, first)

            turn(1, True)
            with dve.Fori(2, G - 1) as g:
                B.enter(g - 2, 2), chain.enter(g - 2, 21)
                turn(g, False)
                B.leave(G - 3), chain.leave(G - 3)
            bank_b(x1nT[:, 4:8, :])
            dve.wait_ge(xd_ready, G - 1)
            residual(G - 1, 0)
            residual(G - 1, 1)
            recurrence(G - 2, {1: lambda: bank_b(x1nT[:, 4:8, :])})
            recurrence(G - 1, {4: lambda: dve.wait_ge(c_full, 2 * G - 2)})
            add_states(G - 2, False)
            add_states(G - 1, False, xd_last, 2, x2_last)

            dve.wait_ge(dve_chain, chain.n)
            ts(vz, mvz[:, :, 1], LN_EPS, None, ALU.add).then_inc(zv_ready, 1)
            dve.wait_ge(zr_ready, 1)
            then(tt(zshift, mvz[:, :, 0], zscale, ALU.mult))
            ts(zshift, zshift, -1.0, None, ALU.mult).then_inc(zshift_ready, 1)

            dve.sem_inc(g_read, 2)
            dve.sem_inc(gate_stored, 16)

            st_n = Count(st_in)

            def packed_norm(dst, src, eps, n, meanwhile=None):
                then(nc.vector.bn_stats(s6f, src))
                st_n.one(tt(s24, s6f[:, None, :].broadcast_to([P, NJ, 6]),
                            group_mask[:, :, None].broadcast_to([P, NJ, 6]), ALU.mult))
                if meanwhile:
                    meanwhile()
                dve.wait_ge(st_full, st_n.term + st_n.n)
                settled()
                then(nc.vector.bn_aggr(mv, bank(7)[:, 0:24]))
                nc.vector.tensor_scalar_add(veps, mv[:, 1:2], eps).then_inc(var_ready, 1)
                then(norm(dst, src, n))

            dve.wait_ge(par_loaded, 16 * 7 * NJ)
            dve.wait_ge(th_loaded, 48 * NJ)
            dve.wait_ge(const_ready, 2)
            def first_z():
                dve.wait_ge(x2_stored, 16 * G)
                bank_b(zT[:, 4:8, :])

            packed_norm(tn, th, LN_EPS, 2 * G)
            packed_norm(thb, tn, FFN_EPS, 2 * G + 1, first_z)
            then(tt(thb, thb, packed["in_g"], ALU.mult))
            tt(tn, thb, packed["in_b"], ALU.add).then_inc(tn_ready, 1)
            dve.wait_ge(slot_used, AGG)
            then(tt(th, bank(6)[:, 0:W4], packed["agg_b"], ALU.add))

            dve.wait_ge(gbias_loaded, 16 * (1 + NJ))

            def gate_sum(t, n):
                h = slice(n * BANK, (n + 1) * BANK)
                dve.wait_ge(g_full, 2 * t + n + 1)
                if n == 0:
                    dve.wait_ge(gate_stored, 16 * t + 16)
                tt(gate_out[:, h], bank(4 + n), gate_bias[:, h], ALU.add).then_inc(g_read, 1)

            def hidden_sum(step, i):
                h = slice(i * BANK, (i + 1) * BANK)
                dve.wait_ge(hp_full, 2 * step + i + 1)
                tt(hid[:, h], bank(2 + i), d1_bias[:, h], ALU.add).then_inc(hsum_ready, 1)

            def thinking(step, more):
                packed_norm(tn, th, FFN_EPS, step + 2 * G + 2, lambda: gate_sum(2 * step, 0))
                then(tt(tn, tn, packed["pn_g"], ALU.mult))
                tt(tn, tn, packed["pn_b"], ALU.add).then_inc(tn_ready, 1)
                then(tt(thb, th, packed["d2_b"], ALU.add))
                gate_sum(2 * step, 1)
                bank_b(zT[:, 4:8, :])
                hidden_sum(step, 0)
                gate_sum(2 * step + 1, 0)
                hidden_sum(step, 1)
                bank_b(hidT[:, 4:8, :])
                gate_sum(2 * step + 1, 1)
                if more:
                    bank_b(zT[:, 4:8, :])
                dve.wait_ge(p_full, step + 1)
                then(tt(th, bank(6)[:, 0:W4], thb, ALU.add))

            with dve.Fori(0, STEPS - 1) as step:
                B.enter(step, 3), chain.enter(step, 6), st_n.enter(step, 1)
                thinking(step, True)
                B.leave(STEPS - 1), chain.leave(STEPS - 1), st_n.leave(STEPS - 1)
            thinking(STEPS - 1, False)
            nc.vector.tensor_copy(tn, th).then_inc(tn_ready, 1)

            dve.wait_ge(slot_used, BC_DONE)
            dve.wait_ge(bzero, 1)
            for j in range(NJ):
                r = slice(32 * j, 32 * j + 32)
                last = tt(bcast[r, j, :], bank(6)[r, 0:W4], packed["bc_b"][r, :], ALU.add)
            last.then_inc(bc_ready, 1)

            def gated(t):
                dve.wait_ge(sig_ready, t + 1)
                for n in range(2):
                    h = slice(n * BANK, (n + 1) * BANK)
                    dve.wait_ge(bb_full, 2 * t + n + 1)
                    tt(gate_back[:, t, h], bank(2 + 2 * (t % 2) + n), gate_back[:, t, h], ALU.mult).then_inc(bb_read, 1)

            def finish(t):
                dve.wait_ge(rstd_ready, t + (2 * G + STEPS + 3))
                dve.wait_ge(skip_ready, t + 1)
                dve.wait_ge(centred, t + 1)
                stt(x_back[:, t, :], gate_back[:, t, :], t_rstd[t % 2], x_back[:, t, :], ALU.mult, ALU.add)\
                    .then_inc(fin_ready, 1)

            dve.wait_ge(tail_in, 32)
            gated(0)
            for t in range(G):
                e, total = t % 2, gate_back[:, t, :]
                if t == 0:
                    dve.wait_ge(tz_ready, 1)
                    dve.wait_ge(bb_read, 2)
                    chain.one(tt(total, total, t_z[t], ALU.add))
                if t + 1 < G:
                    gated(t + 1)
                if t == 0:
                    dve.wait_ge(dve_chain, chain.n)
                else:
                    dve.wait_ge(z_added, t)
                for i in range(2):
                    ins = nc.vector.bn_stats(s6[:, i, :], total[:, i * BANK:(i + 1) * BANK])
                    chain.one(ins) if i == 0 else then(ins)
                then(nc.vector.bn_aggr(t_mv[e], s6))
                if t >= 2:
                    dve.wait_ge(fin_ready, t - 1)
                nc.vector.tensor_scalar_add(t_rstd[e], t_mv[e][:, 1:2], FFN_EPS).then_inc(var_ready, 1)
                stt(total, total, t_mv[e][:, 0:1], t_gamma, ALU.subtract, ALU.mult).then_inc(centred, 1)
                if t >= 1:
                    finish(t - 1)
            finish(G - 1)

        @block.tensor
        def _(pe):
            A, B = Count(a_full), Count(b_full)

            def four(fulls, free, dst, blocks):
                if not (isinstance(fulls.term, int) and fulls.term + fulls.n == 0):
                    pe.wait_ge(free, fulls.term + fulls.n)
                for i, b in enumerate(blocks):
                    last = nc.tensor.transpose(dst[:, i * P:(i + 1) * P], b, ident)
                fulls.one(last)

            def bank_a(*blocks):
                four(A, a_free, TA, blocks)

            def bank_b(*blocks):
                four(B, b_free, TB, blocks)

            def cols(ap, *ks):
                return [ap[:, k * P:(k + 1) * P] for k in ks]

            def product(dst, lhsTs, rhss):
                for k, (l, r) in enumerate(zip(lhsTs, rhss)):
                    last = nc.tensor.matmul(dst, l, r, start=(k == 0), stop=(k == len(lhsTs) - 1))
                return last

            pe.wait_ge(const_ready, 1)
            for s in range(4):
                pe.wait_ge(raw_in[s], 16)
                bank_a(*cols(raw[s], 0, 1, 2, 3))
                bank_b(*cols(raw[s], 4, 5, 6, 7))

            def heads_product(f, w, acts, ks):
                for c in range(4 * f, 4 * f + 4):
                    last = product(bank(2 + f)[:, (c % 4) * P:(c % 4 + 1) * P],
                                   [w[:, k, c * P:(c + 1) * P] for k in range(ks)],
                                   [acts[:, k, :] for k in range(ks)])
                last.then_inc(qk_full, 1)

            def transposed_context(g):
                pe.wait_ge(ctx_loaded, 16 * BT * g + 16 * BT)
                bank_a(*cols(ctx_in, 0, 1))

            def keys(g, f):
                heads_product(f, wkvT, ctxT, KL)

            def values(g, n, first=False):
                if not first:
                    pe.wait_ge(o_evac, 2 * g - 1 + n)
                product(bank(4 + n), [ctxT[:, k, :] for k in range(KL)],
                        [wkvT[:, k, D + n * BANK:D + (n + 1) * BANK] for k in range(KL)]).then_inc(v_full, 1)

            transposed_context(0)
            for n in range(KD):
                pe.wait_ge(raw_in[n % 4], 16 * (n // 4) + 32)
                bank_a(*cols(raw[n % 4], 0, 1, 2, 3))
                bank_b(*cols(raw[n % 4], 4, 5, 6, 7))
                if n < 2:
                    keys(0, n)
                elif n < 4:
                    values(0, n - 2, True)

            def transposed_x(g):
                pe.wait_ge(xn_ready, g + 1)
                bank_a(*cols(xn, 0, 1, 2, 3))
                bank_b(*cols(xn, 4, 5, 6, 7))

            def prepare_bc(g):
                pe.wait_ge(bc_loaded, 64 * g + 64)
                bank_b(*cols(raw_bc, 0, 1, 2, 3))

            def queries(g, first):
                pe.wait_ge(a_free, A.n if first else A.term + A.n - 1)
                pe.wait_ge(b_free, B.term + B.n)
                for f in range(2):
                    pe.wait_ge(qk_evac, f + 1 if first else 4 * g - 1 + f)
                    heads_product(f, wqT, xnT, KD)
                    if f == 0:
                        pe.wait_ge(wo_loaded, 16 * g + 16)
                        bank_b(*cols(raw_wo, 0, 1, 2, 3))
                bank_a(*cols(raw_wo, 4, 5, 6, 7))

            def score(g):
                pe.wait_ge(qk_evac, 4 * g + 4)
                pe.wait_ge(s_read, g + 1)
                pe.sem_inc(passed_pe, 1)
                for c in range(KD):
                    for e in range(2):
                        for j in range(BT):
                            r, t = slice(64 * e, 64 * e + HD), slice(32 * j, 32 * j + SQ)
                            last = nc.tensor.matmul(bank(6 + e)[t, c * SQ:(c + 1) * SQ], qT[r, c, t], kT[r, c, t],
                                                    start=True, stop=True)
                last.then_inc(s_full, 1)

            def weighted(g):
                pe.wait_ge(pT_ready, g + 1)
                pe.wait_ge(v_evac, 2 * g + 2)
                for n in range(2):
                    for h in range(8 * n, 8 * n + 8):
                        last = nc.tensor.matmul(bank(4 + n)[:, (h % 8) * HD:(h % 8 + 1) * HD], probsT[:, h, :],
                                                v[:, h * HD:(h + 1) * HD], start=True, stop=True)
                    last.then_inc(o_full, 1)

            transposed_x(0)
            queries(0, True)
            prepare_bc(0)
            with pe.Fori(0, G - 1) as it:
                A.enter(it, PER_TILE), B.enter(it, PER_TILE)
                transposed_x(it + 1)
                score(it)
                transposed_context(it + 1)
                queries(it + 1, False)
                weighted(it)
                prepare_bc(it + 1)
                for f in range(2):
                    pe.wait_ge(qk_evac, 4 * it + 5 + f)
                    keys(it + 1, f)
                for n in range(2):
                    values(it + 1, n)
                A.leave(G - 1), B.leave(G - 1)

            def load_o(g):
                pe.wait_ge(ost_ready, g + 1)
                bank_a(*cols(o_st, 0, 1, 2, 3))
                bank_b(*cols(o_st, 4, 5, 6, 7))

            def project(g, n, first=False):
                if not first:
                    pe.wait_ge(y_read, 2 * g - 1 + n)
                product(bank(2 + n), [oT[:, k, :] for k in range(KD)],
                        [woT[:, k, n * BANK:(n + 1) * BANK] for k in range(KD)]).then_inc(y_full, 1)

            def transpose_x1n(g):
                pe.wait_ge(x1n_ready, g + 1)
                bank_a(*cols(x1n, 0, 1, 2, 3))
                bank_b(*cols(x1n, 4, 5, 6, 7))

            def inputs(g):
                pe.wait_ge(bu_evac, g + 1)
                pe.wait_ge(a_free, A.term + A.n)
                pe.wait_ge(b_free, B.term + B.n)
                for c in range(2):
                    last = product(bank(6)[:, c * P:(c + 1) * P], [bT[:, c, k, :] for k in range(KD)],
                                   [x1nT[:, k, :] for k in range(KD)])
                last.then_inc(bu_full, 1)

            def outputs(g, first, at=4):
                pe.wait_ge(h_ready, g + 1)
                for n in range(2):
                    if not first:
                        pe.wait_ge(c_read, 2 * g + n)
                    product(bank(at + n), [hT[:, c].rearrange("p b t -> p (b t)") for c in range(2)],
                            [cT[:, c, n * BANK:(n + 1) * BANK] for c in range(2)]).then_inc(c_full, 1)

            score(G - 1)
            load_o(0)
            pe.wait_ge(a_free, A.n)
            pe.wait_ge(b_free, B.n)
            project(0, 0, True)
            weighted(G - 1)
            project(0, 1, True)
            load_o(1)
            pe.wait_ge(a_free, A.n)
            pe.wait_ge(b_free, B.n)
            project(1, 0)
            transpose_x1n(0)
            inputs(0)
            project(1, 1)
            load_o(2)
            outputs(0, True)

            def turn(g):
                transpose_x1n(g - 1)
                project(g, 0)
                inputs(g - 1)
                project(g, 1)
                load_o(g + 1)
                outputs(g - 1, False)

            with pe.Fori(2, G - 1) as g:
                A.enter(g - 2, 2), B.enter(g - 2, 2)
                turn(g)
                A.leave(G - 3), B.leave(G - 3)
            transpose_x1n(G - 2)
            project(G - 1, 0)
            project(G - 1, 1)
            inputs(G - 2)
            transpose_x1n(G - 1)
            inputs(G - 1)
            outputs(G - 2, False)
            pe.wait_ge(y_read, 2 * G)
            outputs(G - 1, True, 2)

            pe.wait_ge(const_ready, 2)
            fills = [Count(s) for s in slot_in]
            used = Count(slot_used)

            def stats(n):
                pe.wait_ge(st_in, n)
                nc.tensor.matmul(bank(7)[:, 0:24], same_row, small[:, 107:131], start=True, stop=True)\
                    .then_inc(st_full, 1)

            def transposed_thought(n):
                pe.wait_ge(tn_ready, n)
                bank_a(*cols(tn, 0, 1))

            def streamed(s):
                fills[s].n += 16
                pe.wait_ge(slot_in[s], fills[s].term + fills[s].n)

            def rows_product(last_piece=None):
                for n in range(AGG):
                    if n == AGG - 1 and last_piece is not None:
                        pe.wait_ge(agg_loaded, 32)
                        chunks = last_piece
                    else:
                        streamed(n % RING)
                        chunks = [ring[n % RING][:, c * D:(c + 1) * D] for c in range(2)]
                    for c in range(2):
                        k = 2 * n + c
                        for j in range(NJ):
                            last = nc.tensor.matmul(bank(6)[32 * j:32 * j + 32, 0:W4],
                                                    tT[:, k % 2, 32 * (k // 2):32 * (k // 2) + 32],
                                                    chunks[c][:, j * W4:(j + 1) * W4],
                                                    start=(k == 0), stop=(k == KD - 1))
                    used.one(last)

            def z_transposes(t):
                pe.wait_ge(z_ready, t + 1)
                bank_a(*cols(zst, 0, 1, 2, 3))
                bank_b(*cols(zst, 4, 5, 6, 7))

            def gate_product(t, u):
                n, k = divmod(u, KD)
                if k == 0:
                    pe.wait_ge(g_read, 2 * t + n + 1)
                last = nc.tensor.matmul(bank(4 + n), zT[:, k, :], gw[:, k, n * BANK:(n + 1) * BANK],
                                        start=(k == 0), stop=(k == KD - 1))
                if k == KD - 1:
                    last.then_inc(g_full, 1)

            def gates(t, lo, hi):
                for u in range(lo, hi):
                    gate_product(t, u)

            def next_piece(q, m):
                if q in RESIDENT_Q:
                    return as_piece(resident[RESIDENT_Q.index(q)], q), m
                streamed(m % RING)
                return as_piece(ring[m % RING], q), m + 1

            def thinking(step, more):
                before, first, second = 2 * step, 2 * step + 1, 2 * step + 2
                m = 0
                stats(step + 3)
                gates(before, 8, 11)
                transposed_thought(step + 2)
                gates(before, 11, 12)
                pe.wait_ge(a_free, A.term + A.n)
                for q in range(D1P):
                    i, k = divmod(q, KD)
                    if q == RESIDENT_Q[EARLY]:
                        pe.wait_ge(res_late, 16 * (RES - EARLY))
                    piece, m = next_piece(q, m)
                    for j in range(NJ):
                        last = nc.tensor.matmul(bank(2 + i)[32 * j:32 * j + 32, :],
                                                tT[:, k % 2, 32 * (k // 2):32 * (k // 2) + 32],
                                                piece[:, j, :], start=(k == 0), stop=(k == KD - 1))
                    if k == KD - 1:
                        last.then_inc(hp_full, 1)
                    else:
                        used.one(last) if q not in RESIDENT_Q else None
                    if q < 4:
                        gate_product(before, 12 + q)
                    if q == 3:
                        z_transposes(first)
                    if q == 5:
                        pe.wait_ge(a_free, A.term + A.n)
                        pe.wait_ge(b_free, B.term + B.n)
                    if q >= 5 and q % 3 != 1:
                        gate_product(first, (5, 6, 8, 9, 11, 12, 14, 15).index(q))
                gates(first, 8, 10)
                pe.wait_ge(hid_ready, 2 * step + 1)
                bank_a(*cols(hid, 0, 1, 2, 3))
                pe.wait_ge(hid_ready, 2 * step + 2)
                bank_b(*cols(hid, 4, 5, 6, 7))
                gates(first, 10, 12)
                pe.wait_ge(a_free, A.term + A.n)
                for q in range(D1P, PIECES):
                    c, jp = divmod(q - D1P, 2)
                    if c == H4 // P // 2 and jp == 0:
                        pe.wait_ge(b_free, B.term + B.n)
                    piece, m = next_piece(q, m)
                    for jj in range(2):
                        j = 2 * jp + jj
                        for n in range(NJ):
                            last = nc.tensor.matmul(bank(6)[32 * n:32 * n + 32, 0:W4],
                                                    hidT[:, c, 32 * j:32 * j + 32],
                                                    piece[:, jj, n * W4:(n + 1) * W4],
                                                    start=(c == 0 and j == 0), stop=(q == PIECES - 1 and jj == 1))
                    if q == PIECES - 1:
                        last.then_inc(p_full, 1)
                    elif q not in RESIDENT_Q:
                        used.one(last)
                    if q - D1P in (1, 2, 4, 5):
                        gate_product(first, 12 + (1, 2, 4, 5).index(q - D1P))
                    if more and q - D1P == 5:
                        z_transposes(second)
                    if more and q - D1P == 7:
                        pe.wait_ge(a_free, A.term + A.n)
                        pe.wait_ge(b_free, B.term + B.n)
                    if more and q - D1P in (7, 8, 10, 11, 13, 14):
                        gate_product(second, (7, 8, 10, 11, 13, 14).index(q - D1P))
                if more:
                    gates(second, 6, 8)

            pe.wait_ge(gw_loaded, 16)
            stats(1)
            z_transposes(0)
            stats(2)
            pe.wait_ge(a_free, A.n)
            pe.wait_ge(b_free, B.n)
            gates(0, 0, 3)
            transposed_thought(1)
            gates(0, 3, 4)
            pe.wait_ge(a_free, A.n)
            rows_product(agg_last)
            gates(0, 4, 8)
            pe.wait_ge(res_in, 16 * EARLY)
            with pe.Fori(0, STEPS - 1) as step:
                A.enter(step, 4), B.enter(step, 3), used.enter(step, N_RING)
                for f in fills:
                    f.enter(step, 16 * N_RING // RING)
                thinking(step, True)
                A.leave(STEPS - 1), B.leave(STEPS - 1), used.leave(STEPS - 1)
                for f in fills:
                    f.leave(STEPS - 1)
            thinking(STEPS - 1, False)
            transposed_thought(STEPS + 2)
            pe.wait_ge(a_free, A.n)
            rows_product()

            pe.wait_ge(bc_ready, 1)
            pe.wait_ge(g_read, 2 * G + 2)
            for t in range(G):
                for n in range(2):
                    if t >= 2:
                        pe.wait_ge(bb_read, 2 * t - 3 + n)
                    nc.tensor.matmul(bank(2 + 2 * (t % 2) + n), spread[:, t, :],
                                     bcast.rearrange("p j n -> p (j n)")[:, n * BANK:(n + 1) * BANK],
                                     start=True, stop=True).then_inc(bb_full, 1)


_INS = ["x", "ctx_512", "L0_xattn_Wq", "L0_xattn_Wkv_expand", "L0_xattn_Wout", "L0_attn_nu_log",
        "L0_attn_theta_log", "L0_attn_B_re", "L0_attn_B_im", "L0_attn_C_re", "L0_attn_C_im", "L0_attn_D",
        "L0_ffn_in_gamma", "L0_ffn_in_beta", "L0_ffn_agg_w", "L0_ffn_agg_b", "L0_ffn_pn_gamma",
        "L0_ffn_pn_beta", "L0_ffn_d1_w", "L0_ffn_d1_b", "L0_ffn_d2_w", "L0_ffn_d2_b", "L0_ffn_bc_w",
        "L0_ffn_bc_b", "L0_ffn_gate_w", "L0_ffn_gate_b", "L0_ffn_out_gamma", "L0_ffn_out_beta"]


def kernel(**inputs):
    import numpy as _np
    import concourse.bacc as _bacc
    from concourse import mybir as _mybir
    from concourse.bass_utils import run_bass_kernel_spmd as _run

    nc = _bacc.Bacc("TRN2", target_bir_lowering=False, num_devices=1)
    arrays, args = {}, []
    for name in _INS:
        a = _np.ascontiguousarray(inputs[name])
        arrays[f"in_{name}_dram"] = a
        args.append(nc.dram_tensor(f"in_{name}_dram", a.shape, _mybir.dt.from_np(a.dtype), kind="ExternalInput").ap())
    shape = inputs["x"].shape
    args.append(nc.dram_tensor("out_0_dram", shape, _mybir.dt.float32, kind="ExternalOutput").ap())
    build(nc, *args)
    r = _run(nc, [arrays], core_ids=[0])
    return r.results[0]["out_0_dram"]
```
